# Optimizing a Trainium2 kernel written in Bass

```python
import numpy as np
import jax
import jax.numpy as jnp

def _softmax(x, axis=-1):
    return jax.nn.softmax(x, axis=axis)

def _gelu(x):
    return jax.nn.gelu(x, approximate=True)

def _silu(x):
    return jax.nn.silu(x)

def _sigmoid(x):
    return jax.nn.sigmoid(x)

def _layernorm(x, axis=-1, eps=1e-05):
    m = jnp.mean(x, axis=axis, keepdims=True)
    v = jnp.var(x, axis=axis, keepdims=True)
    return (x - m) / jnp.sqrt(v + eps)

def _scatter_add(tgt, idx, src, axis=0):
    return tgt.at[idx].add(src)

def _segment_sum(src, seg, n):
    return jax.ops.segment_sum(src, seg, n)
kernel_name = 'mk_gnn_preln_d4_gnn_r8_370970'

def setup_inputs(seed: int=0):
    np.random.seed(seed)
    _w = jnp.asarray

    def _rec_inputs():
        import jax
        import jax.numpy as jnp
        _gk = jax.random.key(seed)
        x = -0.0003713 + 1 * jax.random.normal(jax.random.fold_in(_gk, 1), (6250, 256), jnp.float32)
        src = jax.random.randint(jax.random.fold_in(_gk, 2), (100000,), 0, 6250, jnp.int32)
        dst = jax.random.randint(jax.random.fold_in(_gk, 3), (100000,), 0, 6250, jnp.int32)
        _o = jnp.argsort(dst, stable=True)
        src = src[_o]
        dst = dst[_o]
        edge_attr_256 = -4.21973e-05 + 0.999841 * jax.random.normal(jax.random.fold_in(_gk, 12), (100000, 256), jnp.float32)
        edge_attr_64 = 0.000151818 + 1.00006 * jax.random.normal(jax.random.fold_in(_gk, 13), (100000, 64), jnp.float32)
        edge_weight = jax.random.uniform(jax.random.fold_in(_gk, 16), (100000,), jnp.float32, 0.0, 4.99999)
        return (x, src, dst, edge_attr_256, edge_attr_64, edge_weight)
    x, src, dst, edge_attr_256, edge_attr_64, edge_weight = _rec_inputs()

    def _L0_gnn_setup():
        import jax, jax.numpy as jnp
        import numpy as np
        N_NODES = 6250
        key = jax.random.key(seed)
        k1, k2, k3 = jax.random.split(key, 3)
        x = jax.random.normal(k1, (N_NODES, 256), dtype=jnp.float32)
        W = jax.random.normal(k2, (256, 256), dtype=jnp.float32) * (1.0 / np.sqrt(256))
        edge_index = jax.random.randint(k3, (2, 200000), 0, N_NODES, dtype=jnp.int64)
        return {'x': x, 'W': W, 'edge_index': edge_index}
    _L0_gnn_all = _L0_gnn_setup()
    _L0_gnn_in = {k: v for k, v in _L0_gnn_all.items() if k in ('W',)}
    del _L0_gnn_all

    def _L1_gnn_setup():
        import jax, jax.numpy as jnp
        import numpy as np
        H = 256
        R = 64
        N = 2500
        E = 40000
        CUTOFF_LO = 0.0
        CUTOFF_UP = 5.0
        LN_EPS = 1e-05

        def _layernorm(x, g, b):
            mu = jnp.mean(x, axis=-1, keepdims=True)
            var = jnp.var(x, axis=-1, keepdims=True)
            return (x - mu) * jax.lax.rsqrt(var + LN_EPS) * g + b

        def _cosine_cutoff(r):
            c = 0.5 * (jnp.cos(r * (jnp.pi / CUTOFF_UP)) + 1.0)
            return c * (r < CUTOFF_UP).astype(r.dtype)
        key = jax.random.key(seed)
        ks = jax.random.split(key, 16)

        def xavier(k, shape):
            fan_in, fan_out = (shape[1], shape[0])
            lim = np.sqrt(6.0 / (fan_in + fan_out))
            return jax.random.uniform(k, shape, jnp.float32, -lim, lim)
        x = jax.random.normal(ks[0], (N, H), jnp.float32)
        edge_index = jax.random.randint(ks[1], (2, E), 0, N, jnp.int64)
        edge_weight = jax.random.uniform(ks[2], (E,), jnp.float32, 0.0, CUTOFF_UP)
        edge_attr = jax.random.normal(ks[3], (E, R), jnp.float32)
        return {'x': x, 'edge_index': edge_index, 'edge_weight': edge_weight, 'edge_attr': edge_attr, 'ln_g': jnp.ones((H,), jnp.float32), 'ln_b': jnp.zeros((H,), jnp.float32), 'Wq': xavier(ks[4], (H, H)), 'bq': jnp.zeros((H,), jnp.float32), 'Wk': xavier(ks[5], (H, H)), 'bk': jnp.zeros((H,), jnp.float32), 'Wv': xavier(ks[6], (H, H)), 'bv': jnp.zeros((H,), jnp.float32), 'Wo': xavier(ks[7], (H, H)), 'bo': jnp.zeros((H,), jnp.float32), 'Wdk': xavier(ks[8], (H, R)), 'bdk': jnp.zeros((H,), jnp.float32), 'Wdv': xavier(ks[9], (H, R)), 'bdv': jnp.zeros((H,), jnp.float32)}
    _L1_gnn_all = _L1_gnn_setup()
    _L1_gnn_in = {k: v for k, v in _L1_gnn_all.items() if k in ('ln_g', 'ln_b', 'Wq', 'bq', 'Wk', 'bk', 'Wv', 'bv', 'Wo', 'bo', 'Wdk', 'bdk', 'Wdv', 'bdv')}
    del _L1_gnn_all

    def _L2_gnn_setup():
        import jax, jax.numpy as jnp
        import numpy as np
        N_NODES = 5000
        N_EDGES = 37500
        EMBED = 256
        LN_EPS = 1e-05
        LEAKY_SLOPE = 0.01

        def _layer_norm(x, w, b):
            mu = jnp.mean(x, axis=-1, keepdims=True)
            var = jnp.mean(jnp.square(x - mu), axis=-1, keepdims=True)
            return (x - mu) * jax.lax.rsqrt(var + LN_EPS) * w + b
        key = jax.random.key(seed)
        ks = jax.random.split(key, 5)
        H = jax.random.normal(ks[0], (N_NODES, EMBED), dtype=jnp.float32)
        E = jax.random.normal(ks[1], (N_EDGES, EMBED), dtype=jnp.float32)
        ht = jax.random.randint(ks[2], (N_EDGES, 2), 0, N_NODES, dtype=jnp.int64)
        W_fwd = jax.random.normal(ks[3], (EMBED, 2 * EMBED), dtype=jnp.float32) * (1.0 / np.sqrt(2 * EMBED))
        W_back = jax.random.normal(ks[4], (EMBED, 2 * EMBED), dtype=jnp.float32) * (1.0 / np.sqrt(2 * EMBED))
        return {'H': H, 'E': E, 'ht': ht, 'queries': jnp.zeros((1,), jnp.float32), 'influence_weights': jnp.zeros((1,), jnp.float32), 'W_fwd': W_fwd, 'b_fwd': jnp.zeros((EMBED,), jnp.float32), 'W_back': W_back, 'b_back': jnp.zeros((EMBED,), jnp.float32), 'ln_w': jnp.ones((EMBED,), jnp.float32), 'ln_b': jnp.zeros((EMBED,), jnp.float32)}
    _L2_gnn_all = _L2_gnn_setup()
    _L2_gnn_in = {k: v for k, v in _L2_gnn_all.items() if k in ('queries', 'influence_weights', 'W_fwd', 'b_fwd', 'W_back', 'b_back', 'ln_w', 'ln_b')}
    del _L2_gnn_all

    def _L3_gnn_setup():
        import jax, jax.numpy as jnp
        import numpy as np
        from itertools import combinations
        NDIM = 256
        BATCH = 8192

        def _build_mat(rots, idx_i, idx_j, ndim):

            def step(mat, t):
                i, j, theta = t
                c = jnp.cos(theta)
                s = jnp.sin(theta)
                ri = mat[i]
                rj = mat[j]
                mat = mat.at[i].set(c * ri - s * rj)
                mat = mat.at[j].set(s * ri + c * rj)
                return (mat, None)
            mat0 = jnp.eye(ndim, dtype=rots.dtype)
            mat, _ = jax.lax.scan(step, mat0, (idx_i, idx_j, rots))
            return mat.T
        key = jax.random.key(seed)
        k1, k2 = jax.random.split(key)
        pairs = np.array(list(combinations(range(NDIM), 2)), dtype=np.int32)
        return {'x': jax.random.normal(k1, (BATCH, NDIM), dtype=jnp.float32), 'rots': jax.random.normal(k2, (pairs.shape[0],), dtype=jnp.float32), 'idx_i': jnp.asarray(pairs[:, 0]), 'idx_j': jnp.asarray(pairs[:, 1])}
    _L3_gnn_all = _L3_gnn_setup()
    _L3_gnn_in = {k: v for k, v in _L3_gnn_all.items() if k in ()}
    del _L3_gnn_all
    return {'x': x, 'src': src, 'dst': dst, 'edge_attr_256': edge_attr_256, 'edge_attr_64': edge_attr_64, 'edge_weight': edge_weight, 'L0_gnn_W': _L0_gnn_in['W'], 'L1_gnn_ln_g': _L1_gnn_in['ln_g'], 'L1_gnn_ln_b': _L1_gnn_in['ln_b'], 'L1_gnn_Wq': _L1_gnn_in['Wq'], 'L1_gnn_bq': _L1_gnn_in['bq'], 'L1_gnn_Wk': _L1_gnn_in['Wk'], 'L1_gnn_bk': _L1_gnn_in['bk'], 'L1_gnn_Wv': _L1_gnn_in['Wv'], 'L1_gnn_bv': _L1_gnn_in['bv'], 'L1_gnn_Wo': _L1_gnn_in['Wo'], 'L1_gnn_bo': _L1_gnn_in['bo'], 'L1_gnn_Wdk': _L1_gnn_in['Wdk'], 'L1_gnn_bdk': _L1_gnn_in['bdk'], 'L1_gnn_Wdv': _L1_gnn_in['Wdv'], 'L1_gnn_bdv': _L1_gnn_in['bdv'], 'L2_gnn_queries': _L2_gnn_in['queries'], 'L2_gnn_influence_weights': _L2_gnn_in['influence_weights'], 'L2_gnn_W_fwd': _L2_gnn_in['W_fwd'], 'L2_gnn_b_fwd': _L2_gnn_in['b_fwd'], 'L2_gnn_W_back': _L2_gnn_in['W_back'], 'L2_gnn_b_back': _L2_gnn_in['b_back'], 'L2_gnn_ln_w': _L2_gnn_in['ln_w'], 'L2_gnn_ln_b': _L2_gnn_in['ln_b']}

def reference(x, src, dst, edge_attr_256, edge_attr_64, edge_weight, L0_gnn_W, L1_gnn_ln_g, L1_gnn_ln_b, L1_gnn_Wq, L1_gnn_bq, L1_gnn_Wk, L1_gnn_bk, L1_gnn_Wv, L1_gnn_bv, L1_gnn_Wo, L1_gnn_bo, L1_gnn_Wdk, L1_gnn_bdk, L1_gnn_Wdv, L1_gnn_bdv, L2_gnn_queries, L2_gnn_influence_weights, L2_gnn_W_fwd, L2_gnn_b_fwd, L2_gnn_W_back, L2_gnn_b_back, L2_gnn_ln_w, L2_gnn_ln_b):
    import jax
    import jax.numpy as jnp

    def _L0_gnn_ref(x, W, edge_index):
        import jax, jax.numpy as jnp
        import numpy as np
        N_NODES = 6250
        N = x.shape[0]
        src, dst = (edge_index[0], edge_index[1])
        h = x @ W
        deg = jax.ops.segment_sum(jnp.ones_like(dst, dtype=h.dtype), dst, num_segments=N)
        deg_inv_sqrt = jnp.where(deg > 0, jax.lax.rsqrt(jnp.maximum(deg, 1)), 0.0)
        norm = deg_inv_sqrt[src] * deg_inv_sqrt[dst]
        msgs = h[src] * norm[:, None]
        out = jax.ops.segment_sum(msgs, dst, num_segments=N)
        return out

    def _L1_gnn_ref(x, edge_index, edge_weight, edge_attr, ln_g, ln_b, Wq, bq, Wk, bk, Wv, bv, Wo, bo, Wdk, bdk, Wdv, bdv):
        import jax, jax.numpy as jnp
        import numpy as np
        H = 256
        R = 64
        N = 2500
        E = 40000
        CUTOFF_LO = 0.0
        CUTOFF_UP = 5.0
        LN_EPS = 1e-05

        def _layernorm(x, g, b):
            mu = jnp.mean(x, axis=-1, keepdims=True)
            var = jnp.var(x, axis=-1, keepdims=True)
            return (x - mu) * jax.lax.rsqrt(var + LN_EPS) * g + b

        def _cosine_cutoff(r):
            c = 0.5 * (jnp.cos(r * (jnp.pi / CUTOFF_UP)) + 1.0)
            return c * (r < CUTOFF_UP).astype(r.dtype)
        src = edge_index[0]
        dst = edge_index[1]
        x_norm = _layernorm(x, ln_g, ln_b)
        q = x_norm @ Wq.T + bq
        k = x_norm @ Wk.T + bk
        v = x_norm @ Wv.T + bv
        dk = jax.nn.silu(edge_attr @ Wdk.T + bdk)
        dv = jax.nn.silu(edge_attr @ Wdv.T + bdv)
        q_i = q[dst]
        k_j = k[src]
        v_j = v[src]
        attn = jnp.sum(q_i * k_j * dk, axis=1)
        attn = jax.nn.silu(attn) * _cosine_cutoff(edge_weight)
        msg = v_j * dv * attn[:, None]
        agg = jax.ops.segment_sum(msg, dst, num_segments=x.shape[0])
        out = agg @ Wo.T + bo
        return x + out

    def _L2_gnn_ref(H, E, ht, queries, influence_weights, W_fwd, b_fwd, W_back, b_back, ln_w, ln_b):
        import jax, jax.numpy as jnp
        import numpy as np
        N_NODES = 5000
        N_EDGES = 37500
        EMBED = 256
        LN_EPS = 1e-05
        LEAKY_SLOPE = 0.01

        def _layer_norm(x, w, b):
            mu = jnp.mean(x, axis=-1, keepdims=True)
            var = jnp.mean(jnp.square(x - mu), axis=-1, keepdims=True)
            return (x - mu) * jax.lax.rsqrt(var + LN_EPS) * w + b
        heads = ht[:, 0]
        tails = ht[:, 1]
        n = H.shape[0]
        msg_fwd = jnp.concatenate([H[heads], E], axis=1) @ W_fwd.T + b_fwd
        msg_back = jnp.concatenate([H[tails], E], axis=1) @ W_back.T + b_back
        msg_dst = jnp.concatenate([tails, heads], axis=0)
        messages = jnp.concatenate([msg_fwd, msg_back], axis=0)
        agg = jax.ops.segment_sum(messages, msg_dst, num_segments=n)
        counts = jax.ops.segment_sum(jnp.ones_like(msg_dst, dtype=H.dtype), msg_dst, num_segments=n)
        agg = agg / counts[:, None]
        out = _layer_norm(jax.nn.leaky_relu(agg, LEAKY_SLOPE) + H, ln_w, ln_b)
        return out

    def _L3_gnn_ref(x, rots, idx_i, idx_j):
        import jax, jax.numpy as jnp
        import numpy as np
        from itertools import combinations
        NDIM = 256
        BATCH = 8192

        def _build_mat(rots, idx_i, idx_j, ndim):

            def step(mat, t):
                i, j, theta = t
                c = jnp.cos(theta)
                s = jnp.sin(theta)
                ri = mat[i]
                rj = mat[j]
                mat = mat.at[i].set(c * ri - s * rj)
                mat = mat.at[j].set(s * ri + c * rj)
                return (mat, None)
            mat0 = jnp.eye(ndim, dtype=rots.dtype)
            mat, _ = jax.lax.scan(step, mat0, (idx_i, idx_j, rots))
            return mat.T
        m = _build_mat(rots, idx_i, idx_j, x.shape[-1])
        return x @ m
    edge_index = jnp.stack([src, dst])
    edge_index_t = jnp.stack([src, dst], axis=1)
    h = jnp.maximum(_layernorm(x, axis=-1), 0.0)
    x = x + _L0_gnn_ref(h, L0_gnn_W, edge_index)
    h = jnp.maximum(_layernorm(x, axis=-1), 0.0)
    x = x + _L1_gnn_ref(h, edge_index, edge_weight, edge_attr_64, L1_gnn_ln_g, L1_gnn_ln_b, L1_gnn_Wq, L1_gnn_bq, L1_gnn_Wk, L1_gnn_bk, L1_gnn_Wv, L1_gnn_bv, L1_gnn_Wo, L1_gnn_bo, L1_gnn_Wdk, L1_gnn_bdk, L1_gnn_Wdv, L1_gnn_bdv)
    h = jnp.maximum(_layernorm(x, axis=-1), 0.0)
    x = x + _L2_gnn_ref(h, edge_attr_256, edge_index_t, L2_gnn_queries, L2_gnn_influence_weights, L2_gnn_W_fwd, L2_gnn_b_fwd, L2_gnn_W_back, L2_gnn_b_back, L2_gnn_ln_w, L2_gnn_ln_b)
    h = jnp.maximum(_layernorm(x, axis=-1), 0.0)
    x = x + _L3_gnn_ref(h, edge_weight, src, dst)
    return x

_drawn_inputs = setup_inputs


def setup_inputs(seed=0):
    import zlib

    import numpy as np

    out = dict(_drawn_inputs(seed))
    spreads = {'L1_gnn_ln_g': (1.0, 0.2),
     'L1_gnn_ln_b': (0.0, 0.1),
     'L1_gnn_bq': (0.0, 0.1),
     'L1_gnn_bk': (0.0, 0.1),
     'L1_gnn_bv': (0.0, 0.1),
     'L1_gnn_bo': (0.0, 0.391),
     'L1_gnn_bdk': (0.0, 0.1),
     'L1_gnn_bdv': (0.0, 0.1),
     'L2_gnn_b_fwd': (0.0, 0.75),
     'L2_gnn_b_back': (0.0, 0.771),
     'L2_gnn_ln_w': (1.0, 0.2),
     'L2_gnn_ln_b': (0.0, 0.444)}
    factors = {}
    for name, (base, spread) in spreads.items():
        noise = np.random.default_rng([zlib.crc32(name.encode()), seed]).standard_normal(out[name].shape)
        drawn = base * np.exp(spread * noise) if base else spread * noise
        out[name] = jnp.asarray(drawn.astype(out[name].dtype))
    for name, factor in factors.items():
        out[name] = (out[name] * factor).astype(out[name].dtype)
    return out
```

```python
from contextlib import ExitStack, contextmanager

import numpy as np
import concourse.bass as bass
from concourse import mybir

F32, I32, BF16 = mybir.dt.float32, mybir.dt.int32, mybir.dt.bfloat16
ALU = mybir.AluOpType
ACT = mybir.ActivationFunctionType
AX = mybir.AxisListType

P = 128
NODES, EDGES, D, R = 6250, 100000, 256, 64
NODE_TILES = -(-NODES // P)
NODES_PAD = NODE_TILES * P
PAD_NODE = NODES_PAD - 1
EDGE_TILES = -(-EDGES // P)
EDGES_PAD = EDGE_TILES * P
ROW_BLOCKS = 7
STEPS = 832
STEP_COLS = ROW_BLOCKS * P
GROUP = 7
GROUPS = NODE_TILES // GROUP
HALF = STEPS // 2
EPS = 1e-5
CH_EDGES = 64
BATCH = 4
BATCH_EDGES = CH_EDGES * BATCH
ROT_LIST = EDGES_PAD + BATCH_EDGES
SORT_ROW = 516
OUT_OF_BOUNDS = 1 << 20
TWO_PI = 6.283185307179586
TWO_PI_HI = 6.28125
TWO_PI_LO = TWO_PI - TWO_PI_HI
ROUND = 12582912.0
SIN_MAX = 3.1415925
CUTOFF = 5.0


class Chain:

    def __init__(self, eng, sem):
        self.eng, self.sem, self.n = eng, sem, 0

    def __call__(self, ins):
        self.n = self.n + 1
        ins.then_inc(self.sem, 1)
        self.eng.wait_ge(self.sem, self.n)

    def loop(self, i, per, first):
        self.n = i * per + first


def settle(eng, sem):
    eng.sem_inc(sem, 1)


def col(ap, c, n=1):
    return ap[:, bass.ds(c, n)]


@contextmanager
def phase(nc):
    with ExitStack() as c:
        sems = []

        def sem(name):
            sems.append(nc.alloc_semaphore(name))
            return sems[-1]

        yield (lambda n, s, d=F32: c.enter_context(nc.sbuf_tensor(n, s, d)),
               lambda n, s, d=F32: c.enter_context(nc.psum_tensor(n, s, d)), sem)
    nc.clear_and_free_semaphores(sems)
    nc.all_engine_barrier()


def constants(nc, k):
    with phase(nc) as (sb, ps, sem), nc.Block() as block:
        s_z, s_id = sem("const_zero"), sem("const_done")

        @block.gpsimd
        def _(pool):
            nc.gpsimd.memset(k.ident[:, :], 0.0).then_inc(s_z, 1)
            nc.gpsimd.memset(k.ones[:, :], 1.0).then_inc(s_z, 1)
            nc.gpsimd.iota(k.iota[:, :], [[1, P]], base=0, channel_multiplier=0, allow_small_or_imprecise_dtypes=True).then_inc(s_z, 1)
            pool.wait_ge(s_z, 3)
            nc.gpsimd.affine_select(out=k.ident[:, :], in_=k.ident[:, :], compare_op=ALU.not_equal, fill=1.0,
                                    base=0, pattern=[[-1, P]], channel_multiplier=1).then_inc(s_id, 1)
            nc.gpsimd.affine_select(out=k.upper[:, :], in_=k.ones[:, :], compare_op=ALU.is_gt, fill=0.0,
                                    base=0, pattern=[[1, P]], channel_multiplier=-1).then_inc(s_id, 1)
            pool.wait_ge(s_id, 2)


def node_counts_and_sort(nc, k):
    with phase(nc) as (sb, ps, sem):
        TB = 17
        NB = EDGE_TILES // TB
        raw = sb("cs_raw", [P, 2, EDGE_TILES], I32)
        low_i = sb("cs_low_i", [P, 2, EDGE_TILES], I32)
        high_i = sb("cs_high_i", [P, 2, EDGE_TILES], I32)
        low = sb("cs_low", [P, 2, EDGE_TILES], F32)
        high = sb("cs_high", [P, 2, EDGE_TILES], F32)
        ohl = sb("cs_ohl", [P, 2, TB, P], BF16)
        ohh = sb("cs_ohh", [P, 2, TB, NODE_TILES], BF16)
        zb = sb("cs_zb", [P, P], BF16)
        degs = sb("cs_degs", [NODE_TILES, 2, P], F32)
        eq = sb("cs_eq", [P, EDGE_TILES], F32)
        zeros = sb("cs_zeros", [P, EDGE_TILES], F32)
        scan = sb("cs_scan", [P, EDGE_TILES], F32)
        tmp = sb("cs_tmp", [P, EDGE_TILES], F32)
        rank = sb("cs_rank", [P, EDGE_TILES], F32)
        tot = sb("cs_tot", [P, 64], F32)
        end = sb("cs_end", [P, 64], F32)
        off = sb("cs_off", [P, 64], F32)
        deg_ps = ps("cs_deg", [P, 2, P], F32)
        t_ps = ps("cs_t", [P, 2, P], F32)
        o_ps = ps("cs_o", [P, 64], F32)
        tt_ps = ps("cs_tt", [P, 64], F32)
        loaded, chain_s = sem("cs_loaded"), sem("cs_chain")
        ohl_rdy, ohh_rdy, counted, zdone = sem("cs_ohl_rdy"), sem("cs_ohh_rdy"), sem("cs_counted"), sem("cs_zero")
        degs_copied, transposed, split = sem("cs_degcopied"), sem("cs_transposed"), sem("cs_split")
        tot_rdy, off_rdy, highs_rdy = sem("cs_tot_rdy"), sem("cs_off_rdy"), sem("cs_highs")
        with nc.Block() as block:
            @block.sync
            def _(sp):
                sp.dma_start(raw[:, 0, :], k.dst_cols[:, 0:EDGE_TILES]).then_inc(loaded, 16)
                sp.dma_start(raw[:, 1, :], k.src_cols[:, 0:EDGE_TILES]).then_inc(loaded, 16)
                sp.wait_ge(loaded, 32)

            @block.vector
            def _(dve):
                link = Chain(dve, chain_s)
                dve.wait_ge(loaded, 32)
                link(nc.vector.tensor_scalar(low_i[:, :, :], raw[:, :, :], 127, None, ALU.bitwise_and))
                link(nc.vector.tensor_scalar(high_i[:, :, :], raw[:, :, :], 7, None, ALU.arith_shift_right))
                nc.vector.memset(zb[:, :], 0.0).then_inc(zdone, 1)
                link(nc.vector.tensor_copy(low[:, :, :], low_i[:, :, :]))
                nc.vector.tensor_copy(high[:, :, :], high_i[:, :, :]).then_inc(highs_rdy, 1)
                dve.wait_ge(highs_rdy, 1)
                for a in range(2):
                    with dve.Fori(0, NB // 2) as i:
                        for u in range(2):
                            dve.wait_ge(counted, i * 2 + (u + a * NB + 1))
                            nc.vector.tensor_tensor(
                                ohl[:, u, :, :],
                                k.iota[:, :].unsqueeze(1).to_broadcast([P, TB, P]),
                                low[:, a, bass.ds((i * 2 + u) * TB, TB)].unsqueeze(2).to_broadcast([P, TB, P]),
                                ALU.is_equal).then_inc(ohl_rdy, 1)
                            nc.vector.tensor_tensor(
                                ohh[:, u, :, :],
                                k.iota[:, 0:NODE_TILES].unsqueeze(1).to_broadcast([P, TB, NODE_TILES]),
                                high[:, a, bass.ds((i * 2 + u) * TB, TB)].unsqueeze(2).to_broadcast([P, TB, NODE_TILES]),
                                ALU.is_equal).then_inc(ohh_rdy, 1)
                dve.wait_ge(counted, 2 * NB + 2)
                nc.vector.tensor_copy(degs[:, :, :], deg_ps[0:NODE_TILES, :, :]).then_inc(degs_copied, 1)
                dve.wait_ge(transposed, 2)
                nc.vector.tensor_copy(k.cnt[:, :, :], t_ps[:, :, 0:NODE_TILES]).then_inc(split, 1)
                dve.wait_ge(highs_rdy, 1)
                link(nc.vector.memset(zeros[:, :], 0.0))
                link(nc.vector.memset(rank[:, :], 0.0))
                link(nc.vector.memset(k.place[:, EDGE_TILES:STEP_COLS], 0.0))
                base = link.n
                with dve.Fori(0, NODE_TILES) as h:
                    link.loop(h, 5, base)
                    hcol = col(k.iota, h)
                    link(nc.vector.tensor_scalar(eq[:, :], high[:, 1, :], hcol, None, ALU.is_equal))
                    link(nc.vector.tensor_tensor_scan(scan[:, :], eq[:, :], zeros[:, :], 0.0, ALU.add, ALU.add))
                    link(nc.vector.tensor_tensor(tmp[:, :], eq[:, :], scan[:, :], ALU.mult))
                    link(nc.vector.tensor_copy(col(tot, h), scan[:, EDGE_TILES - 1:EDGE_TILES]))
                    link(nc.vector.tensor_tensor(rank[:, :], rank[:, :], tmp[:, :], ALU.add))
                link.n = base + 5 * NODE_TILES
                nc.vector.tensor_scalar(tmp[:, 0:1], tot[:, 0:1], 0.0, None, ALU.mult).then_inc(tot_rdy, 1)
                dve.wait_ge(off_rdy, 1)
                link(nc.vector.tensor_tensor_scan(end[:, 0:NODE_TILES], tt_ps[:, 0:NODE_TILES], zeros[:, 0:NODE_TILES],
                                                  0.0, ALU.add, ALU.add))
                link(nc.vector.tensor_copy(k.bucket_end[:, :], end[:, 0:NODE_TILES]))
                link(nc.vector.tensor_tensor(off[:, 0:NODE_TILES], end[:, 0:NODE_TILES], tt_ps[:, 0:NODE_TILES], ALU.subtract))
                link(nc.vector.tensor_tensor(off[:, 0:NODE_TILES], off[:, 0:NODE_TILES], o_ps[:, 0:NODE_TILES], ALU.add))
                link(nc.vector.tensor_scalar(off[:, 0:NODE_TILES], off[:, 0:NODE_TILES], -1.0, None, ALU.add))
                base = link.n
                with dve.Fori(0, NODE_TILES) as h:
                    link.loop(h, 2, base)
                    link(nc.vector.tensor_scalar(eq[:, :], high[:, 1, :], col(k.iota, h), col(off, h), ALU.is_equal, ALU.mult))
                    link(nc.vector.tensor_tensor(rank[:, :], rank[:, :], eq[:, :], ALU.add))
                link.n = base + 2 * NODE_TILES
                link(nc.vector.tensor_copy(k.place[:, 0:EDGE_TILES], rank[:, :]))

            @block.tensor
            def _(pe):
                pe.wait_ge(zdone, 1)
                nc.tensor.matmul(deg_ps[0:NODE_TILES, :, :], zb[:, 0:NODE_TILES],
                                 zb[:, :].unsqueeze(1).to_broadcast([P, 2, P]), start=True, stop=True).then_inc(counted, 2)
                for a in range(2):
                    with pe.Fori(0, NB // 2) as i:
                        for u in range(2):
                            pe.wait_ge(ohl_rdy, i * 2 + (u + a * NB + 1))
                            pe.wait_ge(ohh_rdy, i * 2 + (u + a * NB + 1))
                            for t in range(TB):
                                last = nc.tensor.matmul(deg_ps[0:NODE_TILES, a, :], ohh[:, u, t, :], ohl[:, u, t, :],
                                                        start=False, stop=True, skip_group_check=True)
                            last.then_inc(counted, 1)
                pe.wait_ge(degs_copied, 1)
                for a in range(2):
                    nc.tensor.transpose(t_ps[:, a, 0:NODE_TILES], degs[:, a, :], k.ident[0:NODE_TILES, 0:NODE_TILES]).then_inc(transposed, 1)
                pe.wait_ge(tot_rdy, 1)
                nc.tensor.matmul(o_ps[:, 0:NODE_TILES], k.upper[:, :], tot[:, 0:NODE_TILES], start=True, stop=True)
                nc.tensor.matmul(tt_ps[:, 0:NODE_TILES], k.ones[:, :], tot[:, 0:NODE_TILES], start=True, stop=True).then_inc(off_rdy, 1)


def step_lists(nc, k):
    with phase(nc) as (sb, ps, sem):
        B = ROW_BLOCKS
        ends_i = sb("sl_ends_i", [P, 3, B], I32)
        lo = sb("sl_lo", [P, 2, B], F32)
        hi = sb("sl_hi", [P, 2, B], F32)
        prev = sb("sl_prev", [P, 2, B], F32)
        cnt = sb("sl_cnt", [P, 2, B], F32)
        start = sb("sl_start", [P, 2, B], F32)
        tot = sb("sl_tot", [P, 2, B], F32)
        inc = sb("sl_inc", [P, 2, B], F32)
        zero = sb("sl_zero", [P, B], F32)
        wgt = sb("sl_wgt", [P, 2, B, 2], F32)
        pos = sb("sl_pos", [P, 3, B], F32)
        cmp49 = sb("sl_cmp49", [P, NODE_TILES], F32)
        kk = sb("sl_kk", [P, STEP_COLS], F32)
        valid = sb("sl_valid", [P, B], F32)
        tidx = sb("sl_tidx", [P, B], F32)
        cmp = sb("sl_cmp", [P, 2, B, STEPS], F32)
        row = sb("sl_row", [1, 2, 2, STEPS], F32)
        krow = sb("sl_krow", [1, STEPS], F32)
        kcol = sb("sl_kcol", [P, B], F32)
        colv = sb("sl_colv", [P, B, 2], F32)
        e_idx = sb("sl_e_idx", [P, B], I32)
        n128 = sb("sl_n128", [P, B], F32)
        n_row = sb("sl_n_row", [1, STEPS], F32)
        e_list2, n_list2 = sb("sl_e_list2", [1, STEP_COLS], I32), sb("sl_n_list2", [1, STEP_COLS], I32)
        rows_i = sb("sl_rows_i", [P, 2, B, P], I32)
        rows_w = sb("sl_rows_w", [P, B, P], F32)
        rows_f = sb("sl_rows_f", [P, 2, B, P], F32)
        m_ps = ps("sl_m", [P, 2, 2, B], F32)
        r_ps = ps("sl_r", [1, 2, 512], F32)
        c_ps = ps("sl_c", [P, B, 2], F32)
        x_ps = ps("sl_x", [P, 2, 512], F32)
        place_t = sb("sl_place_t", [P, B, P], F32)
        rows_p = sb("sl_rows_p", [P, B, P], F32)
        inside = sb("sl_inside", [P, B, P], F32)
        pt_rdy, pt_free, place_out = sem("sl_pt_rdy"), sem("sl_pt_free"), sem("sl_place_out")
        loaded, chain_s, iota_s, memset_s = sem("sl_loaded"), sem("sl_chain"), sem("sl_iota"), sem("sl_memset")
        cnt_rdy, summed, cmp_rdy, row_ps_rdy, row_free = sem("sl_cnt_rdy"), sem("sl_summed"), sem("sl_cmp_rdy"), sem("sl_row_ps"), sem("sl_row_free")
        col_rdy, n_rdy, walk_out, idx_rdy = sem("sl_col_rdy"), sem("sl_n_rdy"), sem("sl_walk_out"), sem("sl_idx")
        gath, rows_rdy, x_rdy, x_free = sem("sl_gath"), sem("sl_rows_rdy"), sem("sl_x_rdy"), sem("sl_x_free")
        with nc.Block() as block:
            @block.sync
            def _(sp):
                flat = k.dst_rows.rearrange("a e -> (a e)")
                last = k.dst_rows.rearrange("(b p) e -> p b e", p=P)
                with nc.allow_non_contiguous_dma(reason="the ends of edge tiles"):
                    sp.dma_start(ends_i[:, 0, :].unsqueeze(2), last[:, :, 0:1]).then_inc(loaded, 16)
                    sp.dma_start(ends_i[:, 1, :].unsqueeze(2), last[:, :, P - 1:P]).then_inc(loaded, 16)
                    sp.wait_ge(memset_s, 1)
                    sp.dma_start(ends_i[1:P, 2, 0:1], k.dst_rows[0:P - 1, P - 1:P]).then_inc(loaded, 16)
                    for b in range(1, B):
                        sp.dma_start(ends_i[:, 2, b:b + 1], k.dst_rows[b * P - 1:b * P + P - 1, P - 1:P]).then_inc(loaded, 16)
                sp.wait_ge(loaded, 16 * (B + 2))
                sp.wait_ge(pt_free, B)
                sp.dma_start(k.place_rows.rearrange("(b p) e -> p b e", p=P), place_t[:, :, :]).then_inc(place_out, 16)
                sp.wait_ge(n_rdy, 1)
                sp.dma_start(k.walk_lists[0:1, :], e_list2[:, :]).then_inc(walk_out, 16)
                sp.dma_start(k.walk_lists[1:2, :], n_list2[:, :]).then_inc(walk_out, 16)
                sp.dma_start(k.walk_n128, n_row[:, :]).then_inc(walk_out, 16)
                sp.wait_ge(walk_out, 48)
                sp.wait_ge(place_out, 16)

            @block.gpsimd
            def _(pool):
                kw = dict(allow_small_or_imprecise_dtypes=True)
                nc.gpsimd.memset(ends_i[:, 2, :], -P).then_inc(memset_s, 1)
                nc.gpsimd.iota(kk[:, :], [[1, STEP_COLS]], base=0, channel_multiplier=0, **kw).then_inc(iota_s, 1)
                nc.gpsimd.iota(krow[:, :], [[1, STEPS]], base=0, channel_multiplier=0, **kw).then_inc(iota_s, 1)
                nc.gpsimd.iota(kcol[:, :], [[P, B]], base=0, channel_multiplier=1, **kw).then_inc(iota_s, 1)
                for n, b0 in enumerate((0, P - 1, -1)):
                    nc.gpsimd.iota(pos[:, n, :], [[P * P, B]], base=b0, channel_multiplier=P, **kw).then_inc(iota_s, 1)
                nc.gpsimd.iota(tidx[:, :], [[P, B]], base=0, channel_multiplier=1, **kw).then_inc(iota_s, 1)
                pool.wait_ge(idx_rdy, 1)
                pool.wait_ge(place_out, 16)
                for b in range(B):
                    pool.indirect_dma_start(out=rows_p[:, b, :], out_offset=None, in_=k.place_rows,
                                            in_offset=bass.IndirectOffsetOnAxis(ap=e_idx[:, b:b + 1], axis=0)).then_inc(gath, 16)
                    for n, rows in ((0, k.src_rows), (1, k.dst_rows)):
                        pool.indirect_dma_start(out=rows_i[:, n, b, :], out_offset=None, in_=rows,
                                                in_offset=bass.IndirectOffsetOnAxis(ap=e_idx[:, b:b + 1], axis=0)).then_inc(gath, 16)
                    pool.indirect_dma_start(out=rows_w[:, b, :], out_offset=None, in_=k.w_rows,
                                            in_offset=bass.IndirectOffsetOnAxis(ap=e_idx[:, b:b + 1], axis=0)).then_inc(gath, 16)
                pool.wait_ge(gath, 16 * 4 * B)

            @block.vector
            def _(dve):
                link = Chain(dve, chain_s)
                for b in range(B):
                    dve.wait_ge(pt_rdy, b + 1)
                    nc.vector.tensor_copy(place_t[:, b, :], x_ps[:, b % 2, 0:P]).then_inc(pt_free, 1)
                dve.wait_ge(loaded, 16 * (B + 2))
                dve.wait_ge(iota_s, 7)
                link(nc.vector.memset(zero[:, :], 0.0))
                link(nc.vector.tensor_scalar(ends_i[:, :, :], ends_i[:, :, :], 7, None, ALU.arith_shift_right))
                link(nc.vector.tensor_copy(lo[:, 0, :], ends_i[:, 0, :]))
                link(nc.vector.tensor_copy(hi[:, 0, :], ends_i[:, 1, :]))
                link(nc.vector.tensor_copy(prev[:, 0, :], ends_i[:, 2, :]))
                for n, out in enumerate((lo, hi, prev)):
                    for b in range(B):
                        link(nc.vector.tensor_scalar(cmp49[:, :], k.bucket_end[:, :], pos[:, n, b:b + 1], None, ALU.is_le))
                        link(nc.vector.tensor_reduce(out[:, 1, b:b + 1], cmp49[:, :], AX.X, ALU.add))
                link(nc.vector.memset(prev[0:1, 1, 0:1], -1.0))
                link(nc.vector.tensor_scalar(valid[:, :], tidx[:, :], float(EDGE_TILES) - 0.5, None, ALU.is_lt))
                link(nc.vector.tensor_tensor(cnt[:, :, :], hi[:, :, :], lo[:, :, :], ALU.subtract))
                nc.vector.tensor_scalar(cnt[:, :, :], cnt[:, :, :], 1.0, None, ALU.add).then_inc(cnt_rdy, 1)
                dve.wait_ge(summed, 1)
                for w in range(2):
                    link(nc.vector.tensor_tensor_scan(inc[:, w, :], m_ps[:, 1, w, :], zero[:, :], 0.0, ALU.add, ALU.add))
                link(nc.vector.tensor_tensor(tot[:, :, :], inc[:, :, :], m_ps[:, 1, :, :], ALU.subtract))
                link(nc.vector.tensor_tensor(start[:, :, :], tot[:, :, :], m_ps[:, 0, :, :], ALU.add))
                for w in range(2):
                    link(nc.vector.tensor_tensor(inc[:, w, :], lo[:, w, :], prev[:, w, :], ALU.subtract))
                    link(nc.vector.tensor_scalar(inc[:, w, :], inc[:, w, :], -1.0, None, ALU.add))
                    link(nc.vector.tensor_tensor(wgt[:, w, :, 1], inc[:, w, :], valid[:, :], ALU.mult))
                    link(nc.vector.tensor_copy(wgt[:, w, :, 0], valid[:, :]))
                    for b in range(B):
                        link(nc.vector.tensor_scalar(cmp[:, w, b, :], kk[:, 0:STEPS], start[:, w, b:b + 1], None, ALU.is_ge))
                    nc.vector.tensor_scalar(cmp49[:, 0:1], kk[:, 0:1], 0.0, None, ALU.mult).then_inc(cmp_rdy, 1)
                    dve.wait_ge(cmp_rdy, w + 1)
                for w in range(2):
                    for f in range(2):
                        dve.wait_ge(row_ps_rdy, 2 * w + f + 1)
                        nc.vector.tensor_copy(row[0:1, w, f, :].rearrange("p (h c) -> p h c", h=2),
                                              r_ps[0:1, :, 0:HALF]).then_inc(row_free, 1)
                        dve.wait_ge(row_free, 2 * w + f + 1)
                    link(nc.vector.tensor_scalar(row[0:1, w, 0, :], row[0:1, w, 0, :], -1.0, None, ALU.add))
                    link(nc.vector.tensor_tensor(row[0:1, w, 1, :], row[0:1, w, 1, :], krow[0:1, :], ALU.add))
                    link(nc.vector.tensor_scalar(row[0:1, w, 1, :], row[0:1, w, 1, :], float(NODE_TILES), None, ALU.min))
                    e_list, n_list = (k.e_list, k.n_list) if w == 0 else (e_list2, n_list2)
                    link(nc.vector.tensor_copy(e_list[0:1, 0:STEPS], row[0:1, w, 0, :]))
                    link(nc.vector.memset(n_list[0:1, 0:1], NODE_TILES))
                    link(nc.vector.tensor_copy(n_list[0:1, 1:STEPS + 1], row[0:1, w, 1, :]))
                    link(nc.vector.memset(n_list[0:1, STEPS + 1:STEP_COLS], NODE_TILES))
                    link(nc.vector.memset(e_list[0:1, STEPS:STEP_COLS], EDGE_TILES - 1))
                nc.vector.tensor_scalar(n_row[0:1, :], row[0:1, 1, 1, :], float(P), None, ALU.mult).then_inc(n_rdy, 1)
                dve.wait_ge(col_rdy, 1)
                link(nc.vector.memset(colv[:, :, :], 0.0))
                link(nc.vector.memset(colv[:, B - 1, 0:1], float(EDGE_TILES)))
                link(nc.vector.tensor_copy(colv[:, 0:B - 1, :], c_ps[:, 0:B - 1, :]))
                link(nc.vector.tensor_copy(colv[0:STEPS - (B - 1) * P, B - 1, :], c_ps[0:STEPS - (B - 1) * P, B - 1, :]))
                link(nc.vector.tensor_scalar(colv[:, :, 0], colv[:, :, 0], -1.0, None, ALU.add))
                link(nc.vector.tensor_tensor(n128[:, :], colv[:, :, 1], kcol[:, :], ALU.add))
                link(nc.vector.tensor_scalar(n128[:, :], n128[:, :], float(P), None, ALU.mult))
                nc.vector.tensor_copy(e_idx[:, :], colv[:, :, 0]).then_inc(idx_rdy, 1)
                dve.wait_ge(gath, 16 * 4 * B)
                link(nc.vector.tensor_copy(rows_f[:, :, :, :], rows_i[:, :, :, :]))
                for b in range(B):
                    link(nc.vector.tensor_scalar(rows_f[:, 1, b, :], rows_f[:, 1, b, :], n128[:, b:b + 1], None, ALU.subtract))
                link(nc.vector.tensor_scalar(inside[:, :, :], rows_f[:, 1, :, :], 0.0, None, ALU.is_ge))
                link(nc.vector.scalar_tensor_tensor(inside[:, :, :], rows_f[:, 1, :, :], P - 0.5, inside[:, :, :], ALU.is_lt, ALU.mult))
                link(nc.vector.scalar_tensor_tensor(rows_p[:, :, :], rows_p[:, :, :], -float(OUT_OF_BOUNDS), inside[:, :, :], ALU.add, ALU.mult))
                nc.vector.tensor_scalar(rows_p[:, :, :], rows_p[:, :, :], float(OUT_OF_BOUNDS), None, ALU.add).then_inc(rows_rdy, 1)
                m = 0
                for b in range(B):
                    for dest in (k.step_src, k.step_rel, k.step_w, k.step_place):
                        m += 1
                        dve.wait_ge(x_rdy, m)
                        nc.vector.tensor_copy(dest[:, b * P:(b + 1) * P], x_ps[:, m % 2, 0:P]).then_inc(x_free, 1)
                dve.wait_ge(x_free, m)

            @block.tensor
            def _(pe):
                for b in range(B):
                    if b >= 2:
                        pe.wait_ge(pt_free, b - 1)
                    nc.tensor.transpose(x_ps[:, b % 2, 0:P], k.place[:, b * P:(b + 1) * P], k.ident[:, :]).then_inc(pt_rdy, 1)
                pe.wait_ge(cnt_rdy, 1)
                nc.tensor.matmul(m_ps[:, 0, :, :], k.upper[:, :], cnt[:, :, :], start=True, stop=True)
                nc.tensor.matmul(m_ps[:, 1, :, :], k.ones[:, :], cnt[:, :, :], start=True, stop=True).then_inc(summed, 1)
                for w in range(2):
                    pe.wait_ge(cmp_rdy, w + 1)
                    for f in range(2):
                        if w or f:
                            pe.wait_ge(row_free, 2 * w + f)
                        for h in range(2):
                            for b in range(B):
                                last = nc.tensor.matmul(r_ps[0:1, h, 0:HALF], wgt[:, w, b, f:f + 1],
                                                        cmp[:, w, b, h * HALF:(h + 1) * HALF], start=(b == 0), stop=(b == B - 1))
                        last.then_inc(row_ps_rdy, 1)
                for q in range(B):
                    m = min(P, STEPS - q * P)
                    for b in range(B):
                        last = nc.tensor.matmul(c_ps[0:m, q, :], cmp[:, 0, b, q * P:q * P + m], wgt[:, 0, b, :],
                                                start=(b == 0), stop=(b == B - 1))
                last.then_inc(col_rdy, 1)
                pe.wait_ge(rows_rdy, 1)
                m = 0
                for b in range(B):
                    for src in (rows_f[:, 0, b, :], rows_f[:, 1, b, :], rows_w[:, b, :], rows_p[:, b, :]):
                        m += 1
                        if m > 2:
                            pe.wait_ge(x_free, m - 2)
                        else:
                            pe.wait_ge(pt_free, B)
                        nc.tensor.transpose(x_ps[:, m % 2, 0:P], src, k.ident[:, :]).then_inc(x_rdy, 1)


class Kernel:
    pass


def persistent(nc, c, k):
    sb = lambda n, s, d: c.enter_context(nc.sbuf_tensor(n, s, d))
    k.ident = sb("ident", [P, P], F32)
    k.iota = sb("iota", [P, P], F32)
    k.ones = sb("ones", [P, P], F32)
    k.upper = sb("upper", [P, P], F32)
    k.cnt = sb("cnt", [P, 2, NODE_TILES], F32)
    k.bucket_end = sb("bucket_end", [P, NODE_TILES], F32)
    k.e_list = sb("e_list", [1, STEP_COLS], I32)
    k.n_list = sb("n_list", [1, STEP_COLS], I32)
    k.step_src = sb("step_src", [P, STEP_COLS], I32)
    k.step_rel = sb("step_rel", [P, STEP_COLS], F32)
    k.step_w = sb("step_w", [P, STEP_COLS], F32)
    k.step_place = sb("step_place", [P, STEP_COLS], I32)
    k.batches = sb("batches", [P, 1], I32)
    k.dinv = sb("dinv", [P, NODE_TILES], F32)
    k.rot_t = sb("rot_t", [P, 2, D], F32)


class Project:

    def __init__(self, sem, name):
        self.src_ready = sem(name + "_src_ready")
        self.turned = sem(name + "_turned")
        self.copied = sem(name + "_copied")
        self.product = sem(name + "_product")
        self.used = sem(name + "_used")


def pe_project(nc, pe, k, g, s, src, parts, turned_ps, turned_sb, outs):
    def turn(u):
        if u == 0:
            pe.wait_ge(s.src_ready, g + 1)
        pe.wait_ge(s.copied, g * GROUP + max(u - 1, 0))
        for q in range(parts):
            last = nc.tensor.transpose(turned_ps[:, u % 2, q * P:(q + 1) * P], src[:, u, q * P:(q + 1) * P], k.ident[:, :])
        last.then_inc(s.turned, 1)

    def multiply(u):
        pe.wait_ge(s.copied, g * GROUP + (u + 1))
        pe.wait_ge(s.used, g * GROUP + max(u - 1, 0))
        for out, w in outs:
            width = w.shape[-1]
            for q in range(parts):
                last = nc.tensor.matmul(out[:, u % 2, 0:width], turned_sb[:, u % 2, q * P:(q + 1) * P], w[:, q, :],
                                        start=(q == 0), stop=(q == parts - 1))
        last.then_inc(s.product, 1)

    turn(0)
    for u in range(GROUP):
        if u + 1 < GROUP:
            turn(u + 1)
        multiply(u)


def act_project(nc, act, g, s, parts, turned_ps, turned_sb, scale=None, bias=None):
    for u in range(GROUP):
        act.wait_ge(s.turned, g * GROUP + (u + 1))
        act.wait_ge(s.product, g * GROUP + max(u - 1, 0))
        if scale is None:
            nc.scalar.copy(turned_sb[:, u % 2, 0:parts * P], turned_ps[:, u % 2, 0:parts * P]).then_inc(s.copied, 1)
        else:
            for q in range(parts):
                last = nc.scalar.activation(turned_sb[:, u % 2, q * P:(q + 1) * P], turned_ps[:, u % 2, q * P:(q + 1) * P],
                                            ACT.Identity, scale=scale[:, q:q + 1], bias=bias[:, q:q + 1])
            last.then_inc(s.copied, 1)


def dve_norm(nc, dve, link, g, n, per_group, sb, x, out):
    for u in range(GROUP):
        link(nc.vector.bn_stats(sb.stats[:, u, :], x[:, u, :]))
    settle(dve, sb.settled)
    for u in range(GROUP):
        nc.vector.bn_aggr(sb.mv[:, u, :], sb.stats[:, u, :]).then_inc(sb.aggregated, 1)
    dve.wait_ge(sb.aggregated, (g * per_group + (n + 1)) * GROUP)
    nc.vector.tensor_scalar(sb.var[:, :], sb.mv[:, :, 1], EPS, None, ALU.add).then_inc(sb.var_ready, 1)
    dve.wait_ge(sb.root_ready, g * per_group + (n + 1))
    link(nc.vector.reciprocal(sb.rstd[:, :], sb.root[:, :]))
    for u in range(GROUP):
        link(nc.vector.tensor_scalar(out[:, u, :], x[:, u, :], sb.mv[:, u, 0:1], sb.rstd[:, u:u + 1], ALU.subtract, ALU.mult))


NORM_LINKS = 2 * GROUP + 1


def act_root(nc, act, g, n, per_group, sb):
    act.wait_ge(sb.var_ready, g * per_group + (n + 1))
    nc.scalar.activation(sb.root[:, :], sb.var[:, :], ACT.Sqrt).then_inc(sb.root_ready, 1)


def norm_buffers(sb, sem, name):
    b = Kernel()
    b.stats = sb(name + "_stats", [P, GROUP, 6], F32)
    b.mv = sb(name + "_mv", [P, GROUP, 2], F32)
    b.var = sb(name + "_var", [P, GROUP], F32)
    b.root = sb(name + "_root", [P, GROUP], F32)
    b.rstd = sb(name + "_rstd", [P, GROUP], F32)
    b.aggregated, b.settled = sem(name + "_aggregated"), sem(name + "_settled")
    b.var_ready, b.root_ready = sem(name + "_var_ready"), sem(name + "_root_ready")
    return b


def tiles(ap):
    return ap.rearrange("(n p) d -> p n d", p=P)


def node_phase_0(nc, k):
    with phase(nc) as (sb, ps, sem):
        xg, yg = sb("n0_x", [P, GROUP, D]), sb("n0_y", [P, GROUP, D])
        h = sb("n0_h", [P, GROUP, D])
        root49, mask49 = sb("n0_droot", [P, NODE_TILES]), sb("n0_mask", [P, NODE_TILES])
        nb = norm_buffers(sb, sem, "n0")
        loaded, consumed, made, stored = sem("n0_loaded"), sem("n0_consumed"), sem("n0_made"), sem("n0_stored")
        chain_s, deg_ready, deg_root = sem("n0_chain"), sem("n0_deg_ready"), sem("n0_deg_root")
        with nc.Block() as block:
            @block.sync
            def _(sp):
                with sp.Fori(0, GROUPS) as g:
                    sp.wait_ge(consumed, g)
                    sp.dma_start(xg[:, :, :], tiles(k.x)[:, bass.ds(g * GROUP, GROUP), :]).then_inc(loaded, 16)
                    sp.wait_ge(made, g + 1)
                    sp.dma_start(tiles(k.tab_y)[:, bass.ds(g * GROUP, GROUP), :], yg[:, :, :]).then_inc(stored, 16)
                sp.wait_ge(stored, 16 * GROUPS)

            @block.scalar
            def _(act):
                act.wait_ge(deg_ready, 1)
                nc.scalar.activation(root49[:, :], k.dinv[:, :], ACT.Sqrt).then_inc(deg_root, 1)
                with act.Fori(0, GROUPS) as g:
                    act_root(nc, act, g, 0, 1, nb)

            @block.vector
            def _(dve):
                link = Chain(dve, chain_s)
                link(nc.vector.tensor_scalar(mask49[:, :], k.cnt[:, 0, :], 0.0, None, ALU.is_gt))
                nc.vector.tensor_scalar(k.dinv[:, :], k.cnt[:, 0, :], 1.0, None, ALU.max).then_inc(deg_ready, 1)
                dve.wait_ge(deg_root, 1)
                link(nc.vector.reciprocal(k.dinv[:, :], root49[:, :]))
                link(nc.vector.tensor_tensor(k.dinv[:, :], k.dinv[:, :], mask49[:, :], ALU.mult))
                base, per = link.n, NORM_LINKS
                with dve.Fori(0, GROUPS) as g:
                    link.loop(g, per, base)
                    dve.wait_ge(loaded, g * 16 + 16)
                    dve_norm(nc, dve, link, g, 0, 1, nb, xg, h)
                    dve.wait_ge(stored, g * 16)
                    for u in range(GROUP):
                        last = nc.vector.tensor_scalar(yg[:, u, :], h[:, u, :], 0.0, col(k.dinv, g * GROUP + u), ALU.max, ALU.mult)
                    last.then_inc(made, 1)
                    nc.vector.tensor_scalar(nb.var[:, 0:1], nb.rstd[:, 0:1], 0.0, None, ALU.mult).then_inc(consumed, 1)


def pass_0(nc, k):
    with phase(nc) as (sb, ps, sem):
        begun, tiny = sem("begunpass_0"), sb("tinypass_0", [P, 1])
        U, RING = 16, 8
        rows = sb("p0_rows", [P, RING, D])
        idx = sb("p0_idx", [P, U], I32)
        s_mat = sb("p0_s", [P, 2, P])
        acc_ps = [ps(f"p0_acc{i}", [P, 512]) for i in range(2)]
        warm = ps("p0_warm", [P, 512])
        gathered = [sem(f"p0_gathered{r}") for r in range(RING)]
        idx_ready, s_ready, summed, added = sem("p0_idx_ready"), sem("p0_s_ready"), sem("p0_summed"), sem("p0_added")
        with nc.Block() as block:
            @block.gpsimd
            def _(pool):
                nc.gpsimd.memset(tiny[:, :], 0.0).then_inc(begun, 1)
                with pool.Fori(0, STEPS // U) as i:
                    for u in range(U):
                        if u % RING == 0:
                            pool.wait_ge(summed, i * U + u)
                            settle(pool, begun)
                            nc.gpsimd.tensor_copy(idx[:, u:u + RING], col(k.step_src, i * U + u, RING)).then_inc(idx_ready, 1)
                            pool.wait_ge(idx_ready, i * 2 + (u // RING + 1))
                        pool.wait_ge(summed, i * U + (u + 1))
                        settle(pool, begun)
                        pool.indirect_dma_start(out=rows[:, u % RING, :], out_offset=None, in_=k.tab_y,
                                                in_offset=bass.IndirectOffsetOnAxis(ap=idx[:, u:u + 1], axis=0)
                                                ).then_inc(gathered[u % RING], 16)

            @block.vector
            def _(dve):
                nc.vector.memset(k.acc[:, :], 0.0).then_inc(added, 2)
                for u in range(2):
                    nc.vector.tensor_scalar(s_mat[:, u, :], k.iota[:, :], k.step_rel[:, u:u + 1], None, ALU.is_equal).then_inc(s_ready, 1)
                with dve.Fori(0, STEPS // U) as i:
                    for u in range(U):
                        n = dve.value_load(k.n_list[0:1, bass.ds(i * U + (u + 1), 1)], min_val=0, max_val=NODE_TILES)
                        dve.wait_ge(summed, i * U + (RING + u + 1))
                        nc.vector.tensor_scalar(s_mat[:, u % 2, :], k.iota[:, :], col(k.step_rel, i * U + (u + 2)), None,
                                                ALU.is_equal).then_inc(s_ready, 1)
                        dve.wait_ge(added, i * U + (u + 2))
                        nc.vector.tensor_tensor(k.acc[:, bass.ds(n * D, D)], k.acc[:, bass.ds(n * D, D)],
                                                acc_ps[u % 2][:, 0:D], ALU.add).then_inc(added, 1)

            @block.tensor
            def _(pe):
                nc.tensor.transpose(warm[:, 0:P], k.ident[:, :], k.ident[:, :]).then_inc(summed, RING)
                with pe.Fori(0, STEPS // U) as i:
                    for u in range(U):
                        pe.wait_ge(s_ready, i * U + (u + 1))
                        pe.wait_ge(gathered[u % RING], i * (16 * U // RING) + 16 * (u // RING + 1))
                        pe.wait_ge(added, i * U + (u + 1))
                        nc.tensor.matmul(acc_ps[u % 2][:, 0:D], s_mat[:, u % 2, :], rows[:, u % RING, :],
                                         start=True, stop=True).then_inc(summed, 1)


def node_phase_1(nc, k):
    with phase(nc) as (sb, ps, sem):
        part = GROUP * D
        xg, ag, h, z = (k.spare[:, n * part:(n + 1) * part].rearrange("p (n d) -> p n d", d=D) for n in range(4))
        kv = k.spare[:, 4 * part:6 * part].rearrange("p (n d) -> p n d", d=2 * D)
        w0 = sb("n1_w0", [P, 2, D])
        wkvq = sb("n1_wkvq", [P, 2, 3 * D])
        bkvq = sb("n1_bkvq", [P, 3 * D])
        bo = sb("n1_bo", [P, D])
        lng, lnb = sb("n1_lng", [P, 2]), sb("n1_lnb", [P, 2])
        turned_sb = sb("n1_turned", [P, 2, D])
        zt_sb = sb("n1_zt", [P, 2, D])
        turned_ps = ps("n1_turned_ps", [P, 2, 512])
        out_ps = ps("n1_out_ps", [P, 2, 512])
        q_ps = ps("n1_q_ps", [P, 2, 512])
        pa, pb = Project(sem, "n1a"), Project(sem, "n1b")
        nb = norm_buffers(sb, sem, "n1")
        weights, loaded, consumed, stored, chain_s = sem("n1_weights"), sem("n1_loaded"), sem("n1_consumed"), sem("n1_stored"), sem("n1_chain")
        z_psum_free = sem("n1_z_psum_free")
        NW = 7
        with nc.Block() as block:
            @block.sync
            def _(sp):
                sp.dma_start(w0[:, :, :], k.w0.rearrange("(q p) n -> p q n", p=P)).then_inc(weights, 16)
                sp.dma_start(wkvq[:, :, :], k.wkvq.rearrange("(q p) n -> p q n", p=P)).then_inc(weights, 16)
                sp.dma_start(bkvq[:, :], k.bkvq.to_broadcast([P, 3 * D])).then_inc(weights, 16)
                sp.dma_start(bo[:, :], k.bo.to_broadcast([P, D])).then_inc(weights, 16)
                with nc.allow_non_contiguous_dma(reason="small vectors"):
                    sp.dma_start(lng[:, :].unsqueeze(2), k.ln1_g.rearrange("(q p o) -> p q o", p=P, o=1)).then_inc(weights, 16)
                    sp.dma_start(lnb[:, :].unsqueeze(2), k.ln1_b.rearrange("(q p o) -> p q o", p=P, o=1)).then_inc(weights, 16)
                with sp.Fori(0, GROUPS) as g:
                    sp.wait_ge(stored, g * 32)
                    sp.dma_start(xg[:, :, :], tiles(k.x)[:, bass.ds(g * GROUP, GROUP), :]).then_inc(loaded, 16)
                    sp.wait_ge(pb.used, g * GROUP + GROUP)
                    sp.dma_start(tiles(k.tab_x)[:, bass.ds(g * GROUP, GROUP), :], xg[:, :, :]).then_inc(stored, 16)
                    sp.dma_start(tiles(k.tab_kv)[:, bass.ds(g * GROUP, GROUP), :], kv[:, :, :]).then_inc(stored, 16)
                sp.wait_ge(stored, 32 * GROUPS)

            @block.scalar
            def _(act):
                act.wait_ge(weights, 16 * 6)
                with act.Fori(0, GROUPS) as g:
                    act.wait_ge(pa.product, g * GROUP)
                    nc.scalar.copy(ag[:, :, :], k.acc[:, bass.ds(g * (GROUP * D), GROUP * D)].rearrange("p (n d) -> p n d", d=D)
                                   ).then_inc(pa.src_ready, 1)
                    act_project(nc, act, g, pa, 2, turned_ps, turned_sb)
                    act_root(nc, act, g, 0, 2, nb)
                    act_root(nc, act, g, 1, 2, nb)
                    act_project(nc, act, g, pb, 2, turned_ps, zt_sb, lng, lnb)

            @block.vector
            def _(dve):
                link = Chain(dve, chain_s)
                dve.wait_ge(weights, 16 * 6)
                nc.vector.memset(k.node_tab[:, NODE_TILES * D:], 0.0)
                base, per = link.n, 2 * NORM_LINKS + 3
                with dve.Fori(0, GROUPS) as g:
                    link.loop(g, per, base)
                    dve.wait_ge(loaded, g * 16 + 16)
                    for u in range(GROUP):
                        dve.wait_ge(pa.product, g * GROUP + (u + 1))
                        nc.vector.scalar_tensor_tensor(xg[:, u, :], out_ps[:, u % 2, 0:D], col(k.dinv, g * GROUP + u), xg[:, u, :],
                                                       ALU.mult, ALU.add).then_inc(pa.used, 1)
                    dve.wait_ge(pa.used, g * GROUP + GROUP)
                    dve_norm(nc, dve, link, g, 0, 2, nb, xg, h)
                    link(nc.vector.tensor_scalar(h[:, :, :], h[:, :, :], 0.0, None, ALU.max))
                    dve_norm(nc, dve, link, g, 1, 2, nb, h, z)
                    link(nc.vector.tensor_tensor(xg[:, :, :], xg[:, :, :], h[:, :, :], ALU.add))
                    link(nc.vector.tensor_tensor(xg[:, :, :], xg[:, :, :], bo[:, :].unsqueeze(1).to_broadcast([P, GROUP, D]), ALU.add))
                    nc.vector.tensor_scalar(nb.var[:, 0:1], nb.rstd[:, 0:1], 0.0, None, ALU.mult).then_inc(pb.src_ready, 1)
                    for u in range(GROUP):
                        dve.wait_ge(pb.product, g * GROUP + (u + 1))
                        dve.wait_ge(stored, g * 32)
                        nc.vector.tensor_tensor(kv[:, u, :], out_ps[:, u % 2, :], bkvq[:, 0:2 * D], ALU.add)
                        nc.vector.tensor_tensor(k.node_tab[:, bass.ds(g * (GROUP * D) + u * D, D)], q_ps[:, u % 2, 0:D],
                                                bkvq[:, 2 * D:3 * D], ALU.add).then_inc(pb.used, 1)

            @block.tensor
            def _(pe):
                pe.wait_ge(weights, 16 * 6)
                with pe.Fori(0, GROUPS) as g:
                    pe.wait_ge(pb.copied, g * GROUP)
                    pe.wait_ge(pb.used, g * GROUP)
                    pe_project(nc, pe, k, g, pa, ag, 2, turned_ps, turned_sb, [(out_ps, w0)])
                    pe.wait_ge(pa.used, g * GROUP + GROUP)
                    pe_project(nc, pe, k, g, pb, z, 2, turned_ps, zt_sb, [(out_ps, wkvq[:, :, 0:2 * D]), (q_ps, wkvq[:, :, 2 * D:3 * D])])


def reduce_angle(nc, link, out, turns, x, scale, shift):
    link(nc.vector.tensor_scalar(out, x, scale, shift, ALU.mult, ALU.add))
    link(nc.vector.tensor_scalar(turns, out, 1.0 / TWO_PI, ROUND, ALU.mult, ALU.add))
    link(nc.vector.tensor_scalar(turns, turns, -ROUND, None, ALU.add))
    link(nc.vector.scalar_tensor_tensor(out, turns, -TWO_PI_HI, out, ALU.mult, ALU.add))
    link(nc.vector.scalar_tensor_tensor(out, turns, -TWO_PI_LO, out, ALU.mult, ALU.add))
    link(nc.vector.tensor_scalar(out, out, SIN_MAX, -SIN_MAX, ALU.min, ALU.max))


def cutoffs(nc, k):
    with phase(nc) as (sb, ps, sem):
        ang, turns, cosv, mask = (sb("cut_" + n, [P, STEP_COLS]) for n in ("ang", "turns", "cos", "mask"))
        chain_s, ang_ready, cos_ready = sem("cut_chain"), sem("cut_ang_ready"), sem("cut_cos_ready")
        with nc.Block() as block:
            @block.vector
            def _(dve):
                link = Chain(dve, chain_s)
                reduce_angle(nc, link, ang[:, :], turns[:, :], k.step_w[:, :], float(np.pi / CUTOFF), float(np.pi / 2))
                nc.vector.tensor_scalar(mask[:, :], k.step_w[:, :], CUTOFF, 0.5, ALU.is_lt, ALU.mult).then_inc(ang_ready, 1)
                dve.wait_ge(cos_ready, 1)
                dve.wait_ge(ang_ready, 1)
                link(nc.vector.scalar_tensor_tensor(k.step_w[:, :], cosv[:, :], 1.0, mask[:, :], ALU.add, ALU.mult))

            @block.scalar
            def _(act):
                act.wait_ge(ang_ready, 1)
                nc.scalar.activation(cosv[:, :], ang[:, :], ACT.Sin).then_inc(cos_ready, 1)


def pass_1(nc, k):
    with phase(nc) as (sb, ps, sem):
        begun, tiny = sem("begunpass_1"), sb("tinypass_1", [P, 1])
        U, RING = 16, 8
        kv = k.spare[:, 0:RING * 2 * D].rearrange("p (r d) -> p r d", d=2 * D)
        ea = sb("p1_ea", [R + 1, RING, P])
        idx = sb("p1_idx", [P, U], I32)
        wd = sb("p1_wd", [R + 1, 2 * D])
        s_mat = sb("p1_s", [P, 4, P])
        st_sb = sb("p1_st", [P, 2, P])
        dkv = sb("p1_dkv", [P, 2, 2 * D])
        qk, qkd = sb("p1_qk", [P, D]), sb("p1_qkd", [P, D])
        dots, acts, attn = sb("p1_dots", [P, 2]), sb("p1_acts", [P, 2]), sb("p1_attn", [P, 2])
        sa = sb("p1_sa", [P, 2, P])
        msg = sb("p1_msg", [P, 2, D])
        sq_ps = [ps(f"p1_sq{i}", [P, 512]) for i in range(2)]
        d_ps = [ps(f"p1_d{i}", [P, 512]) for i in range(2)]
        acc_ps = [ps(f"p1_acc{i}", [P, 512]) for i in range(2)]
        warm = ps("p1_warm", [P, 512])
        gathered = [sem(f"p1_gathered{r}") for r in range(RING)]
        ea_loaded = [sem(f"p1_ea_loaded{r}") for r in range(RING)]
        weights, idx_ready, acc_zero = sem("p1_weights"), sem("p1_idx_ready"), sem("p1_acc_zero")
        s_ready, turned, st_ready = sem("p1_s_ready"), sem("p1_turned"), sem("p1_st_ready")
        d_made, silu_done, q_made, qk_done = sem("p1_d_made"), sem("p1_silu_done"), sem("p1_q_made"), sem("p1_qk_done")
        dot_done, act_done, attn_ready = sem("p1_dot_done"), sem("p1_act_done"), sem("p1_attn_ready")
        msg_ready, summed, added = sem("p1_msg_ready"), sem("p1_summed"), sem("p1_added")
        with nc.Block() as block:
            @block.sync
            def _(sp):
                sp.dma_start(wd[:, :], k.wd).then_inc(weights, 16)
                with sp.Fori(0, STEPS // U) as i:
                    for u in range(U):
                        e = sp.value_load(k.e_list[0:1, bass.ds(i * U + u, 1)], min_val=0, max_val=EDGE_TILES - 1)
                        sp.wait_ge(d_made, i * U + (u + 1))
                        sp.dma_start(ea[:, u % RING, :], k.ea_t[:, bass.ds(e * P, P)]).then_inc(ea_loaded[u % RING], 16)
                for r in range(RING):
                    sp.wait_ge(ea_loaded[r], 16 * STEPS // RING)

            @block.gpsimd
            def _(pool):
                nc.gpsimd.memset(tiny[:, :], 0.0).then_inc(begun, 1)
                with pool.Fori(0, STEPS // U) as i:
                    for u in range(U):
                        if u % RING == 0:
                            pool.wait_ge(msg_ready, i * U + u)
                            settle(pool, begun)
                            nc.gpsimd.tensor_copy(idx[:, u:u + RING], col(k.step_src, i * U + u, RING)).then_inc(idx_ready, 1)
                            pool.wait_ge(idx_ready, i * 2 + (u // RING + 1))
                        pool.wait_ge(msg_ready, i * U + (u + 1))
                        settle(pool, begun)
                        pool.indirect_dma_start(out=kv[:, u % RING, :], out_offset=None, in_=k.tab_kv,
                                                in_offset=bass.IndirectOffsetOnAxis(ap=idx[:, u:u + 1], axis=0)
                                                ).then_inc(gathered[u % RING], 16)

            @block.vector
            def _(dve):
                nc.vector.memset(msg[:, :, :], 0.0)
                nc.vector.memset(sa[:, :, :], 0.0)
                nc.vector.memset(k.acc[:, :], 0.0).then_inc(acc_zero, 1)
                dve.wait_ge(acc_zero, 1)
                nc.vector.tensor_scalar(qk[:, 0:1], k.iota[:, 0:1], 0.0, None, ALU.mult).then_inc(msg_ready, RING)
                for u in range(2):
                    nc.vector.tensor_scalar(s_mat[:, u, :], k.iota[:, :], k.step_rel[:, u:u + 1], None, ALU.is_equal).then_inc(s_ready, 1)
                nc.vector.tensor_scalar(qkd[:, 0:1], k.iota[:, 0:1], 0.0, None, ALU.mult).then_inc(added, 1)
                with dve.Fori(0, STEPS // U) as i:
                    for u in range(U):
                        n = dve.value_load(k.n_list[0:1, bass.ds(i * U + u, 1)], min_val=0, max_val=NODE_TILES)
                        dve.wait_ge(q_made, i * U + (u + 1))
                        nc.vector.tensor_scalar(s_mat[:, (u + 2) % 4, :], k.iota[:, :], col(k.step_rel, i * U + (u + 2)), None,
                                                ALU.is_equal).then_inc(s_ready, 1)
                        dve.wait_ge(gathered[u % RING], i * (16 * U // RING) + 16 * (u // RING + 1))
                        nc.vector.tensor_tensor(qk[:, :], sq_ps[u % 2][:, P:P + D], kv[:, u % RING, 0:D], ALU.mult).then_inc(qk_done, 1)
                        dve.wait_ge(silu_done, i * U + (u + 1))
                        dve.wait_ge(qk_done, i * U + (u + 1))
                        nc.vector.tensor_tensor_reduce(out=qkd[:, :], in0=qk[:, :], in1=dkv[:, u % 2, 0:D], scale=1.0, scalar=0.0,
                                                       op0=ALU.mult, op1=ALU.add, accum_out=dots[:, u % 2:u % 2 + 1]
                                                       ).then_inc(dot_done, 1)
                        dve.wait_ge(summed, i * U + u)
                        nc.vector.tensor_tensor(msg[:, u % 2, :], kv[:, u % RING, D:2 * D], dkv[:, u % 2, D:2 * D], ALU.mult)
                        dve.wait_ge(summed, i * U + (u + 1))
                        dve.wait_ge(added, i * U + (u + 1))
                        nc.vector.tensor_tensor(k.acc[:, bass.ds(n * D, D)], k.acc[:, bass.ds(n * D, D)],
                                                acc_ps[(u + 1) % 2][:, 0:D], ALU.add).then_inc(added, 1)
                        dve.wait_ge(attn_ready, i * U + (u + 1))
                        nc.vector.tensor_scalar(sa[:, u % 2, :], s_mat[:, u % 4, :], attn[:, u % 2:u % 2 + 1], None,
                                                ALU.mult).then_inc(msg_ready, 1)
                n = dve.value_load(k.n_list[0:1, STEPS:STEPS + 1], min_val=0, max_val=NODE_TILES)
                dve.wait_ge(summed, STEPS + 1)
                dve.wait_ge(added, STEPS + 1)
                nc.vector.tensor_tensor(k.acc[:, bass.ds(n * D, D)], k.acc[:, bass.ds(n * D, D)], acc_ps[1][:, 0:D], ALU.add).then_inc(added, 1)
                dve.wait_ge(added, STEPS + 2)

            @block.scalar
            def _(act):
                def prepare(i, s, n):
                    act.wait_ge(turned, n + 1)
                    nc.scalar.copy(st_sb[:, s % 2, :], sq_ps[s % 2][:, 0:P]).then_inc(st_ready, 1)
                    act.wait_ge(d_made, n + (RING + 1))
                    if s >= 2 or i is not None:
                        act.wait_ge(msg_ready, n + (RING - 1))
                    nc.scalar.activation(dkv[:, s % 2, :], d_ps[s % 2][:, :], ACT.Silu).then_inc(silu_done, 1)

                def attention(u, n):
                    act.wait_ge(dot_done, n + 1)
                    nc.scalar.activation(acts[:, u % 2:u % 2 + 1], dots[:, u % 2:u % 2 + 1], ACT.Silu).then_inc(act_done, 1)
                    act.wait_ge(act_done, n + 1)
                    nc.scalar.activation(attn[:, u % 2:u % 2 + 1], acts[:, u % 2:u % 2 + 1], ACT.Copy,
                                         scale=col(k.step_w, n)).then_inc(attn_ready, 1)

                prepare(None, 0, 0)
                with act.Fori(0, STEPS // U - 1) as i:
                    for u in range(U):
                        prepare(i, u + 1, i * U + (u + 1))
                        attention(u, i * U + u)
                last = STEPS - U
                for u in range(U):
                    if u + 1 < U:
                        prepare(STEPS // U - 1, u + 1, last + u + 1)
                    attention(u, last + u)

            @block.tensor
            def _(pe):
                def prepare(i, s, n):
                    if i is not None:
                        pe.wait_ge(qk_done, n - 1)
                    pe.wait_ge(s_ready, n + 1)
                    nc.tensor.transpose(sq_ps[s % 2][:, 0:P], s_mat[:, s % 4, :], k.ident[:, :]).then_inc(turned, 1)
                    if i is not None:
                        pe.wait_ge(silu_done, n - 1)
                    if s < U:
                        pe.wait_ge(ea_loaded[s % RING], (0 if i is None else i * (16 * U // RING)) + 16 * (s // RING + 1))
                    else:
                        pe.wait_ge(ea_loaded[0], i * (16 * U // RING) + (16 * U // RING + 16))
                    nc.tensor.matmul(d_ps[s % 2][:, :], ea[:, s % RING, :], wd[:, :], start=True, stop=True).then_inc(d_made, 1)
                    t = pe.value_load(k.n_list[0:1, bass.ds(n + 1, 1)], min_val=0, max_val=NODE_TILES)
                    pe.wait_ge(st_ready, n + 1)
                    nc.tensor.matmul(sq_ps[s % 2][:, P:P + D], st_sb[:, s % 2, :], k.node_tab[:, bass.ds(t * D, D)],
                                     start=True, stop=True).then_inc(q_made, 1)

                def sum_messages(u, n):
                    pe.wait_ge(added, n)
                    pe.wait_ge(msg_ready, n + (RING + 1))
                    nc.tensor.matmul(acc_ps[u % 2][:, 0:D], sa[:, u % 2, :], msg[:, u % 2, :], start=True, stop=True).then_inc(summed, 1)

                pe.wait_ge(weights, 16)
                nc.tensor.transpose(warm[:, 0:P], k.ident[:, :], k.ident[:, :]).then_inc(d_made, RING)
                pe.wait_ge(acc_zero, 1)
                nc.tensor.matmul(acc_ps[1][:, 0:D], sa[:, 1, :], msg[:, 1, :], start=True, stop=True).then_inc(summed, 1)
                prepare(None, 0, 0)
                with pe.Fori(0, STEPS // U - 1) as i:
                    for u in range(U):
                        prepare(i, u + 1, i * U + (u + 1))
                        sum_messages(u, i * U + u)
                last = STEPS - U
                for u in range(U):
                    if u + 1 < U:
                        prepare(STEPS // U - 1, u + 1, last + u + 1)
                    sum_messages(u, last + u)


def node_phase_2(nc, k):
    with phase(nc) as (sb, ps, sem):
        xg = sb("n2_x", [P, GROUP, D])
        ag = sb("n2_acc", [P, GROUP, D])
        h = sb("n2_h", [P, GROUP, D])
        wo = sb("n2_wo", [P, 2, D])
        turned_sb = sb("n2_turned", [P, 2, D])
        turned_ps, out_ps = ps("n2_turned_ps", [P, 2, 512]), ps("n2_out_ps", [P, 2, 512])
        pa = Project(sem, "n2a")
        nb = norm_buffers(sb, sem, "n2")
        weights, loaded, made, stored, chain_s = sem("n2_weights"), sem("n2_loaded"), sem("n2_made"), sem("n2_stored"), sem("n2_chain")
        with nc.Block() as block:
            @block.sync
            def _(sp):
                sp.dma_start(wo[:, :, :], k.wo.rearrange("(q p) n -> p q n", p=P)).then_inc(weights, 16)
                with sp.Fori(0, GROUPS) as g:
                    sp.wait_ge(stored, g * 32)
                    sp.dma_start(xg[:, :, :], tiles(k.tab_x)[:, bass.ds(g * GROUP, GROUP), :]).then_inc(loaded, 16)
                    sp.wait_ge(made, g + 1)
                    sp.dma_start(tiles(k.tab_x2)[:, bass.ds(g * GROUP, GROUP), :], xg[:, :, :]).then_inc(stored, 16)
                    sp.dma_start(tiles(k.tab_h)[:, bass.ds(g * GROUP, GROUP), :], h[:, :, :]).then_inc(stored, 16)
                sp.wait_ge(stored, 32 * GROUPS)

            @block.scalar
            def _(act):
                with act.Fori(0, GROUPS) as g:
                    act.wait_ge(pa.product, g * GROUP)
                    nc.scalar.copy(ag[:, :, :], k.acc[:, bass.ds(g * (GROUP * D), GROUP * D)].rearrange("p (n d) -> p n d", d=D)
                                   ).then_inc(pa.src_ready, 1)
                    act_project(nc, act, g, pa, 2, turned_ps, turned_sb)
                    act_root(nc, act, g, 0, 1, nb)

            @block.vector
            def _(dve):
                link = Chain(dve, chain_s)
                with dve.Fori(0, GROUPS) as g:
                    link.loop(g, NORM_LINKS + 1, 0)
                    dve.wait_ge(loaded, g * 16 + 16)
                    for u in range(GROUP):
                        dve.wait_ge(pa.product, g * GROUP + (u + 1))
                        nc.vector.tensor_tensor(xg[:, u, :], out_ps[:, u % 2, 0:D], xg[:, u, :], ALU.add).then_inc(pa.used, 1)
                    dve.wait_ge(pa.used, g * GROUP + GROUP)
                    dve_norm(nc, dve, link, g, 0, 1, nb, xg, h)
                    link(nc.vector.tensor_scalar(h[:, :, :], h[:, :, :], 0.0, None, ALU.max))
                    nc.vector.tensor_copy(k.node_tab[:, bass.ds(g * (GROUP * D), GROUP * D)].rearrange("p (n d) -> p n d", d=D),
                                          h[:, :, :]).then_inc(made, 1)

            @block.tensor
            def _(pe):
                pe.wait_ge(weights, 16)
                with pe.Fori(0, GROUPS) as g:
                    pe_project(nc, pe, k, g, pa, ag, 2, turned_ps, turned_sb, [(out_ps, wo)])


def pass_2(nc, k):
    with phase(nc) as (sb, ps, sem):
        begun, tiny = sem("begunpass_2"), sb("tinypass_2", [P, 1])
        U, RING, LEAD = 16, 8, 4
        SLOT = D + SORT_ROW
        slot = sb("p2_slot", [P, RING, SLOT])
        gidx, pidx = sb("p2_gidx", [P, RING], I32), sb("p2_pidx", [P, RING], I32)
        s_mat = sb("p2_s", [P, 4, P])
        st_sb = sb("p2_st", [P, 2, P])
        h_ps = [ps(f"p2_h{i}", [P, 512]) for i in range(2)]
        acc_ps = [ps(f"p2_acc{i}", [P, 512]) for i in range(2)]
        gathered = [sem(f"p2_gathered{r}") for r in range(RING)]
        e_loaded = [sem(f"p2_e_loaded{r}") for r in range(RING)]
        scattered = [sem(f"p2_scattered{r}") for r in range(RING)]
        gidx_ready, pidx_ready = sem("p2_gidx_ready"), sem("p2_pidx_ready")
        s_ready, turned, st_ready, h_made, h_copied = sem("p2_s_ready"), sem("p2_turned"), sem("p2_st_ready"), sem("p2_h_made"), sem("p2_h_copied")
        summed, added, zeroed = sem("p2_summed"), sem("p2_added"), sem("p2_zeroed")
        W = 2 * D
        per = 16 * U // RING
        with nc.Block() as block:
            @block.sync
            def _(sp):
                with sp.Fori(0, STEPS // U) as i:
                    for u in range(U):
                        r = u % RING
                        e = sp.value_load(k.e_list[0:1, bass.ds(i * U + u, 1)], min_val=0, max_val=EDGE_TILES - 1)
                        sp.wait_ge(scattered[r], i * per + 16 * (u // RING))
                        sp.dma_start(slot[:, r, D:2 * D], tiles(k.e256)[:, bass.ds(e, 1), :].rearrange("p o d -> p (o d)")
                                     ).then_inc(e_loaded[r], 16)
                for r in range(RING):
                    sp.wait_ge(e_loaded[r], 16 * STEPS // RING)

            @block.gpsimd
            def _(pool):
                def gather(u, n, count):
                    r = u % RING
                    pool.wait_ge(scattered[r], count)
                    settle(pool, begun)
                    pool.indirect_dma_start(out=slot[:, r, 0:D], out_offset=None, in_=k.tab_h,
                                            in_offset=bass.IndirectOffsetOnAxis(ap=gidx[:, r:r + 1], axis=0)).then_inc(gathered[r], 16)

                nc.gpsimd.memset(tiny[:, :], 0.0).then_inc(begun, 1)
                nc.gpsimd.memset(slot[:, :, 3 * D:SLOT], 0.0).then_inc(zeroed, 1)
                nc.gpsimd.tensor_copy(gidx[:, 0:LEAD], k.step_src[:, 0:LEAD]).then_inc(gidx_ready, 1)
                pool.wait_ge(gidx_ready, 1)
                for u in range(LEAD):
                    gather(u, u, 0)
                with pool.Fori(0, STEPS // U) as i:
                    for u in range(U):
                        r = u % RING
                        if u % LEAD == 0:
                            q = (r + LEAD) % RING
                            for x in range(LEAD):
                                pool.wait_ge(scattered[q + x], i * per + 16 * ((u + LEAD) // RING))
                            settle(pool, begun)
                            nc.gpsimd.tensor_copy(gidx[:, q:q + LEAD], col(k.step_src, i * U + (u + LEAD), LEAD)).then_inc(gidx_ready, 1)
                            for x in range(LEAD):
                                pool.wait_ge(scattered[r + x], i * per + 16 * (u // RING))
                            settle(pool, begun)
                            nc.gpsimd.tensor_copy(pidx[:, r:r + LEAD], col(k.step_place, i * U + u, LEAD)).then_inc(pidx_ready, 1)
                            pool.wait_ge(gidx_ready, i * (U // LEAD) + (u // LEAD + 2))
                            pool.wait_ge(pidx_ready, i * (U // LEAD) + (u // LEAD + 1))
                        gather(u + LEAD, None, i * per + 16 * ((u + LEAD) // RING))
                        pool.wait_ge(e_loaded[r], i * per + 16 * (u // RING + 1))
                        pool.wait_ge(h_copied, i * U + (u + 1))
                        pool.wait_ge(summed, i * U + (u + 1))
                        settle(pool, begun)
                        pool.indirect_dma_start(out=k.tab_sorted, out_offset=bass.IndirectOffsetOnAxis(ap=pidx[:, r:r + 1], axis=0),
                                                in_=slot[:, r, D:SLOT], in_offset=None,
                                                bounds_check=EDGES_PAD - 1, oob_is_err=False).then_inc(scattered[r], 16)
                for r in range(RING):
                    pool.wait_ge(scattered[r], 16 * STEPS // RING)
                    pool.wait_ge(gathered[r], 16 * STEPS // RING + (16 if r < LEAD else 0))

            @block.vector
            def _(dve):
                nc.vector.memset(k.acc2[:, :], 0.0).then_inc(added, 2)
                for u in range(2):
                    nc.vector.tensor_scalar(s_mat[:, u, :], k.iota[:, :], k.step_rel[:, u:u + 1], None, ALU.is_equal).then_inc(s_ready, 1)
                with dve.Fori(0, STEPS // U) as i:
                    for u in range(U):
                        n = dve.value_load(k.n_list[0:1, bass.ds(i * U + (u + 1), 1)], min_val=0, max_val=NODE_TILES)
                        nc.vector.tensor_scalar(s_mat[:, (u + 2) % 4, :], k.iota[:, :], col(k.step_rel, i * U + (u + 2)), None,
                                                ALU.is_equal).then_inc(s_ready, 1)
                        dve.wait_ge(summed, i * U + (u + 1))
                        dve.wait_ge(added, i * U + (u + 2))
                        nc.vector.tensor_tensor(k.acc2[:, bass.ds(n * W, W)], k.acc2[:, bass.ds(n * W, W)],
                                                acc_ps[u % 2][:, :], ALU.add).then_inc(added, 1)
                dve.wait_ge(added, STEPS + 2)

            @block.scalar
            def _(act):
                with act.Fori(0, STEPS // U) as i:
                    for u in range(U):
                        r = u % RING
                        act.wait_ge(turned, i * U + (u + 1))
                        nc.scalar.copy(st_sb[:, u % 2, :], h_ps[u % 2][:, 0:P]).then_inc(st_ready, 1)
                        act.wait_ge(scattered[r], i * per + 16 * (u // RING))
                        if u == 0:
                            act.wait_ge(zeroed, 1)
                        nc.scalar.copy(slot[:, r, 3 * D:3 * D + 1], col(k.step_src, i * U + u))
                        act.wait_ge(h_made, i * U + (u + 1))
                        nc.scalar.copy(slot[:, r, 2 * D:3 * D], h_ps[u % 2][:, P:P + D]).then_inc(h_copied, 1)

            @block.tensor
            def _(pe):
                def turn(s, n):
                    pe.wait_ge(s_ready, n + 1)
                    nc.tensor.transpose(h_ps[s % 2][:, 0:P], s_mat[:, s % 4, :], k.ident[:, :]).then_inc(turned, 1)

                turn(0, 0)
                with pe.Fori(0, STEPS // U) as i:
                    for u in range(U):
                        r = u % RING
                        t = pe.value_load(k.n_list[0:1, bass.ds(i * U + (u + 1), 1)], min_val=0, max_val=NODE_TILES)
                        pe.wait_ge(h_copied, i * U + u)
                        turn(u + 1, i * U + (u + 1))
                        pe.wait_ge(st_ready, i * U + (u + 1))
                        nc.tensor.matmul(h_ps[u % 2][:, P:P + D], st_sb[:, u % 2, :], k.node_tab[:, bass.ds(t * D, D)],
                                         start=True, stop=True).then_inc(h_made, 1)
                        pe.wait_ge(gathered[r], i * per + 16 * (u // RING + 1))
                        pe.wait_ge(e_loaded[r], i * per + 16 * (u // RING + 1))
                        pe.wait_ge(added, i * U + (u + 1))
                        nc.tensor.matmul(acc_ps[u % 2][:, :], s_mat[:, u % 4, :], slot[:, r, 0:W], start=True, stop=True).then_inc(summed, 1)


def node_phase_3(nc, k):
    with phase(nc) as (sb, ps, sem):
        ag = sb("n3_acc", [P, GROUP, 2 * D])
        fg = sb("n3_f", [P, GROUP, D])
        w = sb("n3_w", [P, 4, D])
        b = sb("n3_b", [P, D])
        turned_sb = sb("n3_turned", [P, 2, 2 * D])
        turned_ps, out_ps = ps("n3_turned_ps", [P, 2, 512]), ps("n3_out_ps", [P, 2, 512])
        pa = Project(sem, "n3a")
        weights, stored = sem("n3_weights"), sem("n3_stored")
        with nc.Block() as block:
            @block.sync
            def _(sp):
                sp.dma_start(w[:, :, :], k.wf.rearrange("(q p) n -> p q n", p=P)).then_inc(weights, 16)
                sp.dma_start(b[:, :], k.bf.to_broadcast([P, D])).then_inc(weights, 16)
                with sp.Fori(0, GROUPS) as g:
                    sp.wait_ge(pa.used, g * GROUP + GROUP)
                    sp.dma_start(tiles(k.tab_f)[:, bass.ds(g * GROUP, GROUP), :], fg[:, :, :]).then_inc(stored, 16)
                sp.wait_ge(stored, 16 * GROUPS)

            @block.scalar
            def _(act):
                with act.Fori(0, GROUPS) as g:
                    act.wait_ge(pa.product, g * GROUP)
                    nc.scalar.copy(ag[:, :, :], k.acc2[:, bass.ds(g * (GROUP * 2 * D), GROUP * 2 * D)].rearrange("p (n d) -> p n d", d=2 * D)
                                   ).then_inc(pa.src_ready, 1)
                    act_project(nc, act, g, pa, 4, turned_ps, turned_sb)

            @block.vector
            def _(dve):
                dve.wait_ge(weights, 32)
                with dve.Fori(0, GROUPS) as g:
                    dve.wait_ge(stored, g * 16)
                    for u in range(GROUP):
                        dve.wait_ge(pa.product, g * GROUP + (u + 1))
                        nc.vector.scalar_tensor_tensor(fg[:, u, :], b[:, :], k.cnt[:, 0, bass.ds(g * GROUP + u, 1)], out_ps[:, u % 2, 0:D],
                                                       ALU.mult, ALU.add).then_inc(pa.used, 1)

            @block.tensor
            def _(pe):
                pe.wait_ge(weights, 32)
                with pe.Fori(0, GROUPS) as g:
                    pe_project(nc, pe, k, g, pa, ag, 4, turned_ps, turned_sb, [(out_ps, w)])


def pass_3(nc, k):
    with phase(nc) as (sb, ps, sem):
        U, RING = 16, 8
        W = 2 * D
        slot = sb("p3_slot", [P, RING, SORT_ROW])
        s_mat = sb("p3_s", [P, 2, P])
        e_list, n_list = sb("p3_e_list", [1, STEP_COLS], I32), sb("p3_n_list", [1, STEP_COLS], I32)
        n128 = sb("p3_n128", [P, STEPS])
        walk = sem("p3_walk")
        acc_ps = [ps(f"p3_acc{i}", [P, 512]) for i in range(2)]
        loaded = [sem(f"p3_loaded{r}") for r in range(RING)]
        s_ready, summed, added = sem("p3_s_ready"), sem("p3_summed"), sem("p3_added")
        warm = ps("p3_warm", [P, 512])
        per = 16 * U // RING
        with nc.Block() as block:
            @block.sync
            def _(sp):
                sp.dma_start(e_list[:, :], k.walk_lists[0:1, :]).then_inc(walk, 16)
                sp.dma_start(n_list[:, :], k.walk_lists[1:2, :]).then_inc(walk, 16)
                sp.dma_start(n128[:, :], k.walk_n128.to_broadcast([P, STEPS])).then_inc(walk, 16)
                sp.wait_ge(walk, 48)
                with sp.Fori(0, STEPS // U) as i:
                    for u in range(U):
                        r = u % RING
                        e = sp.value_load(e_list[0:1, bass.ds(i * U + u, 1)], min_val=0, max_val=EDGE_TILES - 1)
                        sp.wait_ge(summed, i * U + (u + 1))
                        sp.dma_start(slot[:, r, :], tiles(k.tab_sorted)[:, bass.ds(e, 1), :].rearrange("p o d -> p (o d)")
                                     ).then_inc(loaded[r], 16)
                for r in range(RING):
                    sp.wait_ge(loaded[r], 16 * STEPS // RING)

            @block.vector
            def _(dve):
                dve.wait_ge(walk, 48)

                def one_hot(u, n, count):
                    r = u % RING
                    dve.wait_ge(loaded[r], count)
                    nc.vector.tensor_scalar(s_mat[:, u % 2, :], k.iota[:, :], col(n128, n), slot[:, r, 2 * D:2 * D + 1],
                                            ALU.add, ALU.is_equal).then_inc(s_ready, 1)

                nc.vector.memset(k.acc2[:, :], 0.0).then_inc(added, 2)
                for u in range(2):
                    one_hot(u, u, 16)
                with dve.Fori(0, STEPS // U - 1) as i:
                    for u in range(U):
                        n = dve.value_load(n_list[0:1, bass.ds(i * U + (u + 1), 1)], min_val=0, max_val=NODE_TILES)
                        dve.wait_ge(summed, i * U + (RING + u + 1))
                        one_hot(u + 2, i * U + (u + 2), i * per + 16 * ((u + 2) // RING + 1))
                        dve.wait_ge(added, i * U + (u + 2))
                        nc.vector.tensor_tensor(k.acc2[:, bass.ds(n * W, W)], k.acc2[:, bass.ds(n * W, W)],
                                                acc_ps[u % 2][:, :], ALU.add).then_inc(added, 1)
                first = STEPS - U
                for u in range(U):
                    n = dve.value_load(n_list[0:1, first + u + 1:first + u + 2], min_val=0, max_val=NODE_TILES)
                    dve.wait_ge(summed, first + RING + u + 1)
                    if u + 2 < U:
                        one_hot(u + 2, first + u + 2, (STEPS // U - 1) * per + 16 * ((u + 2) // RING + 1))
                    dve.wait_ge(added, first + u + 2)
                    nc.vector.tensor_tensor(k.acc2[:, bass.ds(n * W, W)], k.acc2[:, bass.ds(n * W, W)],
                                            acc_ps[u % 2][:, :], ALU.add).then_inc(added, 1)
                dve.wait_ge(added, STEPS + 2)

            @block.tensor
            def _(pe):
                nc.tensor.transpose(warm[:, 0:P], k.ident[:, :], k.ident[:, :]).then_inc(summed, RING)
                with pe.Fori(0, STEPS // U) as i:
                    for u in range(U):
                        r = u % RING
                        pe.wait_ge(s_ready, i * U + (u + 1))
                        pe.wait_ge(loaded[r], i * per + 16 * (u // RING + 1))
                        pe.wait_ge(added, i * U + (u + 1))
                        nc.tensor.matmul(acc_ps[u % 2][:, :], s_mat[:, u % 2, :], slot[:, r, 0:W], start=True, stop=True).then_inc(summed, 1)


def node_phase_4(nc, k):
    with phase(nc) as (sb, ps, sem):
        xg, hg, fg = sb("n4_x", [P, GROUP, D]), sb("n4_h", [P, GROUP, D]), sb("n4_f", [P, GROUP, D])
        ag = sb("n4_acc", [P, GROUP, 2 * D])
        t = sb("n4_t", [P, GROUP, D])
        w = sb("n4_w", [P, 4, D])
        b, lnw, lnb = sb("n4_b", [P, D]), sb("n4_lnw", [P, D]), sb("n4_lnb", [P, D])
        total, inv = sb("n4_total", [P, NODE_TILES]), sb("n4_inv", [P, NODE_TILES])
        padding = sb("n4_padding", [P, NODE_TILES])
        turned_sb = sb("n4_turned", [P, 2, 2 * D])
        turned_ps, out_ps = ps("n4_turned_ps", [P, 2, 512]), ps("n4_out_ps", [P, 2, 512])
        pa, pb = Project(sem, "n4a"), Project(sem, "n4b")
        nb = norm_buffers(sb, sem, "n4")
        weights, loaded, stored, chain_s, pad_s = sem("n4_weights"), sem("n4_loaded"), sem("n4_stored"), sem("n4_chain"), sem("n4_pad")
        with nc.Block() as block:
            @block.gpsimd
            def _(pool):
                nc.gpsimd.memset(padding[:, :], 1.0).then_inc(pad_s, 1)
                pool.wait_ge(pad_s, 1)
                nc.gpsimd.affine_select(out=padding[:, :], in_=padding[:, :], compare_op=ALU.is_ge, fill=0.0,
                                        base=-NODES, pattern=[[P, NODE_TILES]], channel_multiplier=1).then_inc(pad_s, 1)

            @block.sync
            def _(sp):
                sp.dma_start(w[:, :, :], k.wb.rearrange("(q p) n -> p q n", p=P)).then_inc(weights, 16)
                for dest, src in ((b, k.bb), (lnw, k.ln2_w), (lnb, k.ln2_b)):
                    sp.dma_start(dest[:, :], src.to_broadcast([P, D])).then_inc(weights, 16)
                with sp.Fori(0, GROUPS) as g:
                    sp.wait_ge(stored, g * 16)
                    for dest, src in ((xg, k.tab_x2), (hg, k.tab_h), (fg, k.tab_f)):
                        sp.dma_start(dest[:, :, :], tiles(src)[:, bass.ds(g * GROUP, GROUP), :]).then_inc(loaded, 16)
                    sp.wait_ge(pb.used, g * GROUP + GROUP)
                    sp.dma_start(tiles(k.out)[:, bass.ds(g * GROUP, GROUP), :], xg[:, :, :]).then_inc(stored, 16)
                sp.wait_ge(stored, 16 * GROUPS)

            @block.scalar
            def _(act):
                with act.Fori(0, GROUPS) as g:
                    act.wait_ge(pa.product, g * GROUP)
                    nc.scalar.copy(ag[:, :, :], k.acc2[:, bass.ds(g * (GROUP * 2 * D), GROUP * 2 * D)].rearrange("p (n d) -> p n d", d=2 * D)
                                   ).then_inc(pa.src_ready, 1)
                    act.wait_ge(pb.product, g * GROUP)
                    act_project(nc, act, g, pa, 4, turned_ps, turned_sb)
                    act_root(nc, act, g, 0, 2, nb)
                    act_root(nc, act, g, 1, 2, nb)
                    act_project(nc, act, g, pb, 2, turned_ps, turned_sb)

            @block.vector
            def _(dve):
                link = Chain(dve, chain_s)
                dve.wait_ge(weights, 64)
                dve.wait_ge(pad_s, 2)
                link(nc.vector.tensor_tensor(total[:, :], k.cnt[:, 0, :], k.cnt[:, 1, :], ALU.add))
                link(nc.vector.tensor_tensor(total[:, :], total[:, :], padding[:, :], ALU.add))
                link(nc.vector.reciprocal(inv[:, :], total[:, :]))
                base, per = link.n, 2 * NORM_LINKS + 5 + 2 * GROUP
                with dve.Fori(0, GROUPS) as g:
                    link.loop(g, per, base)
                    dve.wait_ge(loaded, g * 48 + 48)
                    for u in range(GROUP):
                        dve.wait_ge(pa.product, g * GROUP + (u + 1))
                        nc.vector.tensor_tensor(t[:, u, :], out_ps[:, u % 2, 0:D], fg[:, u, :], ALU.add).then_inc(pa.used, 1)
                    dve.wait_ge(pa.used, g * GROUP + GROUP)
                    for u in range(GROUP):
                        link(nc.vector.scalar_tensor_tensor(t[:, u, :], b[:, :], k.cnt[:, 1, bass.ds(g * GROUP + u, 1)], t[:, u, :],
                                                            ALU.mult, ALU.add))
                    for u in range(GROUP):
                        link(nc.vector.tensor_scalar(t[:, u, :], t[:, u, :], col(inv, g * GROUP + u), None, ALU.mult))
                    link(nc.vector.scalar_tensor_tensor(t[:, :, :], t[:, :, :], 0.01, t[:, :, :], ALU.mult, ALU.max))
                    link(nc.vector.tensor_tensor(t[:, :, :], t[:, :, :], hg[:, :, :], ALU.add))
                    dve_norm(nc, dve, link, g, 0, 2, nb, t, hg)
                    link(nc.vector.tensor_tensor(hg[:, :, :], hg[:, :, :], lnw[:, :].unsqueeze(1).to_broadcast([P, GROUP, D]), ALU.mult))
                    link(nc.vector.tensor_tensor(hg[:, :, :], hg[:, :, :], lnb[:, :].unsqueeze(1).to_broadcast([P, GROUP, D]), ALU.add))
                    link(nc.vector.tensor_tensor(xg[:, :, :], xg[:, :, :], hg[:, :, :], ALU.add))
                    dve_norm(nc, dve, link, g, 1, 2, nb, xg, t)
                    nc.vector.tensor_scalar(t[:, :, :], t[:, :, :], 0.0, None, ALU.max).then_inc(pb.src_ready, 1)
                    for u in range(GROUP):
                        dve.wait_ge(pb.product, g * GROUP + (u + 1))
                        nc.vector.tensor_tensor(xg[:, u, :], out_ps[:, u % 2, 0:D], xg[:, u, :], ALU.add).then_inc(pb.used, 1)

            @block.tensor
            def _(pe):
                pe.wait_ge(weights, 64)
                with pe.Fori(0, GROUPS) as g:
                    pe.wait_ge(pb.copied, g * GROUP)
                    pe.wait_ge(pb.used, g * GROUP)
                    pe_project(nc, pe, k, g, pa, ag, 4, turned_ps, turned_sb, [(out_ps, w)])
                    pe.wait_ge(pa.used, g * GROUP + GROUP)
                    pe_project(nc, pe, k, g, pb, t, 2, turned_ps, turned_sb, [(out_ps, k.rot_t)])


def rotation_list(nc, k):
    with phase(nc) as (sb, ps, sem):
        begun, tiny = sem("begunrotation_list"), sb("tinyrotation_list", [P, 1])
        T = EDGE_TILES
        U, N = 17, EDGE_TILES // 17
        H = T // 2
        idx_i = sb("rl_idx_i", [P, 2, T], I32)
        f = sb("rl_f", [P, 2, T])
        fc = sb("rl_fc", [P, 2, T])
        m = sb("rl_m", [P, 2, T])
        w = sb("rl_w", [P, T])
        ang = sb("rl_ang", [P, 2, T])
        turns = sb("rl_turns", [P, T])
        sc = sb("rl_sc", [P, 2, T])
        rec = sb("rl_rec", [P, T, 8])
        active = sb("rl_active", [P, T])
        total, incl, pos, zeros = sb("rl_total", [P, T]), sb("rl_incl", [P, T]), sb("rl_pos", [P, T]), sb("rl_zeros", [P, T])
        nb_f = sb("rl_nb_f", [P, 1])
        nb_i = sb("rl_nb_i", [P, 1], I32)
        zrow = sb("rl_zrow", [P, ROT_LIST // P * 8])
        rslot, islot = sb("rl_rslot", [P, U, 8]), sb("rl_islot", [P, U], I32)
        before_ps, total_ps = ps("rl_before", [P, 2, 512]), ps("rl_total_ps", [P, 2, 512])
        loaded, chain_s, ang_ready, sc_ready = sem("rl_loaded"), sem("rl_chain"), sem("rl_ang_ready"), sem("rl_sc_ready")
        active_ready, before_ready, zrow_ready, cleared = sem("rl_active_ready"), sem("rl_before_ready"), sem("rl_zrow_ready"), sem("rl_cleared")
        rec_ready, slots = sem("rl_rec_ready"), sem("rl_slots")
        scattered = [sem(f"rl_scattered{r}") for r in range(U)]
        with nc.Block() as block:
            @block.sync
            def _(sp):
                sp.dma_start(idx_i[:, 0, :], k.src_cols[:, 0:T]).then_inc(loaded, 16)
                sp.dma_start(idx_i[:, 1, :], k.dst_cols[:, 0:T]).then_inc(loaded, 16)
                sp.dma_start(w[:, :], k.w_cols[:, 0:T]).then_inc(loaded, 16)
                sp.wait_ge(loaded, 48)
                sp.wait_ge(zrow_ready, 1)
                sp.dma_start(k.rot_list.rearrange("(p t) f -> p (t f)", p=P), zrow[:, :]).then_inc(cleared, 16)
                sp.wait_ge(cleared, 16)

            @block.scalar
            def _(act):
                act.wait_ge(ang_ready, 1)
                nc.scalar.activation(sc[:, :, :], ang[:, :, :], ACT.Sin).then_inc(sc_ready, 1)
                act.wait_ge(rec_ready, 1)
                with act.Fori(0, N) as i:
                    for u in range(U):
                        act.wait_ge(scattered[u], i * 16)
                        nc.scalar.copy(rslot[:, u, :], rec[:, bass.ds(i * U + u, 1), :].rearrange("p o f -> p (o f)"))
                        nc.scalar.copy(islot[:, u:u + 1], col(pos, i * U + u)).then_inc(slots, 1)

            @block.gpsimd
            def _(pool):
                nc.gpsimd.memset(zrow[:, :], 0.0).then_inc(zrow_ready, 1)
                nc.gpsimd.memset(tiny[:, :], 0.0).then_inc(begun, 1)
                pool.wait_ge(cleared, 16)
                with pool.Fori(0, N) as i:
                    for u in range(U):
                        pool.wait_ge(slots, i * U + (u + 1))
                        settle(pool, begun)
                        pool.indirect_dma_start(out=k.rot_list, out_offset=bass.IndirectOffsetOnAxis(ap=islot[:, u:u + 1], axis=0),
                                                in_=rslot[:, u, :], in_offset=None,
                                                bounds_check=EDGES_PAD - 1, oob_is_err=False).then_inc(scattered[u], 16)
                for u in range(U):
                    pool.wait_ge(scattered[u], 16 * N)

            @block.vector
            def _(dve):
                link = Chain(dve, chain_s)
                dve.wait_ge(loaded, 48)
                link(nc.vector.tensor_copy(f[:, :, :], idx_i[:, :, :]))
                link(nc.vector.tensor_scalar(m[:, :, :], f[:, :, :], D - 0.5, None, ALU.is_lt))
                nc.vector.tensor_tensor(active[:, :], m[:, 0, :], m[:, 1, :], ALU.max).then_inc(active_ready, 1)
                reduce_angle(nc, link, ang[:, 0, :], turns[:, :], w[:, :], 1.0, 0.0)
                reduce_angle(nc, link, ang[:, 1, :], turns[:, :], w[:, :], 1.0, float(np.pi / 2))
                nc.vector.memset(zeros[:, :], 0.0).then_inc(ang_ready, 1)
                dve.wait_ge(ang_ready, 1)
                link(nc.vector.tensor_tensor(turns[:, :], f[:, 0, :], f[:, 1, :], ALU.not_equal))
                link(nc.vector.tensor_tensor(m[:, 0, :], m[:, 0, :], turns[:, :], ALU.mult))
                link(nc.vector.tensor_scalar(fc[:, :, :], f[:, :, :], D - 1.0, None, ALU.min))
                for x in range(2):
                    link(nc.vector.tensor_copy(rec[:, :, 4 * x], f[:, x, :]))
                    link(nc.vector.tensor_copy(rec[:, :, 4 * x + 1], fc[:, 1 - x, :]))
                dve.wait_ge(sc_ready, 1)
                for x in range(2):
                    link(nc.vector.scalar_tensor_tensor(rec[:, :, 4 * x + 2], sc[:, 1, :], -1.0, m[:, x, :], ALU.add, ALU.mult))
                    link(nc.vector.scalar_tensor_tensor(rec[:, :, 4 * x + 3], sc[:, 0, :], 2.0 * x - 1.0, m[:, x, :], ALU.mult, ALU.mult))
                dve.wait_ge(before_ready, 1)
                link(nc.vector.tensor_copy(total[:, :].rearrange("p (h c) -> p h c", h=2), total_ps[:, :, 0:H]))
                link(nc.vector.tensor_tensor_scan(incl[:, :], total[:, :], zeros[:, :], 0.0, ALU.add, ALU.add))
                link(nc.vector.tensor_tensor(pos[:, :], incl[:, :], total[:, :], ALU.subtract))
                link(nc.vector.tensor_tensor(pos[:, :].rearrange("p (h c) -> p h c", h=2), pos[:, :].rearrange("p (h c) -> p h c", h=2),
                                             before_ps[:, :, 0:H], ALU.add))
                link(nc.vector.scalar_tensor_tensor(pos[:, :], pos[:, :], -float(OUT_OF_BOUNDS), active[:, :], ALU.add, ALU.mult))
                link(nc.vector.tensor_scalar(pos[:, :], pos[:, :], float(OUT_OF_BOUNDS), None, ALU.add))
                link(nc.vector.tensor_scalar(nb_f[:, :], incl[:, T - 1:T], float(BATCH_EDGES - 1), None, ALU.add))
                link(nc.vector.tensor_copy(nb_i[:, :], nb_f[:, :]))
                link(nc.vector.tensor_scalar(nb_i[:, :], nb_i[:, :], BATCH_EDGES.bit_length() - 1, None, ALU.arith_shift_right))
                nc.vector.tensor_scalar(k.batches[:, :], nb_i[:, :], 1, None, ALU.max).then_inc(rec_ready, 1)
                dve.wait_ge(rec_ready, 1)

            @block.tensor
            def _(pe):
                pe.wait_ge(active_ready, 1)
                for h in range(2):
                    nc.tensor.matmul(before_ps[:, h, 0:H], k.upper[:, :], active[:, h * H:(h + 1) * H], start=True, stop=True)
                    last = nc.tensor.matmul(total_ps[:, h, 0:H], k.ones[:, :], active[:, h * H:(h + 1) * H], start=True, stop=True)
                last.then_inc(before_ready, 1)


def rotation_matrix(nc, k):
    with phase(nc) as (sb, ps, sem):
        LEVELS = CH_EDGES.bit_length() - 1
        B = BATCH
        rec = sb("rm_rec", [P, B, 4])
        iota = sb("rm_iota", [P, D])
        masks = sb("rm_masks", [P, LEVELS, P])
        mask0 = sb("rm_mask0", [P, P])
        e, f, f1 = sb("rm_e", [P, B, D]), sb("rm_f", [P, B, D]), sb("rm_f1", [P, B, D])
        eb = sb("rm_eb", [P, B, D])
        turned = sb("rm_turned", [P, B, 4, P])
        ltm = sb("rm_ltm", [P, B, LEVELS, P])
        t, tt, x = sb("rm_t", [P, B, P]), sb("rm_tt", [P, B, P]), sb("rm_x", [P, B, P])
        z, y = sb("rm_z", [P, D]), sb("rm_y", [P, D])
        m = sb("rm_m", [P, 2, D])
        turned_ps = [ps(f"rm_turned_ps{i}", [P, 4, P]) for i in range(2)]
        lt_ps, lx_ps = ps("rm_lt_ps", [P, B, P]), ps("rm_lx_ps", [P, B, P])
        d_ps, dt_ps = ps("rm_d_ps", [P, B, P]), ps("rm_dt_ps", [P, B, P])
        zy_ps, u_ps = ps("rm_zy_ps", [P, 2, D]), ps("rm_u_ps", [P, 2, D])
        loaded, ready, chain_s, rec_loaded = sem("rm_loaded"), sem("rm_ready"), sem("rm_chain"), sem("rm_rec_loaded")
        f_ready, turned_made, turned_copied = sem("rm_f_ready"), sem("rm_turned_made"), sem("rm_turned_copied")
        l_made, t_ready, x_made, x_copied, d_made = sem("rm_l_made"), sem("rm_t_ready"), sem("rm_x_made"), sem("rm_x_copied"), sem("rm_d_made")
        z_made, z_copied, y_made, y_copied, u_made, m_ready = (sem("rm_" + n) for n in (
            "z_made", "z_copied", "y_made", "y_copied", "u_made", "m_ready"))
        m_turned, settled = sem("rm_m_turned"), sem("rm_settled")
        V = B * P
        flat = lambda a: a[:, :, :].rearrange("p b s -> p (b s)")

        def batches(eng):
            return eng.value_load(k.batches[0:1, 0:1], min_val=1, max_val=ROT_LIST // BATCH_EDGES)

        with nc.Block() as block:
            @block.sync
            def _(sp):
                sp.dma_start(masks[:, :, :], k.rot_masks).then_inc(loaded, 16)
                sp.dma_start(mask0[:, :], k.rot_mask0).then_inc(loaded, 16)
                n = batches(sp)
                with sp.Fori(0, n) as i:
                    sp.wait_ge(f_ready, i * B)
                    rows = k.rot_list[bass.ds(i * BATCH_EDGES, BATCH_EDGES), :].rearrange("(c s) f -> s c f", s=CH_EDGES)
                    sp.dma_start(rec[0:CH_EDGES, :, :], rows[:, :, 0:4]).then_inc(rec_loaded, 16)
                    sp.dma_start(rec[CH_EDGES:P, :, :], rows[:, :, 4:8]).then_inc(rec_loaded, 16)
                sp.wait_ge(loaded, 32)
                sp.wait_ge(rec_loaded, n * 32)
                settle(sp, settled)

            @block.gpsimd
            def _(pool):
                nc.gpsimd.iota(iota[:, :], [[1, D]], base=0, channel_multiplier=0, allow_small_or_imprecise_dtypes=True).then_inc(ready, 1)
                nc.gpsimd.memset(m[:, :, :], 0.0).then_inc(ready, 1)
                pool.wait_ge(ready, 2)
                for h in range(2):
                    nc.gpsimd.affine_select(out=m[:, h, :], in_=m[:, h, :], compare_op=ALU.not_equal, fill=1.0,
                                            base=h * P, pattern=[[-1, D]], channel_multiplier=1).then_inc(ready, 1)

            @block.vector
            def _(dve):
                dve.wait_ge(ready, 4)
                dve.wait_ge(loaded, 32)
                link = Chain(dve, chain_s)
                with dve.Fori(0, batches(dve)) as i:
                    link.loop(i, 3 + 2 * B, 0)
                    dve.wait_ge(rec_loaded, i * 32 + 32)
                    for c in range(B):
                        col_ = lambda n: rec[:, c, n:n + 1]
                        nc.vector.tensor_scalar(e[:, c, :], iota[:, :], col_(0), None, ALU.is_equal)
                        link(nc.vector.tensor_scalar(f1[:, c, :], iota[:, :], col_(0), col_(2), ALU.is_equal, ALU.mult))
                        link(nc.vector.tensor_scalar(eb[:, c, :], iota[:, :], col_(1), None, ALU.is_equal))
                        nc.vector.scalar_tensor_tensor(f[:, c, :], eb[:, c, :], col_(3), f1[:, c, :], ALU.mult, ALU.add).then_inc(f_ready, 1)
                    dve.wait_ge(l_made, i + 1)
                    for c in range(B):
                        last = nc.vector.tensor_tensor(ltm[:, c, :, :], lt_ps[:, c, :].unsqueeze(1).to_broadcast([P, LEVELS, P]),
                                                       masks[:, :, :], ALU.mult)
                    link(last)
                    link(nc.vector.tensor_tensor(t[:, :, :], lx_ps[:, :, :], mask0[:, :].unsqueeze(1).to_broadcast([P, B, P]), ALU.mult))
                    link(nc.vector.tensor_tensor(t[:, :, :], t[:, :, :], k.ident[:, :].unsqueeze(1).to_broadcast([P, B, P]), ALU.add))
                    nc.vector.tensor_tensor(tt[:, :, :], ltm[:, :, 0, :], k.ident[:, :].unsqueeze(1).to_broadcast([P, B, P]), ALU.add
                                            ).then_inc(t_ready, 1)
                    for n in range(1, LEVELS):
                        dve.wait_ge(d_made, i * (LEVELS - 1) + n)
                        dve.wait_ge(t_ready, i * LEVELS + n)
                        if n < LEVELS - 1:
                            nc.vector.tensor_tensor(flat(t), flat(t), flat(d_ps), ALU.add)
                        nc.vector.tensor_tensor(flat(tt), flat(tt), flat(dt_ps), ALU.add).then_inc(t_ready, 1)
                    for c in range(B):
                        dve.wait_ge(u_made, i * B + (c + 1))
                        dve.wait_ge(m_ready, i * B + c)
                        nc.vector.tensor_tensor(m[:, :, :], m[:, :, :], u_ps[:, :, :], ALU.add).then_inc(m_ready, 1)
                dve.wait_ge(m_turned, 1)
                for q in range(2):
                    last = nc.vector.tensor_copy(k.rot_t[:, q, :], turned_ps[0][:, 2 * q:2 * q + 2, :].rearrange("p a b -> p (a b)"))
                last.then_inc(m_turned, 1)

            @block.scalar
            def _(act):
                with act.Fori(0, batches(act)) as i:
                    for c in range(B):
                        act.wait_ge(turned_made, i * B + (c + 1))
                        nc.scalar.copy(turned[:, c, :, :], turned_ps[c % 2][:, :, :]).then_inc(turned_copied, 1)
                    for n in range(1, LEVELS):
                        act.wait_ge(x_made, i * (LEVELS - 1) + n)
                        nc.scalar.copy(flat(x), flat(lx_ps)).then_inc(x_copied, 1)
                    for c in range(B):
                        act.wait_ge(z_made, i * B + (c + 1))
                        nc.scalar.copy(z[:, :], zy_ps[:, 0, :]).then_inc(z_copied, 1)
                        act.wait_ge(y_made, i * B + (c + 1))
                        nc.scalar.copy(y[:, :], zy_ps[:, 1, :]).then_inc(y_copied, 1)

            @block.tensor
            def _(pe):
                pe.wait_ge(ready, 4)
                n_batches = batches(pe)
                with pe.Fori(0, n_batches) as i:
                    for c in range(B):
                        pe.wait_ge(f_ready, i * B + (c + 1))
                        pe.wait_ge(turned_copied, i * B + max(c - 1, 0))
                        for h in range(2):
                            nc.tensor.transpose(turned_ps[c % 2][:, h, :], f[:, c, h * P:(h + 1) * P], k.ident[:, :])
                            last = nc.tensor.transpose(turned_ps[c % 2][:, 2 + h, :], e[:, c, h * P:(h + 1) * P], k.ident[:, :])
                        last.then_inc(turned_made, 1)
                    for c in range(B):
                        pe.wait_ge(turned_copied, i * B + (c + 1))
                        for h in range(2):
                            nc.tensor.matmul(lt_ps[:, c, :], turned[:, c, 2 + h, :], turned[:, c, h, :], start=(h == 0), stop=(h == 1))
                        for h in range(2):
                            last = nc.tensor.matmul(lx_ps[:, c, :], turned[:, c, h, :], turned[:, c, 2 + h, :], start=(h == 0), stop=(h == 1))
                    last.then_inc(l_made, 1)
                    for n in range(1, LEVELS):
                        pe.wait_ge(t_ready, i * LEVELS + n)
                        for c in range(B):
                            last = nc.tensor.matmul(lx_ps[:, c, :], ltm[:, c, n, :], t[:, c, :], start=True, stop=True)
                        last.then_inc(x_made, 1)
                        pe.wait_ge(x_copied, i * (LEVELS - 1) + n)
                        for c in range(B):
                            if n < LEVELS - 1:
                                nc.tensor.matmul(d_ps[:, c, :], tt[:, c, :], x[:, c, :], start=True, stop=True)
                            last = nc.tensor.matmul(dt_ps[:, c, :], x[:, c, :], tt[:, c, :], start=True, stop=True)
                        last.then_inc(d_made, 1)
                    pe.wait_ge(t_ready, i * LEVELS + LEVELS)
                    for c in range(B):
                        pe.wait_ge(m_ready, i * B + c)
                        for h in range(2):
                            last = nc.tensor.matmul(zy_ps[:, 0, :], turned[:, c, h, :], m[:, h, :], start=(h == 0), stop=(h == 1))
                        last.then_inc(z_made, 1)
                        pe.wait_ge(z_copied, i * B + (c + 1))
                        nc.tensor.matmul(zy_ps[:, 1, :], tt[:, c, :], z[:, :], start=True, stop=True).then_inc(y_made, 1)
                        pe.wait_ge(y_copied, i * B + (c + 1))
                        for h in range(2):
                            last = nc.tensor.matmul(u_ps[:, h, :], e[:, c, h * P:(h + 1) * P], y[:, :], start=True, stop=True)
                        last.then_inc(u_made, 1)
                pe.wait_ge(m_ready, n_batches * B)
                for q in range(2):
                    for h in range(2):
                        last = nc.tensor.transpose(turned_ps[0][:, 2 * q + h, :], m[:, h, q * P:(q + 1) * P], k.ident[:, :])
                last.then_inc(m_turned, 1)


def build_program(nc, k):
    with ExitStack() as c:
        persistent(nc, c, k)
        constants(nc, k)
        rotation_list(nc, k)
        rotation_matrix(nc, k)
        with nc.sbuf_tensor("place", [P, STEP_COLS], F32) as k.place:
            node_counts_and_sort(nc, k)
            step_lists(nc, k)
        k.acc2 = c.enter_context(nc.sbuf_tensor("sums", [P, (NODE_TILES + 1) * 2 * D], F32))
        k.acc, k.spare = k.acc2[:, 0:(NODE_TILES + 1) * D], k.acc2[:, (NODE_TILES + 1) * D:]
        with nc.sbuf_tensor("node_tab", [P, (NODE_TILES + 1) * D], F32) as k.node_tab:
            node_phase_0(nc, k)
            pass_0(nc, k)
            node_phase_1(nc, k)
            cutoffs(nc, k)
            pass_1(nc, k)
            node_phase_2(nc, k)
            pass_2(nc, k)
        node_phase_3(nc, k)
        pass_3(nc, k)
        node_phase_4(nc, k)


def _rotation_masks():
    edge = np.arange(P) % CH_EDGES
    levels = CH_EDGES.bit_length() - 1
    out = np.zeros((P, levels, P), np.float32)
    for n in range(levels):
        block = edge >> n
        out[:, n, :] = (block[None, :] % 2 == 1) & (block[:, None] == block[None, :] - 1)
    return out


def kernel(x, src, dst, edge_attr_256, edge_attr_64, edge_weight, L0_gnn_W, L1_gnn_ln_g, L1_gnn_ln_b, L1_gnn_Wq,
           L1_gnn_bq, L1_gnn_Wk, L1_gnn_bk, L1_gnn_Wv, L1_gnn_bv, L1_gnn_Wo, L1_gnn_bo, L1_gnn_Wdk, L1_gnn_bdk,
           L1_gnn_Wdv, L1_gnn_bdv, L2_gnn_queries, L2_gnn_influence_weights, L2_gnn_W_fwd, L2_gnn_b_fwd,
           L2_gnn_W_back, L2_gnn_b_back, L2_gnn_ln_w, L2_gnn_ln_b):
    import concourse.bacc as bacc
    from concourse.bass_utils import run_bass_kernel_spmd

    def padded(a, rows, fill):
        a = np.asarray(a)
        out = np.full((rows,) + a.shape[1:], fill, a.dtype)
        out[:len(a)] = a
        return out

    row = lambda a: np.asarray(a).reshape(1, -1)
    t = lambda a: np.asarray(a).T
    rows = lambda a, fill: padded(a, STEP_COLS * P, fill).reshape(STEP_COLS, P)
    ordered = dict(src=rows(src, PAD_NODE), dst=rows(dst, PAD_NODE), w=rows(edge_weight, 0))
    arrays = {n + "_rows": a for n, a in ordered.items()} | {n + "_cols": a.T for n, a in ordered.items()}
    masks = _rotation_masks()
    back = t(L2_gnn_W_back)
    arrays |= dict(
        x=padded(x, NODES_PAD, 0),
        e256=padded(edge_attr_256, EDGES_PAD, 0),
        ea_t=np.concatenate([padded(edge_attr_64, EDGES_PAD, 0).T, np.ones((1, EDGES_PAD), np.float32)], 0),
        w0=L0_gnn_W, ln1_g=L1_gnn_ln_g, ln1_b=L1_gnn_ln_b, bo=row(L1_gnn_bo), wo=t(L1_gnn_Wo),
        wkvq=np.concatenate([t(L1_gnn_Wk), t(L1_gnn_Wv), t(L1_gnn_Wq)], 1),
        bkvq=np.concatenate([row(L1_gnn_bk), row(L1_gnn_bv), row(L1_gnn_bq)], 1),
        wd=np.concatenate([np.concatenate([t(L1_gnn_Wdk), t(L1_gnn_Wdv)], 1),
                           np.concatenate([row(L1_gnn_bdk), row(L1_gnn_bdv)], 1)], 0),
        wf=t(L2_gnn_W_fwd), bf=row(L2_gnn_b_fwd),
        wb=np.concatenate([back[D:], back[:D]], 0), bb=row(L2_gnn_b_back),
        ln2_w=row(L2_gnn_ln_w), ln2_b=row(L2_gnn_ln_b),
        rot_masks=masks, rot_mask0=masks[:, 0, :].T)
    arrays = {n: np.ascontiguousarray(a) for n, a in arrays.items()}

    nc = bacc.Bacc("TRN2", target_bir_lowering=False, num_devices=1)
    k = Kernel()
    for name, a in arrays.items():
        setattr(k, name, nc.dram_tensor("in_" + name, a.shape, mybir.dt.from_np(a.dtype), kind="ExternalInput").ap())
    scratch = dict(tab_y=(NODES_PAD, D), tab_kv=(NODES_PAD, 2 * D), tab_x=(NODES_PAD, D), tab_x2=(NODES_PAD, D),
                   tab_h=(NODES_PAD, D), tab_f=(NODES_PAD, D), tab_sorted=(EDGES_PAD, SORT_ROW),
                   place_rows=(STEP_COLS, P), walk_n128=(1, STEPS), rot_list=(ROT_LIST, 8))
    for name, shape in scratch.items():
        setattr(k, name, nc.dram_tensor(name, shape, F32).ap())
    k.walk_lists = nc.dram_tensor("walk_lists", (2, STEP_COLS), I32).ap()
    k.out = nc.dram_tensor("out", (NODES_PAD, D), F32, kind="ExternalOutput").ap()
    build_program(nc, k)
    result = run_bass_kernel_spmd(nc, [{"in_" + n: a for n, a in arrays.items()}], core_ids=[0])
    return result.results[0]["out"][:NODES]
```

```python
from contextlib import ExitStack, contextmanager

import numpy as np
import concourse.bass as bass
from concourse import mybir

F32, I32, BF16 = mybir.dt.float32, mybir.dt.int32, mybir.dt.bfloat16
ALU = mybir.AluOpType
ACT = mybir.ActivationFunctionType
AX = mybir.AxisListType

P = 128
NODES, EDGES, D, R = 6250, 100000, 256, 64
NODE_TILES = -(-NODES // P)
NODES_PAD = NODE_TILES * P
PAD_NODE = NODES_PAD - 1
EDGE_TILES = -(-EDGES // P)
EDGES_PAD = EDGE_TILES * P
ROW_BLOCKS = 7
STEPS = 832
STEP_COLS = ROW_BLOCKS * P
GROUP = 7
GROUPS = NODE_TILES // GROUP
HALF = STEPS // 2
EPS = 1e-5
BATCH = 4
BATCH_UPDATES = BATCH * (P - 1)
MAX_BATCHES = -(-2 * EDGES_PAD // BATCH_UPDATES)
REC = 9
ROT_PIECE = 49
ROT_ROWS = -(-(MAX_BATCHES * BATCH_UPDATES + 2) // (P * ROT_PIECE)) * P * ROT_PIECE
SCATTER_ROUNDS = 37
SORT_ROW = 516
OUT_OF_BOUNDS = 1 << 20
TWO_PI = 6.283185307179586
TWO_PI_HI = 6.28125
TWO_PI_LO = TWO_PI - TWO_PI_HI
ROUND = 12582912.0
SIN_MAX = 3.1415925
CUTOFF = 5.0


class Chain:

    def __init__(self, eng, sem):
        self.eng, self.sem, self.n = eng, sem, 0

    def __call__(self, ins):
        self.n = self.n + 1
        ins.then_inc(self.sem, 1)
        self.eng.wait_ge(self.sem, self.n)

    def loop(self, i, per, first):
        self.n = i * per + first


def settle(eng, sem):
    eng.sem_inc(sem, 1)


def rounds(eng, n):
    def run(body):
        body(0)
        with eng.Fori(1, n) as i:
            body(i)
    return run


def col(ap, c, n=1):
    return ap[:, bass.ds(c, n)]


@contextmanager
def phase(nc):
    with ExitStack() as c:
        sems = []

        def sem(name):
            sems.append(nc.alloc_semaphore(name))
            return sems[-1]

        yield (lambda n, s, d=F32: c.enter_context(nc.sbuf_tensor(n, s, d)),
               lambda n, s, d=F32: c.enter_context(nc.psum_tensor(n, s, d)), sem)
    nc.clear_and_free_semaphores(sems)
    nc.all_engine_barrier()


def constants(nc, k):
    with phase(nc) as (sb, ps, sem), nc.Block() as block:
        s_z, s_id = sem("const_zero"), sem("const_done")

        @block.gpsimd
        def _(pool):
            nc.gpsimd.memset(k.ident[:, :], 0.0).then_inc(s_z, 1)
            nc.gpsimd.memset(k.ones[:, :], 1.0).then_inc(s_z, 1)
            nc.gpsimd.iota(k.iota[:, :], [[1, P]], base=0, channel_multiplier=0, allow_small_or_imprecise_dtypes=True).then_inc(s_z, 1)
            pool.wait_ge(s_z, 3)
            nc.gpsimd.affine_select(out=k.ident[:, :], in_=k.ident[:, :], compare_op=ALU.not_equal, fill=1.0,
                                    base=0, pattern=[[-1, P]], channel_multiplier=1).then_inc(s_id, 1)
            nc.gpsimd.affine_select(out=k.upper[:, :], in_=k.ones[:, :], compare_op=ALU.is_gt, fill=0.0,
                                    base=0, pattern=[[1, P]], channel_multiplier=-1).then_inc(s_id, 1)
            pool.wait_ge(s_id, 2)


def node_counts_and_sort(nc, k):
    with phase(nc) as (sb, ps, sem):
        TB = 17
        NB = EDGE_TILES // TB
        raw = sb("cs_raw", [P, 2, EDGE_TILES], I32)
        low_i = sb("cs_low_i", [P, 2, EDGE_TILES], I32)
        high_i = sb("cs_high_i", [P, 2, EDGE_TILES], I32)
        low = sb("cs_low", [P, 2, EDGE_TILES], F32)
        high = sb("cs_high", [P, 2, EDGE_TILES], F32)
        ohl = sb("cs_ohl", [P, 2, TB, P], BF16)
        ohh = sb("cs_ohh", [P, 2, TB, NODE_TILES], BF16)
        zb = sb("cs_zb", [P, P], BF16)
        degs = sb("cs_degs", [NODE_TILES, 2, P], F32)
        eq = sb("cs_eq", [P, EDGE_TILES], F32)
        zeros = sb("cs_zeros", [P, EDGE_TILES], F32)
        scan = sb("cs_scan", [P, EDGE_TILES], F32)
        tmp = sb("cs_tmp", [P, EDGE_TILES], F32)
        rank = sb("cs_rank", [P, EDGE_TILES], F32)
        tot = sb("cs_tot", [P, 64], F32)
        end = sb("cs_end", [P, 64], F32)
        off = sb("cs_off", [P, 64], F32)
        deg_ps = ps("cs_deg", [P, 2, P], F32)
        t_ps = ps("cs_t", [P, 2, P], F32)
        o_ps = ps("cs_o", [P, 64], F32)
        tt_ps = ps("cs_tt", [P, 64], F32)
        loaded, chain_s = sem("cs_loaded"), sem("cs_chain")
        ohl_rdy, ohh_rdy, counted, zdone = sem("cs_ohl_rdy"), sem("cs_ohh_rdy"), sem("cs_counted"), sem("cs_zero")
        degs_copied, transposed, split = sem("cs_degcopied"), sem("cs_transposed"), sem("cs_split")
        tot_rdy, off_rdy, highs_rdy = sem("cs_tot_rdy"), sem("cs_off_rdy"), sem("cs_highs")
        records = RecordScatter(sb, sem, "cs_records", 0, SCATTER_ROUNDS)
        with nc.Block() as block:
            @block.scalar
            def _(act):
                act_records(nc, act, k, records)

            @block.gpsimd
            def _(pool):
                pool_records(nc, pool, k, records)
                wait_records(pool, records)

            @block.sync
            def _(sp):
                sp.dma_start(raw[:, 0, :], k.dst_cols[:, 0:EDGE_TILES]).then_inc(loaded, 16)
                sp.dma_start(raw[:, 1, :], k.src_cols[:, 0:EDGE_TILES]).then_inc(loaded, 16)
                sp.wait_ge(loaded, 32)

            @block.vector
            def _(dve):
                link = Chain(dve, chain_s)
                dve.wait_ge(loaded, 32)
                link(nc.vector.tensor_scalar(low_i[:, :, :], raw[:, :, :], 127, None, ALU.bitwise_and))
                link(nc.vector.tensor_scalar(high_i[:, :, :], raw[:, :, :], 7, None, ALU.arith_shift_right))
                nc.vector.memset(zb[:, :], 0.0).then_inc(zdone, 1)
                link(nc.vector.tensor_copy(low[:, :, :], low_i[:, :, :]))
                nc.vector.tensor_copy(high[:, :, :], high_i[:, :, :]).then_inc(highs_rdy, 1)
                dve.wait_ge(highs_rdy, 1)
                for a in range(2):
                    @rounds(dve, NB // 2)
                    def _(i):
                        for u in range(2):
                            dve.wait_ge(counted, i * 2 + (u + a * NB + 1))
                            nc.vector.tensor_tensor(
                                ohl[:, u, :, :],
                                k.iota[:, :].unsqueeze(1).to_broadcast([P, TB, P]),
                                low[:, a, bass.ds((i * 2 + u) * TB, TB)].unsqueeze(2).to_broadcast([P, TB, P]),
                                ALU.is_equal).then_inc(ohl_rdy, 1)
                            nc.vector.tensor_tensor(
                                ohh[:, u, :, :],
                                k.iota[:, 0:NODE_TILES].unsqueeze(1).to_broadcast([P, TB, NODE_TILES]),
                                high[:, a, bass.ds((i * 2 + u) * TB, TB)].unsqueeze(2).to_broadcast([P, TB, NODE_TILES]),
                                ALU.is_equal).then_inc(ohh_rdy, 1)
                dve.wait_ge(counted, 2 * NB + 2)
                nc.vector.tensor_copy(degs[:, :, :], deg_ps[0:NODE_TILES, :, :]).then_inc(degs_copied, 1)
                dve.wait_ge(transposed, 2)
                nc.vector.tensor_copy(k.cnt[:, :, :], t_ps[:, :, 0:NODE_TILES]).then_inc(split, 1)
                dve.wait_ge(highs_rdy, 1)
                link(nc.vector.memset(zeros[:, :], 0.0))
                link(nc.vector.memset(rank[:, :], 0.0))
                link(nc.vector.memset(k.place[:, EDGE_TILES:STEP_COLS], 0.0))
                base = link.n
                @rounds(dve, NODE_TILES)
                def _(h):
                    link.loop(h, 5, base)
                    hcol = col(k.iota, h)
                    link(nc.vector.tensor_scalar(eq[:, :], high[:, 1, :], hcol, None, ALU.is_equal))
                    link(nc.vector.tensor_tensor_scan(scan[:, :], eq[:, :], zeros[:, :], 0.0, ALU.add, ALU.add))
                    link(nc.vector.tensor_tensor(tmp[:, :], eq[:, :], scan[:, :], ALU.mult))
                    link(nc.vector.tensor_copy(col(tot, h), scan[:, EDGE_TILES - 1:EDGE_TILES]))
                    link(nc.vector.tensor_tensor(rank[:, :], rank[:, :], tmp[:, :], ALU.add))
                link.n = base + 5 * NODE_TILES
                nc.vector.tensor_scalar(tmp[:, 0:1], tot[:, 0:1], 0.0, None, ALU.mult).then_inc(tot_rdy, 1)
                dve.wait_ge(off_rdy, 1)
                link(nc.vector.tensor_tensor_scan(end[:, 0:NODE_TILES], tt_ps[:, 0:NODE_TILES], zeros[:, 0:NODE_TILES],
                                                  0.0, ALU.add, ALU.add))
                link(nc.vector.tensor_copy(k.bucket_end[:, :], end[:, 0:NODE_TILES]))
                link(nc.vector.tensor_tensor(off[:, 0:NODE_TILES], end[:, 0:NODE_TILES], tt_ps[:, 0:NODE_TILES], ALU.subtract))
                link(nc.vector.tensor_tensor(off[:, 0:NODE_TILES], off[:, 0:NODE_TILES], o_ps[:, 0:NODE_TILES], ALU.add))
                link(nc.vector.tensor_scalar(off[:, 0:NODE_TILES], off[:, 0:NODE_TILES], -1.0, None, ALU.add))
                base = link.n
                @rounds(dve, NODE_TILES)
                def _(h):
                    link.loop(h, 2, base)
                    link(nc.vector.tensor_scalar(eq[:, :], high[:, 1, :], col(k.iota, h), col(off, h), ALU.is_equal, ALU.mult))
                    link(nc.vector.tensor_tensor(rank[:, :], rank[:, :], eq[:, :], ALU.add))
                link.n = base + 2 * NODE_TILES
                link(nc.vector.tensor_copy(k.place[:, 0:EDGE_TILES], rank[:, :]))

            @block.tensor
            def _(pe):
                pe.wait_ge(zdone, 1)
                nc.tensor.matmul(deg_ps[0:NODE_TILES, :, :], zb[:, 0:NODE_TILES],
                                 zb[:, :].unsqueeze(1).to_broadcast([P, 2, P]), start=True, stop=True).then_inc(counted, 2)
                for a in range(2):
                    @rounds(pe, NB // 2)
                    def _(i):
                        for u in range(2):
                            pe.wait_ge(ohl_rdy, i * 2 + (u + a * NB + 1))
                            pe.wait_ge(ohh_rdy, i * 2 + (u + a * NB + 1))
                            for t in range(TB):
                                last = nc.tensor.matmul(deg_ps[0:NODE_TILES, a, :], ohh[:, u, t, :], ohl[:, u, t, :],
                                                        start=False, stop=True, skip_group_check=True)
                            last.then_inc(counted, 1)
                pe.wait_ge(degs_copied, 1)
                for a in range(2):
                    nc.tensor.transpose(t_ps[:, a, 0:NODE_TILES], degs[:, a, :], k.ident[0:NODE_TILES, 0:NODE_TILES]).then_inc(transposed, 1)
                pe.wait_ge(tot_rdy, 1)
                nc.tensor.matmul(o_ps[:, 0:NODE_TILES], k.upper[:, :], tot[:, 0:NODE_TILES], start=True, stop=True)
                nc.tensor.matmul(tt_ps[:, 0:NODE_TILES], k.ones[:, :], tot[:, 0:NODE_TILES], start=True, stop=True).then_inc(off_rdy, 1)


def step_lists(nc, k):
    with phase(nc) as (sb, ps, sem):
        B = ROW_BLOCKS
        ends_i = sb("sl_ends_i", [P, 3, B], I32)
        lo = sb("sl_lo", [P, 2, B], F32)
        hi = sb("sl_hi", [P, 2, B], F32)
        prev = sb("sl_prev", [P, 2, B], F32)
        cnt = sb("sl_cnt", [P, 2, B], F32)
        start = sb("sl_start", [P, 2, B], F32)
        tot = sb("sl_tot", [P, 2, B], F32)
        inc = sb("sl_inc", [P, 2, B], F32)
        zero = sb("sl_zero", [P, B], F32)
        wgt = sb("sl_wgt", [P, 2, B, 2], F32)
        pos = sb("sl_pos", [P, 3, B], F32)
        cmp49 = sb("sl_cmp49", [P, NODE_TILES], F32)
        kk = sb("sl_kk", [P, STEP_COLS], F32)
        valid = sb("sl_valid", [P, B], F32)
        tidx = sb("sl_tidx", [P, B], F32)
        cmp = sb("sl_cmp", [P, 2, B, STEPS], F32)
        row = sb("sl_row", [1, 2, 2, STEPS], F32)
        krow = sb("sl_krow", [1, STEPS], F32)
        kcol = sb("sl_kcol", [P, B], F32)
        colv = sb("sl_colv", [P, B, 2], F32)
        e_idx = sb("sl_e_idx", [P, B], I32)
        n128 = sb("sl_n128", [P, B], F32)
        n_row = sb("sl_n_row", [1, STEPS], F32)
        e_list2, n_list2 = sb("sl_e_list2", [1, STEP_COLS], I32), sb("sl_n_list2", [1, STEP_COLS], I32)
        rows_i = sb("sl_rows_i", [P, 2, B, P], I32)
        rows_w = sb("sl_rows_w", [P, B, P], F32)
        rows_f = sb("sl_rows_f", [P, 2, B, P], F32)
        m_ps = ps("sl_m", [P, 2, 2, B], F32)
        r_ps = ps("sl_r", [1, 2, 512], F32)
        c_ps = ps("sl_c", [P, B, 2], F32)
        x_ps = ps("sl_x", [P, 2, 512], F32)
        place_t = sb("sl_place_t", [P, B, P], F32)
        rows_p = sb("sl_rows_p", [P, B, P], F32)
        inside = sb("sl_inside", [P, B, P], F32)
        pt_rdy, pt_free, place_out = sem("sl_pt_rdy"), sem("sl_pt_free"), sem("sl_place_out")
        loaded, chain_s, iota_s, memset_s = sem("sl_loaded"), sem("sl_chain"), sem("sl_iota"), sem("sl_memset")
        cnt_rdy, summed, cmp_rdy, row_ps_rdy, row_free = sem("sl_cnt_rdy"), sem("sl_summed"), sem("sl_cmp_rdy"), sem("sl_row_ps"), sem("sl_row_free")
        col_rdy, n_rdy, walk_out, idx_rdy = sem("sl_col_rdy"), sem("sl_n_rdy"), sem("sl_walk_out"), sem("sl_idx")
        gath, rows_rdy, x_rdy, x_free = sem("sl_gath"), sem("sl_rows_rdy"), sem("sl_x_rdy"), sem("sl_x_free")
        records = RecordScatter(sb, sem, "sl_records", SCATTER_ROUNDS, EDGE_TILES // SCATTER_UNROLL)
        with nc.Block() as block:
            @block.scalar
            def _(act):
                act_records(nc, act, k, records)

            @block.sync
            def _(sp):
                flat = k.dst_rows.rearrange("a e -> (a e)")
                last = k.dst_rows.rearrange("(b p) e -> p b e", p=P)
                with nc.allow_non_contiguous_dma(reason="the ends of edge tiles"):
                    sp.dma_start(ends_i[:, 0, :].unsqueeze(2), last[:, :, 0:1]).then_inc(loaded, 16)
                    sp.dma_start(ends_i[:, 1, :].unsqueeze(2), last[:, :, P - 1:P]).then_inc(loaded, 16)
                    sp.wait_ge(memset_s, 1)
                    sp.dma_start(ends_i[1:P, 2, 0:1], k.dst_rows[0:P - 1, P - 1:P]).then_inc(loaded, 16)
                    for b in range(1, B):
                        sp.dma_start(ends_i[:, 2, b:b + 1], k.dst_rows[b * P - 1:b * P + P - 1, P - 1:P]).then_inc(loaded, 16)
                sp.wait_ge(loaded, 16 * (B + 2))
                sp.wait_ge(pt_free, B)
                sp.dma_start(k.place_rows.rearrange("(b p) e -> p b e", p=P), place_t[:, :, :]).then_inc(place_out, 16)
                sp.wait_ge(n_rdy, 1)
                sp.dma_start(k.walk_lists[0:1, :], e_list2[:, :]).then_inc(walk_out, 16)
                sp.dma_start(k.walk_lists[1:2, :], n_list2[:, :]).then_inc(walk_out, 16)
                sp.dma_start(k.walk_n128, n_row[:, :]).then_inc(walk_out, 16)
                sp.wait_ge(walk_out, 48)
                sp.wait_ge(place_out, 16)

            @block.gpsimd
            def _(pool):
                kw = dict(allow_small_or_imprecise_dtypes=True)
                nc.gpsimd.memset(ends_i[:, 2, :], -P).then_inc(memset_s, 1)
                nc.gpsimd.iota(kk[:, :], [[1, STEP_COLS]], base=0, channel_multiplier=0, **kw).then_inc(iota_s, 1)
                nc.gpsimd.iota(krow[:, :], [[1, STEPS]], base=0, channel_multiplier=0, **kw).then_inc(iota_s, 1)
                nc.gpsimd.iota(kcol[:, :], [[P, B]], base=0, channel_multiplier=1, **kw).then_inc(iota_s, 1)
                for n, b0 in enumerate((0, P - 1, -1)):
                    nc.gpsimd.iota(pos[:, n, :], [[P * P, B]], base=b0, channel_multiplier=P, **kw).then_inc(iota_s, 1)
                nc.gpsimd.iota(tidx[:, :], [[P, B]], base=0, channel_multiplier=1, **kw).then_inc(iota_s, 1)
                pool_records(nc, pool, k, records)
                pool.wait_ge(idx_rdy, 1)
                pool.wait_ge(place_out, 16)
                for b in range(B):
                    pool.indirect_dma_start(out=rows_p[:, b, :], out_offset=None, in_=k.place_rows,
                                            in_offset=bass.IndirectOffsetOnAxis(ap=e_idx[:, b:b + 1], axis=0)).then_inc(gath, 16)
                    for n, rows in ((0, k.src_rows), (1, k.dst_rows)):
                        pool.indirect_dma_start(out=rows_i[:, n, b, :], out_offset=None, in_=rows,
                                                in_offset=bass.IndirectOffsetOnAxis(ap=e_idx[:, b:b + 1], axis=0)).then_inc(gath, 16)
                    pool.indirect_dma_start(out=rows_w[:, b, :], out_offset=None, in_=k.w_rows,
                                            in_offset=bass.IndirectOffsetOnAxis(ap=e_idx[:, b:b + 1], axis=0)).then_inc(gath, 16)
                pool.wait_ge(gath, 16 * 4 * B)
                wait_records(pool, records)

            @block.vector
            def _(dve):
                link = Chain(dve, chain_s)
                for b in range(B):
                    dve.wait_ge(pt_rdy, b + 1)
                    nc.vector.tensor_copy(place_t[:, b, :], x_ps[:, b % 2, 0:P]).then_inc(pt_free, 1)
                dve.wait_ge(loaded, 16 * (B + 2))
                dve.wait_ge(iota_s, 7)
                link(nc.vector.memset(zero[:, :], 0.0))
                link(nc.vector.tensor_scalar(ends_i[:, :, :], ends_i[:, :, :], 7, None, ALU.arith_shift_right))
                link(nc.vector.tensor_copy(lo[:, 0, :], ends_i[:, 0, :]))
                link(nc.vector.tensor_copy(hi[:, 0, :], ends_i[:, 1, :]))
                link(nc.vector.tensor_copy(prev[:, 0, :], ends_i[:, 2, :]))
                for n, out in enumerate((lo, hi, prev)):
                    for b in range(B):
                        link(nc.vector.tensor_scalar(cmp49[:, :], k.bucket_end[:, :], pos[:, n, b:b + 1], None, ALU.is_le))
                        link(nc.vector.tensor_reduce(out[:, 1, b:b + 1], cmp49[:, :], AX.X, ALU.add))
                link(nc.vector.memset(prev[0:1, 1, 0:1], -1.0))
                link(nc.vector.tensor_scalar(valid[:, :], tidx[:, :], float(EDGE_TILES) - 0.5, None, ALU.is_lt))
                link(nc.vector.tensor_tensor(cnt[:, :, :], hi[:, :, :], lo[:, :, :], ALU.subtract))
                nc.vector.tensor_scalar(cnt[:, :, :], cnt[:, :, :], 1.0, None, ALU.add).then_inc(cnt_rdy, 1)
                dve.wait_ge(summed, 1)
                for w in range(2):
                    link(nc.vector.tensor_tensor_scan(inc[:, w, :], m_ps[:, 1, w, :], zero[:, :], 0.0, ALU.add, ALU.add))
                link(nc.vector.tensor_tensor(tot[:, :, :], inc[:, :, :], m_ps[:, 1, :, :], ALU.subtract))
                link(nc.vector.tensor_tensor(start[:, :, :], tot[:, :, :], m_ps[:, 0, :, :], ALU.add))
                for w in range(2):
                    link(nc.vector.tensor_tensor(inc[:, w, :], lo[:, w, :], prev[:, w, :], ALU.subtract))
                    link(nc.vector.tensor_scalar(inc[:, w, :], inc[:, w, :], -1.0, None, ALU.add))
                    link(nc.vector.tensor_tensor(wgt[:, w, :, 1], inc[:, w, :], valid[:, :], ALU.mult))
                    link(nc.vector.tensor_copy(wgt[:, w, :, 0], valid[:, :]))
                    for b in range(B):
                        link(nc.vector.tensor_scalar(cmp[:, w, b, :], kk[:, 0:STEPS], start[:, w, b:b + 1], None, ALU.is_ge))
                    nc.vector.tensor_scalar(cmp49[:, 0:1], kk[:, 0:1], 0.0, None, ALU.mult).then_inc(cmp_rdy, 1)
                    dve.wait_ge(cmp_rdy, w + 1)
                for w in range(2):
                    for f in range(2):
                        dve.wait_ge(row_ps_rdy, 2 * w + f + 1)
                        nc.vector.tensor_copy(row[0:1, w, f, :].rearrange("p (h c) -> p h c", h=2),
                                              r_ps[0:1, :, 0:HALF]).then_inc(row_free, 1)
                        dve.wait_ge(row_free, 2 * w + f + 1)
                    link(nc.vector.tensor_scalar(row[0:1, w, 0, :], row[0:1, w, 0, :], -1.0, None, ALU.add))
                    link(nc.vector.tensor_tensor(row[0:1, w, 1, :], row[0:1, w, 1, :], krow[0:1, :], ALU.add))
                    link(nc.vector.tensor_scalar(row[0:1, w, 1, :], row[0:1, w, 1, :], float(NODE_TILES), None, ALU.min))
                    e_list, n_list = (k.e_list, k.n_list) if w == 0 else (e_list2, n_list2)
                    link(nc.vector.tensor_copy(e_list[0:1, 0:STEPS], row[0:1, w, 0, :]))
                    link(nc.vector.memset(n_list[0:1, 0:1], NODE_TILES))
                    link(nc.vector.tensor_copy(n_list[0:1, 1:STEPS + 1], row[0:1, w, 1, :]))
                    link(nc.vector.memset(n_list[0:1, STEPS + 1:STEP_COLS], NODE_TILES))
                    link(nc.vector.memset(e_list[0:1, STEPS:STEP_COLS], EDGE_TILES - 1))
                nc.vector.tensor_scalar(n_row[0:1, :], row[0:1, 1, 1, :], float(P), None, ALU.mult).then_inc(n_rdy, 1)
                dve.wait_ge(col_rdy, 1)
                link(nc.vector.memset(colv[:, :, :], 0.0))
                link(nc.vector.memset(colv[:, B - 1, 0:1], float(EDGE_TILES)))
                link(nc.vector.tensor_copy(colv[:, 0:B - 1, :], c_ps[:, 0:B - 1, :]))
                link(nc.vector.tensor_copy(colv[0:STEPS - (B - 1) * P, B - 1, :], c_ps[0:STEPS - (B - 1) * P, B - 1, :]))
                link(nc.vector.tensor_scalar(colv[:, :, 0], colv[:, :, 0], -1.0, None, ALU.add))
                link(nc.vector.tensor_tensor(n128[:, :], colv[:, :, 1], kcol[:, :], ALU.add))
                link(nc.vector.tensor_scalar(n128[:, :], n128[:, :], float(P), None, ALU.mult))
                nc.vector.tensor_copy(e_idx[:, :], colv[:, :, 0]).then_inc(idx_rdy, 1)
                dve.wait_ge(gath, 16 * 4 * B)
                link(nc.vector.tensor_copy(rows_f[:, :, :, :], rows_i[:, :, :, :]))
                for b in range(B):
                    link(nc.vector.tensor_scalar(rows_f[:, 1, b, :], rows_f[:, 1, b, :], n128[:, b:b + 1], None, ALU.subtract))
                link(nc.vector.tensor_scalar(inside[:, :, :], rows_f[:, 1, :, :], 0.0, None, ALU.is_ge))
                link(nc.vector.scalar_tensor_tensor(inside[:, :, :], rows_f[:, 1, :, :], P - 0.5, inside[:, :, :], ALU.is_lt, ALU.mult))
                link(nc.vector.scalar_tensor_tensor(rows_p[:, :, :], rows_p[:, :, :], -float(OUT_OF_BOUNDS), inside[:, :, :], ALU.add, ALU.mult))
                nc.vector.tensor_scalar(rows_p[:, :, :], rows_p[:, :, :], float(OUT_OF_BOUNDS), None, ALU.add).then_inc(rows_rdy, 1)
                m = 0
                for b in range(B):
                    for dest in (k.step_src, k.step_rel, k.step_w, k.step_place):
                        m += 1
                        dve.wait_ge(x_rdy, m)
                        nc.vector.tensor_copy(dest[:, b * P:(b + 1) * P], x_ps[:, m % 2, 0:P]).then_inc(x_free, 1)
                dve.wait_ge(x_free, m)

            @block.tensor
            def _(pe):
                for b in range(B):
                    if b >= 2:
                        pe.wait_ge(pt_free, b - 1)
                    nc.tensor.transpose(x_ps[:, b % 2, 0:P], k.place[:, b * P:(b + 1) * P], k.ident[:, :]).then_inc(pt_rdy, 1)
                pe.wait_ge(cnt_rdy, 1)
                nc.tensor.matmul(m_ps[:, 0, :, :], k.upper[:, :], cnt[:, :, :], start=True, stop=True)
                nc.tensor.matmul(m_ps[:, 1, :, :], k.ones[:, :], cnt[:, :, :], start=True, stop=True).then_inc(summed, 1)
                for w in range(2):
                    pe.wait_ge(cmp_rdy, w + 1)
                    for f in range(2):
                        if w or f:
                            pe.wait_ge(row_free, 2 * w + f)
                        for h in range(2):
                            for b in range(B):
                                last = nc.tensor.matmul(r_ps[0:1, h, 0:HALF], wgt[:, w, b, f:f + 1],
                                                        cmp[:, w, b, h * HALF:(h + 1) * HALF], start=(b == 0), stop=(b == B - 1))
                        last.then_inc(row_ps_rdy, 1)
                for q in range(B):
                    m = min(P, STEPS - q * P)
                    for b in range(B):
                        last = nc.tensor.matmul(c_ps[0:m, q, :], cmp[:, 0, b, q * P:q * P + m], wgt[:, 0, b, :],
                                                start=(b == 0), stop=(b == B - 1))
                last.then_inc(col_rdy, 1)
                pe.wait_ge(rows_rdy, 1)
                m = 0
                for b in range(B):
                    for src in (rows_f[:, 0, b, :], rows_f[:, 1, b, :], rows_w[:, b, :], rows_p[:, b, :]):
                        m += 1
                        if m > 2:
                            pe.wait_ge(x_free, m - 2)
                        else:
                            pe.wait_ge(pt_free, B)
                        nc.tensor.transpose(x_ps[:, m % 2, 0:P], src, k.ident[:, :]).then_inc(x_rdy, 1)


class Kernel:
    pass


def persistent(nc, c, k):
    sb = lambda n, s, d: c.enter_context(nc.sbuf_tensor(n, s, d))
    k.ident = sb("ident", [P, P], F32)
    k.iota = sb("iota", [P, P], F32)
    k.ones = sb("ones", [P, P], F32)
    k.upper = sb("upper", [P, P], F32)
    k.cnt = sb("cnt", [P, 2, NODE_TILES], F32)
    k.bucket_end = sb("bucket_end", [P, NODE_TILES], F32)
    k.e_list = sb("e_list", [1, STEP_COLS], I32)
    k.n_list = sb("n_list", [1, STEP_COLS], I32)
    k.step_src = sb("step_src", [P, STEP_COLS], I32)
    k.step_rel = sb("step_rel", [P, STEP_COLS], F32)
    k.step_w = sb("step_w", [P, STEP_COLS], F32)
    k.step_place = sb("step_place", [P, STEP_COLS], I32)
    k.batches = sb("batches", [P, 1], I32)
    k.dinv = sb("dinv", [P, NODE_TILES], F32)
    k.rot_t = sb("rot_t", [P, 2, D], F32)


class Project:

    def __init__(self, sem, name):
        self.src_ready = sem(name + "_src_ready")
        self.turned = sem(name + "_turned")
        self.copied = sem(name + "_copied")
        self.product = sem(name + "_product")
        self.used = sem(name + "_used")


def pe_project(nc, pe, k, g, s, src, parts, turned_ps, turned_sb, outs):
    def turn(u):
        if u == 0:
            pe.wait_ge(s.src_ready, g + 1)
        pe.wait_ge(s.copied, g * GROUP + max(u - 1, 0))
        for q in range(parts):
            last = nc.tensor.transpose(turned_ps[:, u % 2, q * P:(q + 1) * P], src[:, u, q * P:(q + 1) * P], k.ident[:, :])
        last.then_inc(s.turned, 1)

    def multiply(u):
        pe.wait_ge(s.copied, g * GROUP + (u + 1))
        pe.wait_ge(s.used, g * GROUP + max(u - 1, 0))
        for out, w in outs:
            width = w.shape[-1]
            for q in range(parts):
                last = nc.tensor.matmul(out[:, u % 2, 0:width], turned_sb[:, u % 2, q * P:(q + 1) * P], w[:, q, :],
                                        start=(q == 0), stop=(q == parts - 1))
        last.then_inc(s.product, 1)

    turn(0)
    for u in range(GROUP):
        if u + 1 < GROUP:
            turn(u + 1)
        multiply(u)


def act_project(nc, act, g, s, parts, turned_ps, turned_sb, scale=None, bias=None):
    for u in range(GROUP):
        act.wait_ge(s.turned, g * GROUP + (u + 1))
        act.wait_ge(s.product, g * GROUP + max(u - 1, 0))
        if scale is None:
            nc.scalar.copy(turned_sb[:, u % 2, 0:parts * P], turned_ps[:, u % 2, 0:parts * P]).then_inc(s.copied, 1)
        else:
            for q in range(parts):
                last = nc.scalar.activation(turned_sb[:, u % 2, q * P:(q + 1) * P], turned_ps[:, u % 2, q * P:(q + 1) * P],
                                            ACT.Identity, scale=scale[:, q:q + 1], bias=bias[:, q:q + 1])
            last.then_inc(s.copied, 1)


def dve_norm(nc, dve, link, g, n, per_group, sb, x, out):
    for u in range(GROUP):
        link(nc.vector.bn_stats(sb.stats[:, u, :], x[:, u, :]))
    settle(dve, sb.settled)
    for u in range(GROUP):
        nc.vector.bn_aggr(sb.mv[:, u, :], sb.stats[:, u, :]).then_inc(sb.aggregated, 1)
    dve.wait_ge(sb.aggregated, (g * per_group + (n + 1)) * GROUP)
    nc.vector.tensor_scalar(sb.var[:, :], sb.mv[:, :, 1], EPS, None, ALU.add).then_inc(sb.var_ready, 1)
    dve.wait_ge(sb.root_ready, g * per_group + (n + 1))
    link(nc.vector.reciprocal(sb.rstd[:, :], sb.root[:, :]))
    for u in range(GROUP):
        link(nc.vector.tensor_scalar(out[:, u, :], x[:, u, :], sb.mv[:, u, 0:1], sb.rstd[:, u:u + 1], ALU.subtract, ALU.mult))


NORM_LINKS = 2 * GROUP + 1


def act_root(nc, act, g, n, per_group, sb):
    act.wait_ge(sb.var_ready, g * per_group + (n + 1))
    nc.scalar.activation(sb.root[:, :], sb.var[:, :], ACT.Sqrt).then_inc(sb.root_ready, 1)


def norm_buffers(sb, sem, name):
    b = Kernel()
    b.stats = sb(name + "_stats", [P, GROUP, 6], F32)
    b.mv = sb(name + "_mv", [P, GROUP, 2], F32)
    b.var = sb(name + "_var", [P, GROUP], F32)
    b.root = sb(name + "_root", [P, GROUP], F32)
    b.rstd = sb(name + "_rstd", [P, GROUP], F32)
    b.aggregated, b.settled = sem(name + "_aggregated"), sem(name + "_settled")
    b.var_ready, b.root_ready = sem(name + "_var_ready"), sem(name + "_root_ready")
    return b


def tiles(ap):
    return ap.rearrange("(n p) d -> p n d", p=P)


def node_phase_0(nc, k):
    with phase(nc) as (sb, ps, sem):
        xg, yg = sb("n0_x", [P, GROUP, D]), sb("n0_y", [P, GROUP, D])
        h = sb("n0_h", [P, GROUP, D])
        root49, mask49 = sb("n0_droot", [P, NODE_TILES]), sb("n0_mask", [P, NODE_TILES])
        nb = norm_buffers(sb, sem, "n0")
        loaded, consumed, made, stored = sem("n0_loaded"), sem("n0_consumed"), sem("n0_made"), sem("n0_stored")
        chain_s, deg_ready, deg_root = sem("n0_chain"), sem("n0_deg_ready"), sem("n0_deg_root")
        with nc.Block() as block:
            @block.sync
            def _(sp):
                @rounds(sp, GROUPS)
                def _(g):
                    sp.wait_ge(consumed, g)
                    sp.dma_start(xg[:, :, :], tiles(k.x)[:, bass.ds(g * GROUP, GROUP), :]).then_inc(loaded, 16)
                    sp.wait_ge(made, g + 1)
                    sp.dma_start(tiles(k.tab_y)[:, bass.ds(g * GROUP, GROUP), :], yg[:, :, :]).then_inc(stored, 16)
                sp.wait_ge(stored, 16 * GROUPS)

            @block.scalar
            def _(act):
                act.wait_ge(deg_ready, 1)
                nc.scalar.activation(root49[:, :], k.dinv[:, :], ACT.Sqrt).then_inc(deg_root, 1)
                @rounds(act, GROUPS)
                def _(g):
                    act_root(nc, act, g, 0, 1, nb)

            @block.vector
            def _(dve):
                link = Chain(dve, chain_s)
                link(nc.vector.tensor_scalar(mask49[:, :], k.cnt[:, 0, :], 0.0, None, ALU.is_gt))
                nc.vector.tensor_scalar(k.dinv[:, :], k.cnt[:, 0, :], 1.0, None, ALU.max).then_inc(deg_ready, 1)
                dve.wait_ge(deg_root, 1)
                link(nc.vector.reciprocal(k.dinv[:, :], root49[:, :]))
                link(nc.vector.tensor_tensor(k.dinv[:, :], k.dinv[:, :], mask49[:, :], ALU.mult))
                base, per = link.n, NORM_LINKS
                @rounds(dve, GROUPS)
                def _(g):
                    link.loop(g, per, base)
                    dve.wait_ge(loaded, g * 16 + 16)
                    dve_norm(nc, dve, link, g, 0, 1, nb, xg, h)
                    dve.wait_ge(stored, g * 16)
                    for u in range(GROUP):
                        last = nc.vector.tensor_scalar(yg[:, u, :], h[:, u, :], 0.0, col(k.dinv, g * GROUP + u), ALU.max, ALU.mult)
                    last.then_inc(made, 1)
                    nc.vector.tensor_scalar(nb.var[:, 0:1], nb.rstd[:, 0:1], 0.0, None, ALU.mult).then_inc(consumed, 1)


def pass_0(nc, k):
    with phase(nc) as (sb, ps, sem):
        begun, tiny = sem("begunpass_0"), sb("tinypass_0", [P, 1])
        U, RING = 16, 8
        rows = sb("p0_rows", [P, RING, D])
        idx = sb("p0_idx", [P, U], I32)
        s_mat = sb("p0_s", [P, 2, P])
        acc_ps = [ps(f"p0_acc{i}", [P, 512]) for i in range(2)]
        warm = ps("p0_warm", [P, 512])
        gathered = [sem(f"p0_gathered{r}") for r in range(RING)]
        idx_ready, s_ready, summed, added = sem("p0_idx_ready"), sem("p0_s_ready"), sem("p0_summed"), sem("p0_added")
        with nc.Block() as block:
            @block.gpsimd
            def _(pool):
                nc.gpsimd.memset(tiny[:, :], 0.0).then_inc(begun, 1)
                @rounds(pool, STEPS // U)
                def _(i):
                    for u in range(U):
                        if u % RING == 0:
                            pool.wait_ge(summed, i * U + u)
                            settle(pool, begun)
                            nc.gpsimd.tensor_copy(idx[:, u:u + RING], col(k.step_src, i * U + u, RING)).then_inc(idx_ready, 1)
                            pool.wait_ge(idx_ready, i * 2 + (u // RING + 1))
                        pool.wait_ge(summed, i * U + (u + 1))
                        settle(pool, begun)
                        pool.indirect_dma_start(out=rows[:, u % RING, :], out_offset=None, in_=k.tab_y,
                                                in_offset=bass.IndirectOffsetOnAxis(ap=idx[:, u:u + 1], axis=0)
                                                ).then_inc(gathered[u % RING], 16)

            @block.vector
            def _(dve):
                nc.vector.memset(k.acc[:, :], 0.0).then_inc(added, 2)
                for u in range(2):
                    nc.vector.tensor_scalar(s_mat[:, u, :], k.iota[:, :], k.step_rel[:, u:u + 1], None, ALU.is_equal).then_inc(s_ready, 1)
                @rounds(dve, STEPS // U)
                def _(i):
                    for u in range(U):
                        n = dve.value_load(k.n_list[0:1, bass.ds(i * U + (u + 1), 1)], min_val=0, max_val=NODE_TILES)
                        dve.wait_ge(summed, i * U + (RING + u + 1))
                        nc.vector.tensor_scalar(s_mat[:, u % 2, :], k.iota[:, :], col(k.step_rel, i * U + (u + 2)), None,
                                                ALU.is_equal).then_inc(s_ready, 1)
                        dve.wait_ge(added, i * U + (u + 2))
                        nc.vector.tensor_tensor(k.acc[:, bass.ds(n * D, D)], k.acc[:, bass.ds(n * D, D)],
                                                acc_ps[u % 2][:, 0:D], ALU.add).then_inc(added, 1)

            @block.tensor
            def _(pe):
                nc.tensor.transpose(warm[:, 0:P], k.ident[:, :], k.ident[:, :]).then_inc(summed, RING)
                @rounds(pe, STEPS // U)
                def _(i):
                    for u in range(U):
                        pe.wait_ge(s_ready, i * U + (u + 1))
                        pe.wait_ge(gathered[u % RING], i * (16 * U // RING) + 16 * (u // RING + 1))
                        pe.wait_ge(added, i * U + (u + 1))
                        nc.tensor.matmul(acc_ps[u % 2][:, 0:D], s_mat[:, u % 2, :], rows[:, u % RING, :],
                                         start=True, stop=True).then_inc(summed, 1)


def node_phase_1(nc, k):
    with phase(nc) as (sb, ps, sem):
        part = GROUP * D
        xg, ag, h, z = (k.spare[:, n * part:(n + 1) * part].rearrange("p (n d) -> p n d", d=D) for n in range(4))
        kv = k.spare[:, 4 * part:6 * part].rearrange("p (n d) -> p n d", d=2 * D)
        w0 = sb("n1_w0", [P, 2, D])
        wkvq = sb("n1_wkvq", [P, 2, 3 * D])
        bkvq = sb("n1_bkvq", [P, 3 * D])
        bo = sb("n1_bo", [P, D])
        lng, lnb = sb("n1_lng", [P, 2]), sb("n1_lnb", [P, 2])
        turned_sb = sb("n1_turned", [P, 2, D])
        zt_sb = sb("n1_zt", [P, 2, D])
        turned_ps = ps("n1_turned_ps", [P, 2, 512])
        out_ps = ps("n1_out_ps", [P, 2, 512])
        q_ps = ps("n1_q_ps", [P, 2, 512])
        pa, pb = Project(sem, "n1a"), Project(sem, "n1b")
        nb = norm_buffers(sb, sem, "n1")
        weights, loaded, consumed, stored, chain_s = sem("n1_weights"), sem("n1_loaded"), sem("n1_consumed"), sem("n1_stored"), sem("n1_chain")
        z_psum_free = sem("n1_z_psum_free")
        NW = 7
        with nc.Block() as block:
            @block.sync
            def _(sp):
                sp.dma_start(w0[:, :, :], k.w0.rearrange("(q p) n -> p q n", p=P)).then_inc(weights, 16)
                sp.dma_start(wkvq[:, :, :], k.wkvq.rearrange("(q p) n -> p q n", p=P)).then_inc(weights, 16)
                sp.dma_start(bkvq[:, :], k.bkvq.to_broadcast([P, 3 * D])).then_inc(weights, 16)
                sp.dma_start(bo[:, :], k.bo.to_broadcast([P, D])).then_inc(weights, 16)
                with nc.allow_non_contiguous_dma(reason="small vectors"):
                    sp.dma_start(lng[:, :].unsqueeze(2), k.ln1_g.rearrange("(q p o) -> p q o", p=P, o=1)).then_inc(weights, 16)
                    sp.dma_start(lnb[:, :].unsqueeze(2), k.ln1_b.rearrange("(q p o) -> p q o", p=P, o=1)).then_inc(weights, 16)
                @rounds(sp, GROUPS)
                def _(g):
                    sp.wait_ge(stored, g * 32)
                    sp.dma_start(xg[:, :, :], tiles(k.x)[:, bass.ds(g * GROUP, GROUP), :]).then_inc(loaded, 16)
                    sp.wait_ge(pb.used, g * GROUP + GROUP)
                    sp.dma_start(tiles(k.tab_x)[:, bass.ds(g * GROUP, GROUP), :], xg[:, :, :]).then_inc(stored, 16)
                    sp.dma_start(tiles(k.tab_kv)[:, bass.ds(g * GROUP, GROUP), :], kv[:, :, :]).then_inc(stored, 16)
                sp.wait_ge(stored, 32 * GROUPS)

            @block.scalar
            def _(act):
                act.wait_ge(weights, 16 * 6)
                @rounds(act, GROUPS)
                def _(g):
                    act.wait_ge(pa.product, g * GROUP)
                    nc.scalar.copy(ag[:, :, :], k.acc[:, bass.ds(g * (GROUP * D), GROUP * D)].rearrange("p (n d) -> p n d", d=D)
                                   ).then_inc(pa.src_ready, 1)
                    act_project(nc, act, g, pa, 2, turned_ps, turned_sb)
                    act_root(nc, act, g, 0, 2, nb)
                    act_root(nc, act, g, 1, 2, nb)
                    act_project(nc, act, g, pb, 2, turned_ps, zt_sb, lng, lnb)

            @block.vector
            def _(dve):
                link = Chain(dve, chain_s)
                dve.wait_ge(weights, 16 * 6)
                nc.vector.memset(k.node_tab[:, NODE_TILES * D:], 0.0)
                base, per = link.n, 2 * NORM_LINKS + 3
                @rounds(dve, GROUPS)
                def _(g):
                    link.loop(g, per, base)
                    dve.wait_ge(loaded, g * 16 + 16)
                    for u in range(GROUP):
                        dve.wait_ge(pa.product, g * GROUP + (u + 1))
                        nc.vector.scalar_tensor_tensor(xg[:, u, :], out_ps[:, u % 2, 0:D], col(k.dinv, g * GROUP + u), xg[:, u, :],
                                                       ALU.mult, ALU.add).then_inc(pa.used, 1)
                    dve.wait_ge(pa.used, g * GROUP + GROUP)
                    dve_norm(nc, dve, link, g, 0, 2, nb, xg, h)
                    link(nc.vector.tensor_scalar(h[:, :, :], h[:, :, :], 0.0, None, ALU.max))
                    dve_norm(nc, dve, link, g, 1, 2, nb, h, z)
                    link(nc.vector.tensor_tensor(xg[:, :, :], xg[:, :, :], h[:, :, :], ALU.add))
                    link(nc.vector.tensor_tensor(xg[:, :, :], xg[:, :, :], bo[:, :].unsqueeze(1).to_broadcast([P, GROUP, D]), ALU.add))
                    nc.vector.tensor_scalar(nb.var[:, 0:1], nb.rstd[:, 0:1], 0.0, None, ALU.mult).then_inc(pb.src_ready, 1)
                    for u in range(GROUP):
                        dve.wait_ge(pb.product, g * GROUP + (u + 1))
                        dve.wait_ge(stored, g * 32)
                        nc.vector.tensor_tensor(kv[:, u, :], out_ps[:, u % 2, :], bkvq[:, 0:2 * D], ALU.add)
                        nc.vector.tensor_tensor(k.node_tab[:, bass.ds(g * (GROUP * D) + u * D, D)], q_ps[:, u % 2, 0:D],
                                                bkvq[:, 2 * D:3 * D], ALU.add).then_inc(pb.used, 1)

            @block.tensor
            def _(pe):
                pe.wait_ge(weights, 16 * 6)
                @rounds(pe, GROUPS)
                def _(g):
                    pe.wait_ge(pb.copied, g * GROUP)
                    pe.wait_ge(pb.used, g * GROUP)
                    pe_project(nc, pe, k, g, pa, ag, 2, turned_ps, turned_sb, [(out_ps, w0)])
                    pe.wait_ge(pa.used, g * GROUP + GROUP)
                    pe_project(nc, pe, k, g, pb, z, 2, turned_ps, zt_sb, [(out_ps, wkvq[:, :, 0:2 * D]), (q_ps, wkvq[:, :, 2 * D:3 * D])])


def reduce_angle(nc, link, out, turns, x, scale, shift):
    link(nc.vector.tensor_scalar(out, x, scale, shift, ALU.mult, ALU.add))
    link(nc.vector.tensor_scalar(turns, out, 1.0 / TWO_PI, ROUND, ALU.mult, ALU.add))
    link(nc.vector.tensor_scalar(turns, turns, -ROUND, None, ALU.add))
    link(nc.vector.scalar_tensor_tensor(out, turns, -TWO_PI_HI, out, ALU.mult, ALU.add))
    link(nc.vector.scalar_tensor_tensor(out, turns, -TWO_PI_LO, out, ALU.mult, ALU.add))
    link(nc.vector.tensor_scalar(out, out, SIN_MAX, -SIN_MAX, ALU.min, ALU.max))


def cutoffs(nc, k):
    with phase(nc) as (sb, ps, sem):
        ang, turns, cosv, mask = (sb("cut_" + n, [P, STEP_COLS]) for n in ("ang", "turns", "cos", "mask"))
        chain_s, ang_ready, cos_ready = sem("cut_chain"), sem("cut_ang_ready"), sem("cut_cos_ready")
        with nc.Block() as block:
            @block.vector
            def _(dve):
                link = Chain(dve, chain_s)
                reduce_angle(nc, link, ang[:, :], turns[:, :], k.step_w[:, :], float(np.pi / CUTOFF), float(np.pi / 2))
                nc.vector.tensor_scalar(mask[:, :], k.step_w[:, :], CUTOFF, 0.5, ALU.is_lt, ALU.mult).then_inc(ang_ready, 1)
                dve.wait_ge(cos_ready, 1)
                dve.wait_ge(ang_ready, 1)
                link(nc.vector.scalar_tensor_tensor(k.step_w[:, :], cosv[:, :], 1.0, mask[:, :], ALU.add, ALU.mult))

            @block.scalar
            def _(act):
                act.wait_ge(ang_ready, 1)
                nc.scalar.activation(cosv[:, :], ang[:, :], ACT.Sin).then_inc(cos_ready, 1)


def pass_1(nc, k):
    with phase(nc) as (sb, ps, sem):
        begun, tiny = sem("begunpass_1"), sb("tinypass_1", [P, 1])
        U, RING = 16, 8
        kv = k.spare[:, 0:RING * 2 * D].rearrange("p (r d) -> p r d", d=2 * D)
        ea = sb("p1_ea", [R + 1, RING, P])
        idx = sb("p1_idx", [P, U], I32)
        wd = sb("p1_wd", [R + 1, 2 * D])
        s_mat = sb("p1_s", [P, 4, P])
        st_sb = sb("p1_st", [P, 2, P])
        dkv = sb("p1_dkv", [P, 2, 2 * D])
        qk, qkd = sb("p1_qk", [P, D]), sb("p1_qkd", [P, D])
        dots, acts, attn = sb("p1_dots", [P, 2]), sb("p1_acts", [P, 2]), sb("p1_attn", [P, 2])
        sa = sb("p1_sa", [P, 2, P])
        msg = sb("p1_msg", [P, 2, D])
        sq_ps = [ps(f"p1_sq{i}", [P, 512]) for i in range(2)]
        d_ps = [ps(f"p1_d{i}", [P, 512]) for i in range(2)]
        acc_ps = [ps(f"p1_acc{i}", [P, 512]) for i in range(2)]
        warm = ps("p1_warm", [P, 512])
        gathered = [sem(f"p1_gathered{r}") for r in range(RING)]
        ea_loaded = [sem(f"p1_ea_loaded{r}") for r in range(RING)]
        weights, idx_ready, acc_zero = sem("p1_weights"), sem("p1_idx_ready"), sem("p1_acc_zero")
        s_ready, turned, st_ready = sem("p1_s_ready"), sem("p1_turned"), sem("p1_st_ready")
        d_made, silu_done, q_made, qk_done = sem("p1_d_made"), sem("p1_silu_done"), sem("p1_q_made"), sem("p1_qk_done")
        dot_done, act_done, attn_ready = sem("p1_dot_done"), sem("p1_act_done"), sem("p1_attn_ready")
        msg_ready, summed, added = sem("p1_msg_ready"), sem("p1_summed"), sem("p1_added")
        with nc.Block() as block:
            @block.sync
            def _(sp):
                sp.dma_start(wd[:, :], k.wd).then_inc(weights, 16)
                @rounds(sp, STEPS // U)
                def _(i):
                    for u in range(U):
                        e = sp.value_load(k.e_list[0:1, bass.ds(i * U + u, 1)], min_val=0, max_val=EDGE_TILES - 1)
                        sp.wait_ge(d_made, i * U + (u + 1))
                        sp.dma_start(ea[:, u % RING, :], k.ea_t[:, bass.ds(e * P, P)]).then_inc(ea_loaded[u % RING], 16)
                for r in range(RING):
                    sp.wait_ge(ea_loaded[r], 16 * STEPS // RING)

            @block.gpsimd
            def _(pool):
                nc.gpsimd.memset(tiny[:, :], 0.0).then_inc(begun, 1)
                @rounds(pool, STEPS // U)
                def _(i):
                    for u in range(U):
                        if u % RING == 0:
                            pool.wait_ge(msg_ready, i * U + u)
                            settle(pool, begun)
                            nc.gpsimd.tensor_copy(idx[:, u:u + RING], col(k.step_src, i * U + u, RING)).then_inc(idx_ready, 1)
                            pool.wait_ge(idx_ready, i * 2 + (u // RING + 1))
                        pool.wait_ge(msg_ready, i * U + (u + 1))
                        settle(pool, begun)
                        pool.indirect_dma_start(out=kv[:, u % RING, :], out_offset=None, in_=k.tab_kv,
                                                in_offset=bass.IndirectOffsetOnAxis(ap=idx[:, u:u + 1], axis=0)
                                                ).then_inc(gathered[u % RING], 16)

            @block.vector
            def _(dve):
                nc.vector.memset(msg[:, :, :], 0.0)
                nc.vector.memset(sa[:, :, :], 0.0)
                nc.vector.memset(k.acc[:, :], 0.0).then_inc(acc_zero, 1)
                dve.wait_ge(acc_zero, 1)
                nc.vector.tensor_scalar(qk[:, 0:1], k.iota[:, 0:1], 0.0, None, ALU.mult).then_inc(msg_ready, RING)
                for u in range(2):
                    nc.vector.tensor_scalar(s_mat[:, u, :], k.iota[:, :], k.step_rel[:, u:u + 1], None, ALU.is_equal).then_inc(s_ready, 1)
                nc.vector.tensor_scalar(qkd[:, 0:1], k.iota[:, 0:1], 0.0, None, ALU.mult).then_inc(added, 1)
                @rounds(dve, STEPS // U)
                def _(i):
                    for u in range(U):
                        n = dve.value_load(k.n_list[0:1, bass.ds(i * U + u, 1)], min_val=0, max_val=NODE_TILES)
                        dve.wait_ge(q_made, i * U + (u + 1))
                        nc.vector.tensor_scalar(s_mat[:, (u + 2) % 4, :], k.iota[:, :], col(k.step_rel, i * U + (u + 2)), None,
                                                ALU.is_equal).then_inc(s_ready, 1)
                        dve.wait_ge(gathered[u % RING], i * (16 * U // RING) + 16 * (u // RING + 1))
                        nc.vector.tensor_tensor(qk[:, :], sq_ps[u % 2][:, P:P + D], kv[:, u % RING, 0:D], ALU.mult).then_inc(qk_done, 1)
                        dve.wait_ge(silu_done, i * U + (u + 1))
                        dve.wait_ge(qk_done, i * U + (u + 1))
                        nc.vector.tensor_tensor_reduce(out=qkd[:, :], in0=qk[:, :], in1=dkv[:, u % 2, 0:D], scale=1.0, scalar=0.0,
                                                       op0=ALU.mult, op1=ALU.add, accum_out=dots[:, u % 2:u % 2 + 1]
                                                       ).then_inc(dot_done, 1)
                        dve.wait_ge(summed, i * U + u)
                        nc.vector.tensor_tensor(msg[:, u % 2, :], kv[:, u % RING, D:2 * D], dkv[:, u % 2, D:2 * D], ALU.mult)
                        dve.wait_ge(summed, i * U + (u + 1))
                        dve.wait_ge(added, i * U + (u + 1))
                        nc.vector.tensor_tensor(k.acc[:, bass.ds(n * D, D)], k.acc[:, bass.ds(n * D, D)],
                                                acc_ps[(u + 1) % 2][:, 0:D], ALU.add).then_inc(added, 1)
                        dve.wait_ge(attn_ready, i * U + (u + 1))
                        nc.vector.tensor_scalar(sa[:, u % 2, :], s_mat[:, u % 4, :], attn[:, u % 2:u % 2 + 1], None,
                                                ALU.mult).then_inc(msg_ready, 1)
                n = dve.value_load(k.n_list[0:1, STEPS:STEPS + 1], min_val=0, max_val=NODE_TILES)
                dve.wait_ge(summed, STEPS + 1)
                dve.wait_ge(added, STEPS + 1)
                nc.vector.tensor_tensor(k.acc[:, bass.ds(n * D, D)], k.acc[:, bass.ds(n * D, D)], acc_ps[1][:, 0:D], ALU.add).then_inc(added, 1)
                dve.wait_ge(added, STEPS + 2)

            @block.scalar
            def _(act):
                def prepare(i, s, n):
                    act.wait_ge(turned, n + 1)
                    nc.scalar.copy(st_sb[:, s % 2, :], sq_ps[s % 2][:, 0:P]).then_inc(st_ready, 1)
                    act.wait_ge(d_made, n + (RING + 1))
                    if s >= 2 or i is not None:
                        act.wait_ge(msg_ready, n + (RING - 1))
                    nc.scalar.activation(dkv[:, s % 2, :], d_ps[s % 2][:, :], ACT.Silu).then_inc(silu_done, 1)

                def attention(u, n):
                    act.wait_ge(dot_done, n + 1)
                    nc.scalar.activation(acts[:, u % 2:u % 2 + 1], dots[:, u % 2:u % 2 + 1], ACT.Silu).then_inc(act_done, 1)
                    act.wait_ge(act_done, n + 1)
                    nc.scalar.activation(attn[:, u % 2:u % 2 + 1], acts[:, u % 2:u % 2 + 1], ACT.Copy,
                                         scale=col(k.step_w, n)).then_inc(attn_ready, 1)

                prepare(None, 0, 0)
                @rounds(act, STEPS // U - 1)
                def _(i):
                    for u in range(U):
                        prepare(i, u + 1, i * U + (u + 1))
                        attention(u, i * U + u)
                last = STEPS - U
                for u in range(U):
                    if u + 1 < U:
                        prepare(STEPS // U - 1, u + 1, last + u + 1)
                    attention(u, last + u)

            @block.tensor
            def _(pe):
                def prepare(i, s, n):
                    if i is not None:
                        pe.wait_ge(qk_done, n - 1)
                    pe.wait_ge(s_ready, n + 1)
                    nc.tensor.transpose(sq_ps[s % 2][:, 0:P], s_mat[:, s % 4, :], k.ident[:, :]).then_inc(turned, 1)
                    if i is not None:
                        pe.wait_ge(silu_done, n - 1)
                    if s < U:
                        pe.wait_ge(ea_loaded[s % RING], (0 if i is None else i * (16 * U // RING)) + 16 * (s // RING + 1))
                    else:
                        pe.wait_ge(ea_loaded[0], i * (16 * U // RING) + (16 * U // RING + 16))
                    nc.tensor.matmul(d_ps[s % 2][:, :], ea[:, s % RING, :], wd[:, :], start=True, stop=True).then_inc(d_made, 1)
                    t = pe.value_load(k.n_list[0:1, bass.ds(n + 1, 1)], min_val=0, max_val=NODE_TILES)
                    pe.wait_ge(st_ready, n + 1)
                    nc.tensor.matmul(sq_ps[s % 2][:, P:P + D], st_sb[:, s % 2, :], k.node_tab[:, bass.ds(t * D, D)],
                                     start=True, stop=True).then_inc(q_made, 1)

                def sum_messages(u, n):
                    pe.wait_ge(added, n)
                    pe.wait_ge(msg_ready, n + (RING + 1))
                    nc.tensor.matmul(acc_ps[u % 2][:, 0:D], sa[:, u % 2, :], msg[:, u % 2, :], start=True, stop=True).then_inc(summed, 1)

                pe.wait_ge(weights, 16)
                nc.tensor.transpose(warm[:, 0:P], k.ident[:, :], k.ident[:, :]).then_inc(d_made, RING)
                pe.wait_ge(acc_zero, 1)
                nc.tensor.matmul(acc_ps[1][:, 0:D], sa[:, 1, :], msg[:, 1, :], start=True, stop=True).then_inc(summed, 1)
                prepare(None, 0, 0)
                @rounds(pe, STEPS // U - 1)
                def _(i):
                    for u in range(U):
                        prepare(i, u + 1, i * U + (u + 1))
                        sum_messages(u, i * U + u)
                last = STEPS - U
                for u in range(U):
                    if u + 1 < U:
                        prepare(STEPS // U - 1, u + 1, last + u + 1)
                    sum_messages(u, last + u)


def node_phase_2(nc, k):
    with phase(nc) as (sb, ps, sem):
        xg = sb("n2_x", [P, GROUP, D])
        ag = sb("n2_acc", [P, GROUP, D])
        h = sb("n2_h", [P, GROUP, D])
        wo = sb("n2_wo", [P, 2, D])
        turned_sb = sb("n2_turned", [P, 2, D])
        turned_ps, out_ps = ps("n2_turned_ps", [P, 2, 512]), ps("n2_out_ps", [P, 2, 512])
        pa = Project(sem, "n2a")
        nb = norm_buffers(sb, sem, "n2")
        weights, loaded, made, stored, chain_s = sem("n2_weights"), sem("n2_loaded"), sem("n2_made"), sem("n2_stored"), sem("n2_chain")
        with nc.Block() as block:
            @block.sync
            def _(sp):
                sp.dma_start(wo[:, :, :], k.wo.rearrange("(q p) n -> p q n", p=P)).then_inc(weights, 16)
                @rounds(sp, GROUPS)
                def _(g):
                    sp.wait_ge(stored, g * 32)
                    sp.dma_start(xg[:, :, :], tiles(k.tab_x)[:, bass.ds(g * GROUP, GROUP), :]).then_inc(loaded, 16)
                    sp.wait_ge(made, g + 1)
                    sp.dma_start(tiles(k.tab_x2)[:, bass.ds(g * GROUP, GROUP), :], xg[:, :, :]).then_inc(stored, 16)
                    sp.dma_start(tiles(k.tab_h)[:, bass.ds(g * GROUP, GROUP), :], h[:, :, :]).then_inc(stored, 16)
                sp.wait_ge(stored, 32 * GROUPS)

            @block.scalar
            def _(act):
                @rounds(act, GROUPS)
                def _(g):
                    act.wait_ge(pa.product, g * GROUP)
                    nc.scalar.copy(ag[:, :, :], k.acc[:, bass.ds(g * (GROUP * D), GROUP * D)].rearrange("p (n d) -> p n d", d=D)
                                   ).then_inc(pa.src_ready, 1)
                    act_project(nc, act, g, pa, 2, turned_ps, turned_sb)
                    act_root(nc, act, g, 0, 1, nb)

            @block.vector
            def _(dve):
                link = Chain(dve, chain_s)
                @rounds(dve, GROUPS)
                def _(g):
                    link.loop(g, NORM_LINKS + 1, 0)
                    dve.wait_ge(loaded, g * 16 + 16)
                    for u in range(GROUP):
                        dve.wait_ge(pa.product, g * GROUP + (u + 1))
                        nc.vector.tensor_tensor(xg[:, u, :], out_ps[:, u % 2, 0:D], xg[:, u, :], ALU.add).then_inc(pa.used, 1)
                    dve.wait_ge(pa.used, g * GROUP + GROUP)
                    dve_norm(nc, dve, link, g, 0, 1, nb, xg, h)
                    link(nc.vector.tensor_scalar(h[:, :, :], h[:, :, :], 0.0, None, ALU.max))
                    nc.vector.tensor_copy(k.node_tab[:, bass.ds(g * (GROUP * D), GROUP * D)].rearrange("p (n d) -> p n d", d=D),
                                          h[:, :, :]).then_inc(made, 1)

            @block.tensor
            def _(pe):
                pe.wait_ge(weights, 16)
                @rounds(pe, GROUPS)
                def _(g):
                    pe_project(nc, pe, k, g, pa, ag, 2, turned_ps, turned_sb, [(out_ps, wo)])


def pass_2(nc, k):
    with phase(nc) as (sb, ps, sem):
        begun, tiny = sem("begunpass_2"), sb("tinypass_2", [P, 1])
        U, RING, LEAD = 16, 8, 4
        SLOT = D + SORT_ROW
        slot = sb("p2_slot", [P, RING, SLOT])
        gidx, pidx = sb("p2_gidx", [P, RING], I32), sb("p2_pidx", [P, RING], I32)
        s_mat = sb("p2_s", [P, 4, P])
        st_sb = sb("p2_st", [P, 2, P])
        h_ps = [ps(f"p2_h{i}", [P, 512]) for i in range(2)]
        acc_ps = [ps(f"p2_acc{i}", [P, 512]) for i in range(2)]
        gathered = [sem(f"p2_gathered{r}") for r in range(RING)]
        e_loaded = [sem(f"p2_e_loaded{r}") for r in range(RING)]
        scattered = [sem(f"p2_scattered{r}") for r in range(RING)]
        gidx_ready, pidx_ready = sem("p2_gidx_ready"), sem("p2_pidx_ready")
        s_ready, turned, st_ready, h_made, h_copied = sem("p2_s_ready"), sem("p2_turned"), sem("p2_st_ready"), sem("p2_h_made"), sem("p2_h_copied")
        summed, added, zeroed = sem("p2_summed"), sem("p2_added"), sem("p2_zeroed")
        W = 2 * D
        per = 16 * U // RING
        with nc.Block() as block:
            @block.sync
            def _(sp):
                @rounds(sp, STEPS // U)
                def _(i):
                    for u in range(U):
                        r = u % RING
                        e = sp.value_load(k.e_list[0:1, bass.ds(i * U + u, 1)], min_val=0, max_val=EDGE_TILES - 1)
                        sp.wait_ge(scattered[r], i * per + 16 * (u // RING))
                        sp.dma_start(slot[:, r, D:2 * D], tiles(k.e256)[:, bass.ds(e, 1), :].rearrange("p o d -> p (o d)")
                                     ).then_inc(e_loaded[r], 16)
                for r in range(RING):
                    sp.wait_ge(e_loaded[r], 16 * STEPS // RING)

            @block.gpsimd
            def _(pool):
                def gather(u, n, count):
                    r = u % RING
                    pool.wait_ge(scattered[r], count)
                    settle(pool, begun)
                    pool.indirect_dma_start(out=slot[:, r, 0:D], out_offset=None, in_=k.tab_h,
                                            in_offset=bass.IndirectOffsetOnAxis(ap=gidx[:, r:r + 1], axis=0)).then_inc(gathered[r], 16)

                nc.gpsimd.memset(tiny[:, :], 0.0).then_inc(begun, 1)
                nc.gpsimd.memset(slot[:, :, 3 * D:SLOT], 0.0).then_inc(zeroed, 1)
                nc.gpsimd.tensor_copy(gidx[:, 0:LEAD], k.step_src[:, 0:LEAD]).then_inc(gidx_ready, 1)
                pool.wait_ge(gidx_ready, 1)
                for u in range(LEAD):
                    gather(u, u, 0)
                @rounds(pool, STEPS // U)
                def _(i):
                    for u in range(U):
                        r = u % RING
                        if u % LEAD == 0:
                            q = (r + LEAD) % RING
                            for x in range(LEAD):
                                pool.wait_ge(scattered[q + x], i * per + 16 * ((u + LEAD) // RING))
                            settle(pool, begun)
                            nc.gpsimd.tensor_copy(gidx[:, q:q + LEAD], col(k.step_src, i * U + (u + LEAD), LEAD)).then_inc(gidx_ready, 1)
                            for x in range(LEAD):
                                pool.wait_ge(scattered[r + x], i * per + 16 * (u // RING))
                            settle(pool, begun)
                            nc.gpsimd.tensor_copy(pidx[:, r:r + LEAD], col(k.step_place, i * U + u, LEAD)).then_inc(pidx_ready, 1)
                            pool.wait_ge(gidx_ready, i * (U // LEAD) + (u // LEAD + 2))
                            pool.wait_ge(pidx_ready, i * (U // LEAD) + (u // LEAD + 1))
                        gather(u + LEAD, None, i * per + 16 * ((u + LEAD) // RING))
                        pool.wait_ge(e_loaded[r], i * per + 16 * (u // RING + 1))
                        pool.wait_ge(h_copied, i * U + (u + 1))
                        pool.wait_ge(summed, i * U + (u + 1))
                        settle(pool, begun)
                        pool.indirect_dma_start(out=k.tab_sorted, out_offset=bass.IndirectOffsetOnAxis(ap=pidx[:, r:r + 1], axis=0),
                                                in_=slot[:, r, D:SLOT], in_offset=None,
                                                bounds_check=EDGES_PAD - 1, oob_is_err=False).then_inc(scattered[r], 16)
                for r in range(RING):
                    pool.wait_ge(scattered[r], 16 * STEPS // RING)
                    pool.wait_ge(gathered[r], 16 * STEPS // RING + (16 if r < LEAD else 0))

            @block.vector
            def _(dve):
                nc.vector.memset(k.acc2[:, :], 0.0).then_inc(added, 2)
                for u in range(2):
                    nc.vector.tensor_scalar(s_mat[:, u, :], k.iota[:, :], k.step_rel[:, u:u + 1], None, ALU.is_equal).then_inc(s_ready, 1)
                @rounds(dve, STEPS // U)
                def _(i):
                    for u in range(U):
                        n = dve.value_load(k.n_list[0:1, bass.ds(i * U + (u + 1), 1)], min_val=0, max_val=NODE_TILES)
                        nc.vector.tensor_scalar(s_mat[:, (u + 2) % 4, :], k.iota[:, :], col(k.step_rel, i * U + (u + 2)), None,
                                                ALU.is_equal).then_inc(s_ready, 1)
                        dve.wait_ge(summed, i * U + (u + 1))
                        dve.wait_ge(added, i * U + (u + 2))
                        nc.vector.tensor_tensor(k.acc2[:, bass.ds(n * W, W)], k.acc2[:, bass.ds(n * W, W)],
                                                acc_ps[u % 2][:, :], ALU.add).then_inc(added, 1)
                dve.wait_ge(added, STEPS + 2)

            @block.scalar
            def _(act):
                @rounds(act, STEPS // U)
                def _(i):
                    for u in range(U):
                        r = u % RING
                        act.wait_ge(turned, i * U + (u + 1))
                        nc.scalar.copy(st_sb[:, u % 2, :], h_ps[u % 2][:, 0:P]).then_inc(st_ready, 1)
                        act.wait_ge(scattered[r], i * per + 16 * (u // RING))
                        if u == 0:
                            act.wait_ge(zeroed, 1)
                        nc.scalar.copy(slot[:, r, 3 * D:3 * D + 1], col(k.step_src, i * U + u))
                        act.wait_ge(h_made, i * U + (u + 1))
                        nc.scalar.copy(slot[:, r, 2 * D:3 * D], h_ps[u % 2][:, P:P + D]).then_inc(h_copied, 1)

            @block.tensor
            def _(pe):
                def turn(s, n):
                    pe.wait_ge(s_ready, n + 1)
                    nc.tensor.transpose(h_ps[s % 2][:, 0:P], s_mat[:, s % 4, :], k.ident[:, :]).then_inc(turned, 1)

                turn(0, 0)
                @rounds(pe, STEPS // U)
                def _(i):
                    for u in range(U):
                        r = u % RING
                        t = pe.value_load(k.n_list[0:1, bass.ds(i * U + (u + 1), 1)], min_val=0, max_val=NODE_TILES)
                        pe.wait_ge(h_copied, i * U + u)
                        turn(u + 1, i * U + (u + 1))
                        pe.wait_ge(st_ready, i * U + (u + 1))
                        nc.tensor.matmul(h_ps[u % 2][:, P:P + D], st_sb[:, u % 2, :], k.node_tab[:, bass.ds(t * D, D)],
                                         start=True, stop=True).then_inc(h_made, 1)
                        pe.wait_ge(gathered[r], i * per + 16 * (u // RING + 1))
                        pe.wait_ge(e_loaded[r], i * per + 16 * (u // RING + 1))
                        pe.wait_ge(added, i * U + (u + 1))
                        nc.tensor.matmul(acc_ps[u % 2][:, :], s_mat[:, u % 4, :], slot[:, r, 0:W], start=True, stop=True).then_inc(summed, 1)


def node_phase_3(nc, k):
    with phase(nc) as (sb, ps, sem):
        ag = sb("n3_acc", [P, GROUP, 2 * D])
        fg = sb("n3_f", [P, GROUP, D])
        w = sb("n3_w", [P, 4, D])
        b = sb("n3_b", [P, D])
        turned_sb = sb("n3_turned", [P, 2, 2 * D])
        turned_ps, out_ps = ps("n3_turned_ps", [P, 2, 512]), ps("n3_out_ps", [P, 2, 512])
        pa = Project(sem, "n3a")
        weights, stored = sem("n3_weights"), sem("n3_stored")
        with nc.Block() as block:
            @block.sync
            def _(sp):
                sp.dma_start(w[:, :, :], k.wf.rearrange("(q p) n -> p q n", p=P)).then_inc(weights, 16)
                sp.dma_start(b[:, :], k.bf.to_broadcast([P, D])).then_inc(weights, 16)
                @rounds(sp, GROUPS)
                def _(g):
                    sp.wait_ge(pa.used, g * GROUP + GROUP)
                    sp.dma_start(tiles(k.tab_f)[:, bass.ds(g * GROUP, GROUP), :], fg[:, :, :]).then_inc(stored, 16)
                sp.wait_ge(stored, 16 * GROUPS)

            @block.scalar
            def _(act):
                @rounds(act, GROUPS)
                def _(g):
                    act.wait_ge(pa.product, g * GROUP)
                    nc.scalar.copy(ag[:, :, :], k.acc2[:, bass.ds(g * (GROUP * 2 * D), GROUP * 2 * D)].rearrange("p (n d) -> p n d", d=2 * D)
                                   ).then_inc(pa.src_ready, 1)
                    act_project(nc, act, g, pa, 4, turned_ps, turned_sb)

            @block.vector
            def _(dve):
                dve.wait_ge(weights, 32)
                @rounds(dve, GROUPS)
                def _(g):
                    dve.wait_ge(stored, g * 16)
                    for u in range(GROUP):
                        dve.wait_ge(pa.product, g * GROUP + (u + 1))
                        nc.vector.scalar_tensor_tensor(fg[:, u, :], b[:, :], k.cnt[:, 0, bass.ds(g * GROUP + u, 1)], out_ps[:, u % 2, 0:D],
                                                       ALU.mult, ALU.add).then_inc(pa.used, 1)

            @block.tensor
            def _(pe):
                pe.wait_ge(weights, 32)
                @rounds(pe, GROUPS)
                def _(g):
                    pe_project(nc, pe, k, g, pa, ag, 4, turned_ps, turned_sb, [(out_ps, w)])


def pass_3(nc, k):
    with phase(nc) as (sb, ps, sem):
        U, RING = 16, 8
        W = 2 * D
        slot = sb("p3_slot", [P, RING, SORT_ROW])
        s_mat = sb("p3_s", [P, 2, P])
        e_list, n_list = sb("p3_e_list", [1, STEP_COLS], I32), sb("p3_n_list", [1, STEP_COLS], I32)
        n128 = sb("p3_n128", [P, STEPS])
        walk = sem("p3_walk")
        acc_ps = [ps(f"p3_acc{i}", [P, 512]) for i in range(2)]
        loaded = [sem(f"p3_loaded{r}") for r in range(RING)]
        s_ready, summed, added = sem("p3_s_ready"), sem("p3_summed"), sem("p3_added")
        warm = ps("p3_warm", [P, 512])
        per = 16 * U // RING
        with nc.Block() as block:
            @block.sync
            def _(sp):
                sp.dma_start(e_list[:, :], k.walk_lists[0:1, :]).then_inc(walk, 16)
                sp.dma_start(n_list[:, :], k.walk_lists[1:2, :]).then_inc(walk, 16)
                sp.dma_start(n128[:, :], k.walk_n128.to_broadcast([P, STEPS])).then_inc(walk, 16)
                sp.wait_ge(walk, 48)
                @rounds(sp, STEPS // U)
                def _(i):
                    for u in range(U):
                        r = u % RING
                        e = sp.value_load(e_list[0:1, bass.ds(i * U + u, 1)], min_val=0, max_val=EDGE_TILES - 1)
                        sp.wait_ge(summed, i * U + (u + 1))
                        sp.dma_start(slot[:, r, :], tiles(k.tab_sorted)[:, bass.ds(e, 1), :].rearrange("p o d -> p (o d)")
                                     ).then_inc(loaded[r], 16)
                for r in range(RING):
                    sp.wait_ge(loaded[r], 16 * STEPS // RING)

            @block.vector
            def _(dve):
                dve.wait_ge(walk, 48)

                def one_hot(u, n, count):
                    r = u % RING
                    dve.wait_ge(loaded[r], count)
                    nc.vector.tensor_scalar(s_mat[:, u % 2, :], k.iota[:, :], col(n128, n), slot[:, r, 2 * D:2 * D + 1],
                                            ALU.add, ALU.is_equal).then_inc(s_ready, 1)

                nc.vector.memset(k.acc2[:, :], 0.0).then_inc(added, 2)
                for u in range(2):
                    one_hot(u, u, 16)
                @rounds(dve, STEPS // U - 1)
                def _(i):
                    for u in range(U):
                        n = dve.value_load(n_list[0:1, bass.ds(i * U + (u + 1), 1)], min_val=0, max_val=NODE_TILES)
                        dve.wait_ge(summed, i * U + (RING + u + 1))
                        one_hot(u + 2, i * U + (u + 2), i * per + 16 * ((u + 2) // RING + 1))
                        dve.wait_ge(added, i * U + (u + 2))
                        nc.vector.tensor_tensor(k.acc2[:, bass.ds(n * W, W)], k.acc2[:, bass.ds(n * W, W)],
                                                acc_ps[u % 2][:, :], ALU.add).then_inc(added, 1)
                first = STEPS - U
                for u in range(U):
                    n = dve.value_load(n_list[0:1, first + u + 1:first + u + 2], min_val=0, max_val=NODE_TILES)
                    dve.wait_ge(summed, first + RING + u + 1)
                    if u + 2 < U:
                        one_hot(u + 2, first + u + 2, (STEPS // U - 1) * per + 16 * ((u + 2) // RING + 1))
                    dve.wait_ge(added, first + u + 2)
                    nc.vector.tensor_tensor(k.acc2[:, bass.ds(n * W, W)], k.acc2[:, bass.ds(n * W, W)],
                                            acc_ps[u % 2][:, :], ALU.add).then_inc(added, 1)
                dve.wait_ge(added, STEPS + 2)

            @block.tensor
            def _(pe):
                nc.tensor.transpose(warm[:, 0:P], k.ident[:, :], k.ident[:, :]).then_inc(summed, RING)
                @rounds(pe, STEPS // U)
                def _(i):
                    for u in range(U):
                        r = u % RING
                        pe.wait_ge(s_ready, i * U + (u + 1))
                        pe.wait_ge(loaded[r], i * per + 16 * (u // RING + 1))
                        pe.wait_ge(added, i * U + (u + 1))
                        nc.tensor.matmul(acc_ps[u % 2][:, :], s_mat[:, u % 2, :], slot[:, r, 0:W], start=True, stop=True).then_inc(summed, 1)


def node_phase_4(nc, k):
    with phase(nc) as (sb, ps, sem):
        xg, hg, fg = sb("n4_x", [P, GROUP, D]), sb("n4_h", [P, GROUP, D]), sb("n4_f", [P, GROUP, D])
        ag = sb("n4_acc", [P, GROUP, 2 * D])
        t = sb("n4_t", [P, GROUP, D])
        w = sb("n4_w", [P, 4, D])
        b, lnw, lnb = sb("n4_b", [P, D]), sb("n4_lnw", [P, D]), sb("n4_lnb", [P, D])
        total, inv = sb("n4_total", [P, NODE_TILES]), sb("n4_inv", [P, NODE_TILES])
        padding = sb("n4_padding", [P, NODE_TILES])
        turned_sb = sb("n4_turned", [P, 2, 2 * D])
        turned_ps, out_ps = ps("n4_turned_ps", [P, 2, 512]), ps("n4_out_ps", [P, 2, 512])
        pa, pb = Project(sem, "n4a"), Project(sem, "n4b")
        nb = norm_buffers(sb, sem, "n4")
        weights, loaded, stored, chain_s, pad_s = sem("n4_weights"), sem("n4_loaded"), sem("n4_stored"), sem("n4_chain"), sem("n4_pad")
        with nc.Block() as block:
            @block.gpsimd
            def _(pool):
                nc.gpsimd.memset(padding[:, :], 1.0).then_inc(pad_s, 1)
                pool.wait_ge(pad_s, 1)
                nc.gpsimd.affine_select(out=padding[:, :], in_=padding[:, :], compare_op=ALU.is_ge, fill=0.0,
                                        base=-NODES, pattern=[[P, NODE_TILES]], channel_multiplier=1).then_inc(pad_s, 1)

            @block.sync
            def _(sp):
                sp.dma_start(w[:, :, :], k.wb.rearrange("(q p) n -> p q n", p=P)).then_inc(weights, 16)
                for dest, src in ((b, k.bb), (lnw, k.ln2_w), (lnb, k.ln2_b)):
                    sp.dma_start(dest[:, :], src.to_broadcast([P, D])).then_inc(weights, 16)
                @rounds(sp, GROUPS)
                def _(g):
                    sp.wait_ge(stored, g * 16)
                    for dest, src in ((xg, k.tab_x2), (hg, k.tab_h), (fg, k.tab_f)):
                        sp.dma_start(dest[:, :, :], tiles(src)[:, bass.ds(g * GROUP, GROUP), :]).then_inc(loaded, 16)
                    sp.wait_ge(pb.used, g * GROUP + GROUP)
                    sp.dma_start(tiles(k.out)[:, bass.ds(g * GROUP, GROUP), :], xg[:, :, :]).then_inc(stored, 16)
                sp.wait_ge(stored, 16 * GROUPS)

            @block.scalar
            def _(act):
                @rounds(act, GROUPS)
                def _(g):
                    act.wait_ge(pa.product, g * GROUP)
                    nc.scalar.copy(ag[:, :, :], k.acc2[:, bass.ds(g * (GROUP * 2 * D), GROUP * 2 * D)].rearrange("p (n d) -> p n d", d=2 * D)
                                   ).then_inc(pa.src_ready, 1)
                    act.wait_ge(pb.product, g * GROUP)
                    act_project(nc, act, g, pa, 4, turned_ps, turned_sb)
                    act_root(nc, act, g, 0, 2, nb)
                    act_root(nc, act, g, 1, 2, nb)
                    act_project(nc, act, g, pb, 2, turned_ps, turned_sb)

            @block.vector
            def _(dve):
                link = Chain(dve, chain_s)
                dve.wait_ge(weights, 64)
                dve.wait_ge(pad_s, 2)
                link(nc.vector.tensor_tensor(total[:, :], k.cnt[:, 0, :], k.cnt[:, 1, :], ALU.add))
                link(nc.vector.tensor_tensor(total[:, :], total[:, :], padding[:, :], ALU.add))
                link(nc.vector.reciprocal(inv[:, :], total[:, :]))
                base, per = link.n, 2 * NORM_LINKS + 5 + 2 * GROUP
                @rounds(dve, GROUPS)
                def _(g):
                    link.loop(g, per, base)
                    dve.wait_ge(loaded, g * 48 + 48)
                    for u in range(GROUP):
                        dve.wait_ge(pa.product, g * GROUP + (u + 1))
                        nc.vector.tensor_tensor(t[:, u, :], out_ps[:, u % 2, 0:D], fg[:, u, :], ALU.add).then_inc(pa.used, 1)
                    dve.wait_ge(pa.used, g * GROUP + GROUP)
                    for u in range(GROUP):
                        link(nc.vector.scalar_tensor_tensor(t[:, u, :], b[:, :], k.cnt[:, 1, bass.ds(g * GROUP + u, 1)], t[:, u, :],
                                                            ALU.mult, ALU.add))
                    for u in range(GROUP):
                        link(nc.vector.tensor_scalar(t[:, u, :], t[:, u, :], col(inv, g * GROUP + u), None, ALU.mult))
                    link(nc.vector.scalar_tensor_tensor(t[:, :, :], t[:, :, :], 0.01, t[:, :, :], ALU.mult, ALU.max))
                    link(nc.vector.tensor_tensor(t[:, :, :], t[:, :, :], hg[:, :, :], ALU.add))
                    dve_norm(nc, dve, link, g, 0, 2, nb, t, hg)
                    link(nc.vector.tensor_tensor(hg[:, :, :], hg[:, :, :], lnw[:, :].unsqueeze(1).to_broadcast([P, GROUP, D]), ALU.mult))
                    link(nc.vector.tensor_tensor(hg[:, :, :], hg[:, :, :], lnb[:, :].unsqueeze(1).to_broadcast([P, GROUP, D]), ALU.add))
                    link(nc.vector.tensor_tensor(xg[:, :, :], xg[:, :, :], hg[:, :, :], ALU.add))
                    dve_norm(nc, dve, link, g, 1, 2, nb, xg, t)
                    nc.vector.tensor_scalar(t[:, :, :], t[:, :, :], 0.0, None, ALU.max).then_inc(pb.src_ready, 1)
                    for u in range(GROUP):
                        dve.wait_ge(pb.product, g * GROUP + (u + 1))
                        nc.vector.tensor_tensor(xg[:, u, :], out_ps[:, u % 2, 0:D], xg[:, u, :], ALU.add).then_inc(pb.used, 1)

            @block.tensor
            def _(pe):
                pe.wait_ge(weights, 64)
                @rounds(pe, GROUPS)
                def _(g):
                    pe.wait_ge(pb.copied, g * GROUP)
                    pe.wait_ge(pb.used, g * GROUP)
                    pe_project(nc, pe, k, g, pa, ag, 4, turned_ps, turned_sb, [(out_ps, w)])
                    pe.wait_ge(pa.used, g * GROUP + GROUP)
                    pe_project(nc, pe, k, g, pb, t, 2, turned_ps, turned_sb, [(out_ps, k.rot_t)])


def rotation_records(nc, k):
    with phase(nc) as (sb, ps, sem):
        T = EDGE_TILES
        H = T // 2
        rec, pos = k.rec, k.rec_pos
        idx_i = sb("rl_idx_i", [P, 2, T], I32)
        f = sb("rl_f", [P, 2, T])
        fc = sb("rl_fc", [P, 2, T])
        m = sb("rl_m", [P, 2, T])
        w = sb("rl_w", [P, T])
        ang = sb("rl_ang", [P, 2, T])
        turns, sign = sb("rl_turns", [P, T]), sb("rl_sign", [P, T])
        sc = sb("rl_sc", [P, 2, T])
        active, both, count = sb("rl_active", [P, T]), sb("rl_both", [P, T]), sb("rl_count", [P, T])
        total, incl, zeros = sb("rl_total", [P, T]), sb("rl_incl", [P, T]), sb("rl_zeros", [P, T])
        nb_f = sb("rl_nb_f", [P, 1])
        zrow = sb("rl_zrow", [P, ROT_PIECE * REC])
        before_ps, total_ps = ps("rl_before", [P, 2, 512]), ps("rl_total_ps", [P, 2, 512])
        loaded, chain_s, ang_ready, sc_ready = sem("rl_loaded"), sem("rl_chain"), sem("rl_ang_ready"), sem("rl_sc_ready")
        count_ready, before_ready, zrow_ready, cleared = sem("rl_count_ready"), sem("rl_before_ready"), sem("rl_zrow_ready"), sem("rl_cleared")
        with nc.Block() as block:
            @block.sync
            def _(sp):
                sp.dma_start(idx_i[:, 0, :], k.src_cols[:, 0:T]).then_inc(loaded, 16)
                sp.dma_start(idx_i[:, 1, :], k.dst_cols[:, 0:T]).then_inc(loaded, 16)
                sp.dma_start(w[:, :], k.w_cols[:, 0:T]).then_inc(loaded, 16)
                sp.wait_ge(zrow_ready, 1)
                sp.dma_start(k.rot_list.rearrange("(p r t) f -> p r (t f)", p=P, t=ROT_PIECE),
                             zrow[:, :].unsqueeze(1).to_broadcast([P, ROT_ROWS // (P * ROT_PIECE), ROT_PIECE * REC])
                             ).then_inc(cleared, 16)
                sp.wait_ge(loaded, 48)
                sp.wait_ge(cleared, 16)

            @block.scalar
            def _(act):
                act.wait_ge(ang_ready, 1)
                nc.scalar.activation(sc[:, :, :], ang[:, :, :], ACT.Sin).then_inc(sc_ready, 1)

            @block.gpsimd
            def _(pool):
                nc.gpsimd.memset(zrow[:, :], 0.0).then_inc(zrow_ready, 1)

            @block.vector
            def _(dve):
                link = Chain(dve, chain_s)
                dve.wait_ge(loaded, 48)
                link(nc.vector.tensor_copy(f[:, :, :], idx_i[:, :, :]))
                link(nc.vector.tensor_scalar(m[:, :, :], f[:, :, :], D - 0.5, None, ALU.is_lt))
                link(nc.vector.tensor_tensor(turns[:, :], f[:, 0, :], f[:, 1, :], ALU.not_equal))
                link(nc.vector.tensor_tensor(m[:, 0, :], m[:, 0, :], turns[:, :], ALU.mult))
                link(nc.vector.tensor_tensor(active[:, :], m[:, 0, :], m[:, 1, :], ALU.max))
                link(nc.vector.tensor_tensor(both[:, :], m[:, 0, :], m[:, 1, :], ALU.mult))
                nc.vector.tensor_tensor(count[:, :], m[:, 0, :], m[:, 1, :], ALU.add).then_inc(count_ready, 1)
                reduce_angle(nc, link, ang[:, 0, :], turns[:, :], w[:, :], 1.0, 0.0)
                reduce_angle(nc, link, ang[:, 1, :], turns[:, :], w[:, :], 1.0, float(np.pi / 2))
                nc.vector.memset(zeros[:, :], 0.0).then_inc(ang_ready, 1)
                dve.wait_ge(ang_ready, 1)
                link(nc.vector.tensor_scalar(fc[:, :, :], f[:, :, :], D - 1.0, None, ALU.min))
                for n, (own, other) in enumerate(((f[:, 0, :], f[:, 1, :]), (fc[:, 1, :], fc[:, 0, :]))):
                    link(nc.vector.tensor_tensor(total[:, :], own, other, ALU.subtract))
                    link(nc.vector.tensor_tensor(total[:, :], total[:, :], m[:, 0, :], ALU.mult))
                    link(nc.vector.tensor_tensor(rec[:, :, n], total[:, :], other, ALU.add))
                    link(nc.vector.tensor_tensor(rec[:, :, 4 + n], other, both[:, :], ALU.mult))
                link(nc.vector.tensor_scalar(rec[:, :, 8], both[:, :], -1.0, None, ALU.mult))
                link(nc.vector.tensor_scalar(sign[:, :], m[:, 0, :], -2.0, 1.0, ALU.mult, ALU.add))
                dve.wait_ge(sc_ready, 1)
                link(nc.vector.tensor_scalar(rec[:, :, 2], sc[:, 1, :], -1.0, None, ALU.add))
                link(nc.vector.tensor_tensor(rec[:, :, 3], sc[:, 0, :], sign[:, :], ALU.mult))
                link(nc.vector.scalar_tensor_tensor(rec[:, :, 6], sc[:, 1, :], -1.0, both[:, :], ALU.add, ALU.mult))
                link(nc.vector.tensor_tensor(rec[:, :, 7], sc[:, 0, :], both[:, :], ALU.mult))
                dve.wait_ge(before_ready, 1)
                link(nc.vector.tensor_copy(total[:, :].rearrange("p (h c) -> p h c", h=2), total_ps[:, :, 0:H]))
                link(nc.vector.tensor_tensor_scan(incl[:, :], total[:, :], zeros[:, :], 0.0, ALU.add, ALU.add))
                link(nc.vector.tensor_tensor(pos[:, :], incl[:, :], total[:, :], ALU.subtract))
                link(nc.vector.tensor_tensor(pos[:, :].rearrange("p (h c) -> p h c", h=2), pos[:, :].rearrange("p (h c) -> p h c", h=2),
                                             before_ps[:, :, 0:H], ALU.add))
                link(nc.vector.scalar_tensor_tensor(pos[:, :], pos[:, :], 1.0 - OUT_OF_BOUNDS, active[:, :], ALU.add, ALU.mult))
                link(nc.vector.tensor_scalar(pos[:, :], pos[:, :], float(OUT_OF_BOUNDS), None, ALU.add))
                link(nc.vector.tensor_scalar(nb_f[:, :], incl[:, T - 1:T], BATCH_UPDATES / 2 - 0.5, 1.0 / BATCH_UPDATES, ALU.add, ALU.mult))
                link(nc.vector.tensor_scalar(nb_f[:, :], nb_f[:, :], ROUND, None, ALU.add))
                link(nc.vector.tensor_scalar(nb_f[:, :], nb_f[:, :], -ROUND, 2.0, ALU.add, ALU.max))
                link(nc.vector.tensor_copy(k.batches[:, :], nb_f[:, :]))

            @block.tensor
            def _(pe):
                pe.wait_ge(count_ready, 1)
                for h in range(2):
                    nc.tensor.matmul(before_ps[:, h, 0:H], k.upper[:, :], count[:, h * H:(h + 1) * H], start=True, stop=True)
                    last = nc.tensor.matmul(total_ps[:, h, 0:H], k.ones[:, :], count[:, h * H:(h + 1) * H], start=True, stop=True)
                last.then_inc(before_ready, 1)


SCATTER_UNROLL = 17


class RecordScatter:

    def __init__(self, sb, sem, name, first, last):
        self.first, self.last = first, last
        self.rec = sb(name + "_rec", [P, SCATTER_UNROLL, REC])
        self.pos = sb(name + "_pos", [P, SCATTER_UNROLL], I32)
        self.slots, self.settled = sem(name + "_slots"), sem(name + "_settled")
        self.scattered = [sem(f"{name}_scattered{r}") for r in range(SCATTER_UNROLL)]


def act_records(nc, act, k, s):
    U = SCATTER_UNROLL

    @rounds(act, s.last - s.first)
    def _(i):
        for u in range(U):
            act.wait_ge(s.scattered[u], i * 16)
            nc.scalar.copy(s.rec[:, u, :], k.rec[:, bass.ds(i * U + (u + s.first * U), 1), :].rearrange("p o f -> p (o f)"))
            nc.scalar.copy(s.pos[:, u:u + 1], col(k.rec_pos, i * U + (u + s.first * U))).then_inc(s.slots, 1)


def pool_records(nc, pool, k, s):
    U = SCATTER_UNROLL

    @rounds(pool, s.last - s.first)
    def _(i):
        for u in range(U):
            pool.wait_ge(s.slots, i * U + (u + 1))
            settle(pool, s.settled)
            pool.indirect_dma_start(out=k.rot_list, out_offset=bass.IndirectOffsetOnAxis(ap=s.pos[:, u:u + 1], axis=0),
                                    in_=s.rec[:, u, :], in_offset=None,
                                    bounds_check=ROT_ROWS - 1, oob_is_err=False).then_inc(s.scattered[u], 16)


def wait_records(pool, s):
    for u in range(SCATTER_UNROLL):
        pool.wait_ge(s.scattered[u], 16 * (s.last - s.first))


def rotation_matrix(nc, k):
    with phase(nc) as (sb, ps, sem):
        LEVELS = P.bit_length() - 1
        B = BATCH
        rec_in, sec_in = sb("rm_rec_in", [P, B, 4]), sb("rm_sec_in", [P, B, 5])
        rec, gate = sb("rm_rec", [P, B, 4]), sb("rm_gate", [P, B])
        second = sb("rm_second", [P, B])
        iota = sb("rm_iota", [P, D])
        masks = sb("rm_masks", [P, LEVELS + 3, P])
        edge = sb("rm_edge", [P, 2])
        diag, keep, l1, l2 = (sb("rm_" + n, [P, B, P]) for n in ("diag", "keep", "l1", "l2"))
        lt, t, tt, x = (sb("rm_" + n, [P, B, P]) for n in ("lt", "t", "tt", "x"))
        e, f, f1 = sb("rm_e", [P, B, D]), sb("rm_f", [P, B, D]), sb("rm_f1", [P, B, D])
        v, vt, y = sb("rm_v", [P, B, D]), sb("rm_vt", [P, B, D]), sb("rm_y", [P, 2, D])
        m = sb("rm_m", [P, 2, D])
        lx_ps, lt_ps = ps("rm_lx_ps", [P, B, P]), ps("rm_lt_ps", [P, B, P])
        d_ps = [ps(f"rm_d_ps{i}", [P, B, P]) for i in range(2)]
        v_ps = [ps(f"rm_v_ps{i}", [P, 2, D]) for i in range(2)]
        y_ps, u_ps = ps("rm_y_ps", [P, D]), ps("rm_u_ps", [P, 2, D])
        loaded, ready, chain_s, rec_loaded, taken = (sem("rm_" + n) for n in ("loaded", "ready", "chain", "rec_loaded", "taken"))
        diag_ready, row_made, l_ready, lt_made, lt_ready = (sem("rm_" + n) for n in (
            "diag_ready", "row_made", "l_ready", "lt_made", "lt_ready"))
        t_ready, x_made, x_ready, d_made, f_ready = (sem("rm_" + n) for n in ("t_ready", "x_made", "x_ready", "d_made", "f_ready"))
        v_made, v_ready, vt_made, vt_ready = (sem("rm_" + n) for n in ("v_made", "v_ready", "vt_made", "vt_ready"))
        y_made, y_ready, u_made, m_ready, m_turned = (sem("rm_" + n) for n in (
            "y_made", "y_ready", "u_made", "m_ready", "m_turned"))
        flat = lambda a: a[:, :, :].rearrange("p b s -> p (b s)")
        spread = lambda a: a.unsqueeze(1).to_broadcast([P, B, P])
        CHAINED = 9 + B

        def batches(eng):
            return eng.value_load(k.batches[0:1, 0:1], min_val=2, max_val=MAX_BATCHES)

        with nc.Block() as block:
            @block.sync
            def _(sp):
                sp.dma_start(masks[:, :, :], k.rot_masks).then_inc(loaded, 16)
                sp.dma_start(edge[:, :], k.rot_edge).then_inc(loaded, 16)

                @rounds(sp, batches(sp))
                def _(i):
                    sp.wait_ge(taken, i)
                    for c in range(B):
                        at = i * BATCH_UPDATES + c * (P - 1)
                        sp.dma_start(rec_in[:, c, :], k.rot_list[bass.ds(at + 1, P), 0:4]).then_inc(rec_loaded, 16)
                        sp.dma_start(sec_in[:, c, :], k.rot_list[bass.ds(at, P), 4:REC]).then_inc(rec_loaded, 16)
                sp.wait_ge(loaded, 32)

            @block.gpsimd
            def _(pool):
                nc.gpsimd.iota(iota[:, :], [[1, D]], base=0, channel_multiplier=0, allow_small_or_imprecise_dtypes=True).then_inc(ready, 1)
                nc.gpsimd.memset(m[:, :, :], 0.0).then_inc(ready, 1)
                pool.wait_ge(ready, 2)
                for h in range(2):
                    nc.gpsimd.affine_select(out=m[:, h, :], in_=m[:, h, :], compare_op=ALU.not_equal, fill=1.0,
                                            base=h * P, pattern=[[-1, D]], channel_multiplier=1).then_inc(ready, 1)

            @block.vector
            def _(dve):
                dve.wait_ge(ready, 4)
                dve.wait_ge(loaded, 32)
                nc.vector.memset(gate[:, :], 0.0).then_inc(m_ready, B + 1)
                link = Chain(dve, chain_s)
                of = lambda c, n: rec[:, c, n:n + 1]

                def add_update(c, done):
                    dve.wait_ge(u_made, done + 1)
                    dve.wait_ge(m_ready, done + 1)
                    nc.vector.tensor_tensor(m[:, :, :], m[:, :, :], u_ps[:, :, :], ALU.add).then_inc(m_ready, 1)

                @rounds(dve, batches(dve))
                def _(i):
                    link.loop(i, CHAINED, 0)
                    dve.wait_ge(rec_loaded, i * (32 * B) + 32 * B)
                    link(nc.vector.tensor_tensor(rec[:, :, :], rec_in[:, :, :], sec_in[:, :, 0:4], ALU.add))
                    link(nc.vector.tensor_copy(second[:, :], sec_in[:, :, 4]))
                    nc.vector.tensor_scalar(gate[:, :], second[:, :], edge[:, 1:2], edge[:, 0:1], ALU.mult, ALU.add).then_inc(taken, 1)
                    dve.wait_ge(taken, i + 1)
                    for c in range(B):
                        last = nc.vector.tensor_scalar(diag[:, c, :], k.ident[:, :], of(c, 0), None, ALU.mult)
                    last.then_inc(diag_ready, 1)
                    link(nc.vector.tensor_tensor(rec[:, :, 2:4], rec[:, :, 2:4], gate[:, :].unsqueeze(2).to_broadcast([P, B, 2]), ALU.mult))
                    for c in range(B):
                        last = nc.vector.scalar_tensor_tensor(keep[:, c, :], masks[:, LEVELS + 2, :], second[:, c:c + 1],
                                                              masks[:, LEVELS + 1, :], ALU.mult, ALU.add)
                    link(last)
                    dve.wait_ge(row_made, i + 1)
                    for c in range(B):
                        nc.vector.tensor_scalar(l1[:, c, :], lx_ps[:, c, :], of(c, 0), of(c, 2), ALU.is_equal, ALU.mult)
                        last = nc.vector.tensor_scalar(l2[:, c, :], lx_ps[:, c, :], of(c, 1), of(c, 3), ALU.is_equal, ALU.mult)
                    link(last)
                    link(nc.vector.tensor_tensor(flat(l1), flat(l1), flat(l2), ALU.add))
                    nc.vector.tensor_tensor(flat(l1), flat(l1), flat(keep), ALU.mult).then_inc(l_ready, 1)
                    dve.wait_ge(l_ready, i + 1)
                    link(nc.vector.tensor_tensor(t[:, :, :], l1[:, :, :], spread(masks[:, 0, :]), ALU.mult))
                    link(nc.vector.tensor_tensor(t[:, :, :], t[:, :, :], spread(k.ident[:, :]), ALU.add))
                    dve.wait_ge(lt_ready, i + 1)
                    link(nc.vector.tensor_tensor(tt[:, :, :], lt[:, :, :], spread(masks[:, LEVELS, :]), ALU.mult))
                    nc.vector.tensor_tensor(tt[:, :, :], tt[:, :, :], spread(k.ident[:, :]), ALU.add).then_inc(t_ready, 1)
                    for n in range(1, LEVELS):
                        dve.wait_ge(x_made, i * (LEVELS - 1) + n)
                        nc.vector.tensor_tensor(x[:, :, :], lx_ps[:, :, :], spread(masks[:, n, :]), ALU.mult).then_inc(x_ready, 1)
                        if n <= B:
                            c = n - 1
                            nc.vector.tensor_scalar(f1[:, c, :], iota[:, :], of(c, 0), of(c, 2), ALU.is_equal, ALU.mult)
                            link(nc.vector.tensor_scalar(f[:, c, :], iota[:, :], of(c, 1), of(c, 3), ALU.is_equal, ALU.mult))
                        dve.wait_ge(d_made, i * (LEVELS - 1) + n)
                        dve.wait_ge(t_ready, i * LEVELS + n)
                        if n < LEVELS - 1:
                            nc.vector.tensor_tensor(flat(t), flat(t), flat(d_ps[0]), ALU.add)
                        nc.vector.tensor_tensor(flat(tt), flat(tt), flat(d_ps[1]), ALU.add).then_inc(t_ready, 1)
                        if n <= B:
                            if not (isinstance(i, int) and i == 0):
                                add_update(c, i * B + c)
                            nc.vector.tensor_tensor(f[:, c, :], f[:, c, :], f1[:, c, :], ALU.add)
                            nc.vector.tensor_scalar(e[:, c, :], iota[:, :], of(c, 0), None, ALU.is_equal).then_inc(f_ready, 1)

                n = batches(dve)
                for c in range(B):
                    add_update(c, n * B + c)
                dve.wait_ge(m_turned, 1)
                for q in range(2):
                    last = nc.vector.tensor_copy(k.rot_t[:, q, :], v_ps[q][:, 0, :])
                last.then_inc(m_turned, 1)

            @block.scalar
            def _(act):
                def copy_y(c, done):
                    act.wait_ge(y_made, done + 1)
                    nc.scalar.copy(y[:, c % 2, :], y_ps[:, :]).then_inc(y_ready, 1)

                act.sem_inc(y_ready, B)
                act.sem_inc(vt_ready, 1)

                @rounds(act, batches(act))
                def _(i):
                    act.wait_ge(lt_made, i + 1)
                    nc.scalar.copy(flat(lt), flat(lt_ps)).then_inc(lt_ready, 1)
                    if not (isinstance(i, int) and i == 0):
                        for c in range(B):
                            copy_y(c, i * B + c)
                    for h in range(2):
                        act.wait_ge(v_made, i * 2 + (h + 1))
                        nc.scalar.copy(v[:, 2 * h:2 * h + 2, :], v_ps[h][:, :, :]).then_inc(v_ready, 1)
                    for h in range(2):
                        act.wait_ge(vt_made, i * 2 + (h + 1))
                        nc.scalar.copy(vt[:, 2 * h:2 * h + 2, :].rearrange("p c d -> p (c d)"), flat(d_ps[h])).then_inc(vt_ready, 1)

                n = batches(act)
                for c in range(B):
                    copy_y(c, n * B + c)

            @block.tensor
            def _(pe):
                def make_y(c, done):
                    pe.wait_ge(m_ready, done + 1)
                    for h in range(2):
                        last = nc.tensor.matmul(y_ps[:, :], vt[:, c, h * P:(h + 1) * P], m[:, h, :], start=(h == 0), stop=(h == 1))
                    last.then_inc(y_made, 1)

                def make_u(c, done):
                    pe.wait_ge(y_ready, done + 1)
                    for h in range(2):
                        last = nc.tensor.matmul(u_ps[:, h, :], e[:, c, h * P:(h + 1) * P], y[:, c % 2, :], start=True, stop=True)
                    last.then_inc(u_made, 1)

                pe.sem_inc(y_made, B)
                pe.sem_inc(u_made, B)
                pe.wait_ge(ready, 4)
                n_batches = batches(pe)

                @rounds(pe, n_batches)
                def _(i):
                    apply_before = not (isinstance(i, int) and i == 0)
                    pe.wait_ge(diag_ready, i + 1)
                    for c in range(B):
                        last = nc.tensor.matmul(lx_ps[:, c, :], k.ones[:, :], diag[:, c, :], start=True, stop=True)
                    last.then_inc(row_made, 1)
                    pe.wait_ge(l_ready, i + 1)
                    for c in range(B):
                        last = nc.tensor.transpose(lt_ps[:, c, :], l1[:, c, :], k.ident[:, :])
                    last.then_inc(lt_made, 1)
                    if apply_before:
                        pe.wait_ge(vt_ready, i * 2 + 1)
                        make_y(0, i * B)
                    for n in range(1, LEVELS):
                        c = n - 1
                        pe.wait_ge(t_ready, i * LEVELS + n)
                        for b in range(B):
                            last = nc.tensor.matmul(lx_ps[:, b, :], lt[:, b, :], t[:, b, :], start=True, stop=True)
                        last.then_inc(x_made, 1)
                        if apply_before and c < B:
                            make_u(c, i * B + c)
                        pe.wait_ge(x_ready, i * (LEVELS - 1) + n)
                        for b in range(B):
                            if n < LEVELS - 1:
                                nc.tensor.matmul(d_ps[0][:, b, :], tt[:, b, :], x[:, b, :], start=True, stop=True)
                            last = nc.tensor.matmul(d_ps[1][:, b, :], x[:, b, :], tt[:, b, :], start=True, stop=True)
                        last.then_inc(d_made, 1)
                        if apply_before and c + 1 < B:
                            make_y(c + 1, i * B + (c + 1))
                    pe.wait_ge(t_ready, i * LEVELS + LEVELS)
                    pe.wait_ge(f_ready, i * B + B)
                    for c in range(B):
                        last = nc.tensor.matmul(v_ps[c // 2][:, c % 2, :], tt[:, c, :], f[:, c, :], start=True, stop=True)
                        if c % 2 == 1:
                            last.then_inc(v_made, 1)
                    for c in range(B):
                        if c % 2 == 0:
                            pe.wait_ge(v_ready, i * 2 + (c // 2 + 1))
                        for h in range(2):
                            last = nc.tensor.transpose(d_ps[c // 2][:, 2 * (c % 2) + h, :], v[:, c, h * P:(h + 1) * P], k.ident[:, :])
                        if c % 2 == 1:
                            last.then_inc(vt_made, 1)

                pe.wait_ge(vt_ready, n_batches * 2 + 1)
                for c in range(B):
                    make_y(c, n_batches * B + c)
                    make_u(c, n_batches * B + c)
                pe.wait_ge(m_ready, n_batches * B + (B + 1))
                for q in range(2):
                    for h in range(2):
                        last = nc.tensor.transpose(v_ps[q][:, 0, h * P:(h + 1) * P], m[:, h, q * P:(q + 1) * P], k.ident[:, :])
                last.then_inc(m_turned, 1)


def build_program(nc, k):
    with ExitStack() as c:
        persistent(nc, c, k)
        constants(nc, k)
        with (nc.sbuf_tensor("rec", [P, EDGE_TILES, REC], F32) as k.rec,
              nc.sbuf_tensor("rec_pos", [P, EDGE_TILES], F32) as k.rec_pos,
              nc.sbuf_tensor("place", [P, STEP_COLS], F32) as k.place):
            rotation_records(nc, k)
            node_counts_and_sort(nc, k)
            step_lists(nc, k)
        rotation_matrix(nc, k)
        k.acc2 = c.enter_context(nc.sbuf_tensor("sums", [P, (NODE_TILES + 1) * 2 * D], F32))
        k.acc, k.spare = k.acc2[:, 0:(NODE_TILES + 1) * D], k.acc2[:, (NODE_TILES + 1) * D:]
        with nc.sbuf_tensor("node_tab", [P, (NODE_TILES + 1) * D], F32) as k.node_tab:
            node_phase_0(nc, k)
            pass_0(nc, k)
            node_phase_1(nc, k)
            cutoffs(nc, k)
            pass_1(nc, k)
            node_phase_2(nc, k)
            pass_2(nc, k)
        node_phase_3(nc, k)
        pass_3(nc, k)
        node_phase_4(nc, k)


def _rotation_masks():
    place = np.arange(P)
    s, t = place[:, None], place[None, :]
    levels = P.bit_length() - 1
    out = np.zeros((P, levels + 3, P), np.float32)
    for n in range(levels):
        out[:, n, :] = ((s >> n) % 2 == 1) & (t >> n == (s >> n) - 1)
    out[:, levels, :] = out[:, 0, :].T
    out[:, levels + 1, :] = t < s
    out[:, levels + 2, :] = t == s - 1
    return out


def _rotation_edge():
    out = np.zeros((P, 2), np.float32)
    out[:P - 1, 0] = 1
    out[0, 1], out[P - 1, 1] = 1, -1
    return out


def kernel(x, src, dst, edge_attr_256, edge_attr_64, edge_weight, L0_gnn_W, L1_gnn_ln_g, L1_gnn_ln_b, L1_gnn_Wq,
           L1_gnn_bq, L1_gnn_Wk, L1_gnn_bk, L1_gnn_Wv, L1_gnn_bv, L1_gnn_Wo, L1_gnn_bo, L1_gnn_Wdk, L1_gnn_bdk,
           L1_gnn_Wdv, L1_gnn_bdv, L2_gnn_queries, L2_gnn_influence_weights, L2_gnn_W_fwd, L2_gnn_b_fwd,
           L2_gnn_W_back, L2_gnn_b_back, L2_gnn_ln_w, L2_gnn_ln_b):
    import concourse.bacc as bacc
    from concourse.bass_utils import run_bass_kernel_spmd

    def padded(a, rows, fill):
        a = np.asarray(a)
        out = np.full((rows,) + a.shape[1:], fill, a.dtype)
        out[:len(a)] = a
        return out

    row = lambda a: np.asarray(a).reshape(1, -1)
    t = lambda a: np.asarray(a).T
    rows = lambda a, fill: padded(a, STEP_COLS * P, fill).reshape(STEP_COLS, P)
    ordered = dict(src=rows(src, PAD_NODE), dst=rows(dst, PAD_NODE), w=rows(edge_weight, 0))
    arrays = {n + "_rows": a for n, a in ordered.items()} | {n + "_cols": a.T for n, a in ordered.items()}
    back = t(L2_gnn_W_back)
    arrays |= dict(
        x=padded(x, NODES_PAD, 0),
        e256=padded(edge_attr_256, EDGES_PAD, 0),
        ea_t=np.concatenate([padded(edge_attr_64, EDGES_PAD, 0).T, np.ones((1, EDGES_PAD), np.float32)], 0),
        w0=L0_gnn_W, ln1_g=L1_gnn_ln_g, ln1_b=L1_gnn_ln_b, bo=row(L1_gnn_bo), wo=t(L1_gnn_Wo),
        wkvq=np.concatenate([t(L1_gnn_Wk), t(L1_gnn_Wv), t(L1_gnn_Wq)], 1),
        bkvq=np.concatenate([row(L1_gnn_bk), row(L1_gnn_bv), row(L1_gnn_bq)], 1),
        wd=np.concatenate([np.concatenate([t(L1_gnn_Wdk), t(L1_gnn_Wdv)], 1),
                           np.concatenate([row(L1_gnn_bdk), row(L1_gnn_bdv)], 1)], 0),
        wf=t(L2_gnn_W_fwd), bf=row(L2_gnn_b_fwd),
        wb=np.concatenate([back[D:], back[:D]], 0), bb=row(L2_gnn_b_back),
        ln2_w=row(L2_gnn_ln_w), ln2_b=row(L2_gnn_ln_b),
        rot_masks=_rotation_masks(), rot_edge=_rotation_edge())
    arrays = {n: np.ascontiguousarray(a) for n, a in arrays.items()}

    nc = bacc.Bacc("TRN2", target_bir_lowering=False, num_devices=1)
    k = Kernel()
    for name, a in arrays.items():
        setattr(k, name, nc.dram_tensor("in_" + name, a.shape, mybir.dt.from_np(a.dtype), kind="ExternalInput").ap())
    scratch = dict(tab_y=(NODES_PAD, D), tab_kv=(NODES_PAD, 2 * D), tab_x=(NODES_PAD, D), tab_x2=(NODES_PAD, D),
                   tab_h=(NODES_PAD, D), tab_f=(NODES_PAD, D), tab_sorted=(EDGES_PAD, SORT_ROW),
                   place_rows=(STEP_COLS, P), walk_n128=(1, STEPS), rot_list=(ROT_ROWS, REC))
    for name, shape in scratch.items():
        setattr(k, name, nc.dram_tensor(name, shape, F32).ap())
    k.walk_lists = nc.dram_tensor("walk_lists", (2, STEP_COLS), I32).ap()
    k.out = nc.dram_tensor("out", (NODES_PAD, D), F32, kind="ExternalOutput").ap()
    build_program(nc, k)
    result = run_bass_kernel_spmd(nc, [{"in_" + n: a for n, a in arrays.items()}], core_ids=[0])
    return result.results[0]["out"][:NODES]
```

```python
from contextlib import ExitStack, contextmanager

import numpy as np
import concourse.bass as bass
from concourse import mybir

F32, I32, BF16 = mybir.dt.float32, mybir.dt.int32, mybir.dt.bfloat16
ALU = mybir.AluOpType
ACT = mybir.ActivationFunctionType
AX = mybir.AxisListType

P = 128
NODES, EDGES, D, R = 6250, 100000, 256, 64
NODE_TILES = -(-NODES // P)
NODES_PAD = NODE_TILES * P
PAD_NODE = NODES_PAD - 1
EDGE_TILES = -(-EDGES // P)
EDGES_PAD = EDGE_TILES * P
ROW_BLOCKS = 7
STEPS = 832
STEP_COLS = ROW_BLOCKS * P
GROUP = 7
GROUPS = NODE_TILES // GROUP
HALF = STEPS // 2
EPS = 1e-5
BATCH = 4
BATCH_UPDATES = BATCH * (P - 1)
MAX_BATCHES = -(-2 * EDGES_PAD // BATCH_UPDATES)
STEPS_BESIDE_BATCH = 52
BATCHES_BESIDE = STEPS // STEPS_BESIDE_BATCH
REC = 9
ROT_PIECE = 49
ROT_ROWS = -(-(MAX_BATCHES * BATCH_UPDATES + 2) // (P * ROT_PIECE)) * P * ROT_PIECE
SCATTER_ROUNDS = 38
SORT_ROW = 516
OUT_OF_BOUNDS = 1 << 20
TWO_PI = 6.283185307179586
TWO_PI_HI = 6.28125
TWO_PI_LO = TWO_PI - TWO_PI_HI
ROUND = 12582912.0
SIN_MAX = 3.1415925
CUTOFF = 5.0


class Chain:

    def __init__(self, eng, sem):
        self.eng, self.sem, self.n = eng, sem, 0

    def __call__(self, ins):
        self.n = self.n + 1
        ins.then_inc(self.sem, 1)
        self.eng.wait_ge(self.sem, self.n)

    def loop(self, i, per, first):
        self.n = i * per + first


def settle(eng, sem):
    eng.sem_inc(sem, 1)


def rounds(eng, n):
    def run(body):
        body(0)
        with eng.Fori(1, n) as i:
            body(i)
    return run


def col(ap, c, n=1):
    return ap[:, bass.ds(c, n)]


PACK, PACK_BITS = 4, 6


def tile_words(eng, words):
    held = [None]

    def entry(base, e, fresh=False):
        if e % PACK == 0 or fresh:
            held[0] = eng.value_load(words[0:1, bass.ds((base + e // PACK * PACK) // PACK, 1)], min_val=0,
                                     max_val=(1 << PACK * PACK_BITS) - 1)
        tile = (held[0] >> (PACK_BITS * (e % PACK))) & ((1 << PACK_BITS) - 1)
        return tile if isinstance(tile, int) else tile.with_bounds(min_val=0, max_val=NODE_TILES)
    return entry


@contextmanager
def phase(nc):
    with ExitStack() as c:
        sems = []

        def sem(name):
            sems.append(nc.alloc_semaphore(name))
            return sems[-1]

        yield (lambda n, s, d=F32: c.enter_context(nc.sbuf_tensor(n, s, d)),
               lambda n, s, d=F32: c.enter_context(nc.psum_tensor(n, s, d)), sem)
    nc.clear_and_free_semaphores(sems)
    nc.all_engine_barrier()


def constants(nc, k):
    with phase(nc) as (sb, ps, sem), nc.Block() as block:
        s_z, s_id = sem("const_zero"), sem("const_done")

        @block.gpsimd
        def _(pool):
            nc.gpsimd.memset(k.ident[:, :], 0.0).then_inc(s_z, 1)
            nc.gpsimd.memset(k.ones[:, :], 1.0).then_inc(s_z, 1)
            nc.gpsimd.iota(k.iota[:, :], [[1, P]], base=0, channel_multiplier=0, allow_small_or_imprecise_dtypes=True).then_inc(s_z, 1)
            pool.wait_ge(s_z, 3)
            nc.gpsimd.affine_select(out=k.ident[:, :], in_=k.ident[:, :], compare_op=ALU.not_equal, fill=1.0,
                                    base=0, pattern=[[-1, P]], channel_multiplier=1).then_inc(s_id, 1)
            nc.gpsimd.affine_select(out=k.upper[:, :], in_=k.ones[:, :], compare_op=ALU.is_gt, fill=0.0,
                                    base=0, pattern=[[1, P]], channel_multiplier=-1).then_inc(s_id, 1)
            pool.wait_ge(s_id, 2)


def node_counts_and_sort(nc, k):
    with phase(nc) as (sb, ps, sem):
        TB = 17
        NB = EDGE_TILES // TB
        raw = sb("cs_raw", [P, 2, EDGE_TILES], I32)
        low_i = sb("cs_low_i", [P, 2, EDGE_TILES], I32)
        high_i = sb("cs_high_i", [P, 2, EDGE_TILES], I32)
        low = sb("cs_low", [P, 2, EDGE_TILES], F32)
        high = sb("cs_high", [P, 2, EDGE_TILES], F32)
        ohl = sb("cs_ohl", [P, 2, TB, P], BF16)
        ohh = sb("cs_ohh", [P, 2, TB, NODE_TILES], BF16)
        zb = sb("cs_zb", [P, P], BF16)
        degs = sb("cs_degs", [NODE_TILES, 2, P], F32)
        eq = sb("cs_eq", [P, EDGE_TILES], F32)
        zeros = sb("cs_zeros", [P, EDGE_TILES], F32)
        scan = sb("cs_scan", [P, EDGE_TILES], F32)
        tmp = sb("cs_tmp", [P, EDGE_TILES], F32)
        rank = sb("cs_rank", [P, EDGE_TILES], F32)
        tot = sb("cs_tot", [P, 64], F32)
        end = sb("cs_end", [P, 64], F32)
        off = sb("cs_off", [P, 64], F32)
        deg_ps = ps("cs_deg", [P, 2, P], F32)
        t_ps = ps("cs_t", [P, 2, P], F32)
        o_ps = ps("cs_o", [P, 64], F32)
        tt_ps = ps("cs_tt", [P, 64], F32)
        loaded, chain_s = sem("cs_loaded"), sem("cs_chain")
        ohl_rdy, ohh_rdy, counted, zdone = sem("cs_ohl_rdy"), sem("cs_ohh_rdy"), sem("cs_counted"), sem("cs_zero")
        degs_copied, transposed, split = sem("cs_degcopied"), sem("cs_transposed"), sem("cs_split")
        tot_rdy, off_rdy, highs_rdy = sem("cs_tot_rdy"), sem("cs_off_rdy"), sem("cs_highs")
        records = RecordScatter(sb, sem, "cs_records", 0, SCATTER_ROUNDS)
        with nc.Block() as block:
            @block.scalar
            def _(act):
                act_records(nc, act, k, records)

            @block.gpsimd
            def _(pool):
                pool_records(nc, pool, k, records)
                wait_records(pool, records)

            @block.sync
            def _(sp):
                sp.dma_start(raw[:, 0, :], k.dst_cols[:, 0:EDGE_TILES]).then_inc(loaded, 16)
                sp.dma_start(raw[:, 1, :], k.src_cols[:, 0:EDGE_TILES]).then_inc(loaded, 16)
                sp.wait_ge(loaded, 32)

            @block.vector
            def _(dve):
                link = Chain(dve, chain_s)
                dve.wait_ge(loaded, 32)
                link(nc.vector.tensor_scalar(low_i[:, :, :], raw[:, :, :], 127, None, ALU.bitwise_and))
                link(nc.vector.tensor_scalar(high_i[:, :, :], raw[:, :, :], 7, None, ALU.arith_shift_right))
                nc.vector.memset(zb[:, :], 0.0).then_inc(zdone, 1)
                link(nc.vector.tensor_copy(low[:, :, :], low_i[:, :, :]))
                nc.vector.tensor_copy(high[:, :, :], high_i[:, :, :]).then_inc(highs_rdy, 1)
                dve.wait_ge(highs_rdy, 1)
                for a in range(2):
                    @rounds(dve, NB // 2)
                    def _(i):
                        for u in range(2):
                            dve.wait_ge(counted, i * 2 + (u + a * NB + 1))
                            nc.vector.tensor_tensor(
                                ohl[:, u, :, :],
                                k.iota[:, :].unsqueeze(1).to_broadcast([P, TB, P]),
                                low[:, a, bass.ds((i * 2 + u) * TB, TB)].unsqueeze(2).to_broadcast([P, TB, P]),
                                ALU.is_equal).then_inc(ohl_rdy, 1)
                            nc.vector.tensor_tensor(
                                ohh[:, u, :, :],
                                k.iota[:, 0:NODE_TILES].unsqueeze(1).to_broadcast([P, TB, NODE_TILES]),
                                high[:, a, bass.ds((i * 2 + u) * TB, TB)].unsqueeze(2).to_broadcast([P, TB, NODE_TILES]),
                                ALU.is_equal).then_inc(ohh_rdy, 1)
                dve.wait_ge(counted, 2 * NB + 2)
                nc.vector.tensor_copy(degs[:, :, :], deg_ps[0:NODE_TILES, :, :]).then_inc(degs_copied, 1)
                dve.wait_ge(transposed, 2)
                nc.vector.tensor_copy(k.cnt[:, :, :], t_ps[:, :, 0:NODE_TILES]).then_inc(split, 1)
                dve.wait_ge(highs_rdy, 1)
                link(nc.vector.memset(zeros[:, :], 0.0))
                link(nc.vector.memset(rank[:, :], 0.0))
                link(nc.vector.memset(k.place[:, EDGE_TILES:STEP_COLS], 0.0))
                base = link.n
                @rounds(dve, NODE_TILES)
                def _(h):
                    link.loop(h, 5, base)
                    hcol = col(k.iota, h)
                    link(nc.vector.tensor_scalar(eq[:, :], high[:, 1, :], hcol, None, ALU.is_equal))
                    link(nc.vector.tensor_tensor_scan(scan[:, :], eq[:, :], zeros[:, :], 0.0, ALU.add, ALU.add))
                    link(nc.vector.tensor_tensor(tmp[:, :], eq[:, :], scan[:, :], ALU.mult))
                    link(nc.vector.tensor_copy(col(tot, h), scan[:, EDGE_TILES - 1:EDGE_TILES]))
                    link(nc.vector.tensor_tensor(rank[:, :], rank[:, :], tmp[:, :], ALU.add))
                link.n = base + 5 * NODE_TILES
                nc.vector.tensor_scalar(tmp[:, 0:1], tot[:, 0:1], 0.0, None, ALU.mult).then_inc(tot_rdy, 1)
                dve.wait_ge(off_rdy, 1)
                link(nc.vector.tensor_tensor_scan(end[:, 0:NODE_TILES], tt_ps[:, 0:NODE_TILES], zeros[:, 0:NODE_TILES],
                                                  0.0, ALU.add, ALU.add))
                link(nc.vector.tensor_copy(k.bucket_end[:, :], end[:, 0:NODE_TILES]))
                link(nc.vector.tensor_tensor(off[:, 0:NODE_TILES], end[:, 0:NODE_TILES], tt_ps[:, 0:NODE_TILES], ALU.subtract))
                link(nc.vector.tensor_tensor(off[:, 0:NODE_TILES], off[:, 0:NODE_TILES], o_ps[:, 0:NODE_TILES], ALU.add))
                link(nc.vector.tensor_scalar(off[:, 0:NODE_TILES], off[:, 0:NODE_TILES], -1.0, None, ALU.add))
                base = link.n
                @rounds(dve, NODE_TILES)
                def _(h):
                    link.loop(h, 2, base)
                    link(nc.vector.tensor_scalar(eq[:, :], high[:, 1, :], col(k.iota, h), col(off, h), ALU.is_equal, ALU.mult))
                    link(nc.vector.tensor_tensor(rank[:, :], rank[:, :], eq[:, :], ALU.add))
                link.n = base + 2 * NODE_TILES
                link(nc.vector.tensor_copy(k.place[:, 0:EDGE_TILES], rank[:, :]))

            @block.tensor
            def _(pe):
                pe.wait_ge(zdone, 1)
                nc.tensor.matmul(deg_ps[0:NODE_TILES, :, :], zb[:, 0:NODE_TILES],
                                 zb[:, :].unsqueeze(1).to_broadcast([P, 2, P]), start=True, stop=True).then_inc(counted, 2)
                for a in range(2):
                    @rounds(pe, NB // 2)
                    def _(i):
                        for u in range(2):
                            pe.wait_ge(ohl_rdy, i * 2 + (u + a * NB + 1))
                            pe.wait_ge(ohh_rdy, i * 2 + (u + a * NB + 1))
                            for t in range(TB):
                                last = nc.tensor.matmul(deg_ps[0:NODE_TILES, a, :], ohh[:, u, t, :], ohl[:, u, t, :],
                                                        start=False, stop=True, skip_group_check=True)
                            last.then_inc(counted, 1)
                pe.wait_ge(degs_copied, 1)
                for a in range(2):
                    nc.tensor.transpose(t_ps[:, a, 0:NODE_TILES], degs[:, a, :], k.ident[0:NODE_TILES, 0:NODE_TILES]).then_inc(transposed, 1)
                pe.wait_ge(tot_rdy, 1)
                nc.tensor.matmul(o_ps[:, 0:NODE_TILES], k.upper[:, :], tot[:, 0:NODE_TILES], start=True, stop=True)
                nc.tensor.matmul(tt_ps[:, 0:NODE_TILES], k.ones[:, :], tot[:, 0:NODE_TILES], start=True, stop=True).then_inc(off_rdy, 1)


def step_lists(nc, k):
    with phase(nc) as (sb, ps, sem):
        B = ROW_BLOCKS
        ends_i = sb("sl_ends_i", [P, 3, B], I32)
        lo = sb("sl_lo", [P, 2, B], F32)
        hi = sb("sl_hi", [P, 2, B], F32)
        prev = sb("sl_prev", [P, 2, B], F32)
        cnt = sb("sl_cnt", [P, 2, B], F32)
        start = sb("sl_start", [P, 2, B], F32)
        tot = sb("sl_tot", [P, 2, B], F32)
        inc = sb("sl_inc", [P, 2, B], F32)
        zero = sb("sl_zero", [P, B], F32)
        wgt = sb("sl_wgt", [P, 2, B, 2], F32)
        pos = sb("sl_pos", [P, 3, B], F32)
        cmp49 = sb("sl_cmp49", [P, NODE_TILES], F32)
        kk = sb("sl_kk", [P, STEP_COLS], F32)
        valid = sb("sl_valid", [P, B], F32)
        tidx = sb("sl_tidx", [P, B], F32)
        cmp = sb("sl_cmp", [P, 2, B, STEPS], F32)
        row = sb("sl_row", [1, 2, 2, STEPS], F32)
        krow = sb("sl_krow", [1, STEPS], F32)
        kcol = sb("sl_kcol", [P, B], F32)
        colv = sb("sl_colv", [P, B, 2], F32)
        e_idx = sb("sl_e_idx", [P, B], I32)
        n128 = sb("sl_n128", [P, B], F32)
        n_row = sb("sl_n_row", [1, STEPS], F32)
        e_list2, tile_words2 = sb("sl_e_list2", [1, STEP_COLS], I32), sb("sl_tile_words2", [1, STEPS // PACK], I32)
        late, packed = sb("sl_late", [1, STEP_COLS]), sb("sl_packed", [1, STEP_COLS // PACK])
        rows_i = sb("sl_rows_i", [P, 2, B, P], I32)
        rows_w = sb("sl_rows_w", [P, B, P], F32)
        rows_f = sb("sl_rows_f", [P, 2, B, P], F32)
        m_ps = ps("sl_m", [P, 2, 2, B], F32)
        r_ps = ps("sl_r", [1, 2, 512], F32)
        c_ps = ps("sl_c", [P, B, 2], F32)
        x_ps = ps("sl_x", [P, 2, 512], F32)
        place_t = sb("sl_place_t", [P, B, P], F32)
        rows_p = sb("sl_rows_p", [P, B, P], F32)
        inside = sb("sl_inside", [P, B, P], F32)
        pt_rdy, pt_free, place_out = sem("sl_pt_rdy"), sem("sl_pt_free"), sem("sl_place_out")
        loaded, chain_s, iota_s, memset_s = sem("sl_loaded"), sem("sl_chain"), sem("sl_iota"), sem("sl_memset")
        cnt_rdy, summed, cmp_rdy, row_ps_rdy, row_free = sem("sl_cnt_rdy"), sem("sl_summed"), sem("sl_cmp_rdy"), sem("sl_row_ps"), sem("sl_row_free")
        col_rdy, n_rdy, walk_out, idx_rdy = sem("sl_col_rdy"), sem("sl_n_rdy"), sem("sl_walk_out"), sem("sl_idx")
        gath, rows_rdy, x_rdy, x_free = sem("sl_gath"), sem("sl_rows_rdy"), sem("sl_x_rdy"), sem("sl_x_free")
        records = RecordScatter(sb, sem, "sl_records", SCATTER_ROUNDS, EDGE_TILES // SCATTER_UNROLL)
        with nc.Block() as block:
            @block.scalar
            def _(act):
                act_records(nc, act, k, records)

            @block.sync
            def _(sp):
                flat = k.dst_rows.rearrange("a e -> (a e)")
                last = k.dst_rows.rearrange("(b p) e -> p b e", p=P)
                with nc.allow_non_contiguous_dma(reason="the ends of edge tiles"):
                    sp.dma_start(ends_i[:, 0, :].unsqueeze(2), last[:, :, 0:1]).then_inc(loaded, 16)
                    sp.dma_start(ends_i[:, 1, :].unsqueeze(2), last[:, :, P - 1:P]).then_inc(loaded, 16)
                    sp.wait_ge(memset_s, 1)
                    sp.dma_start(ends_i[1:P, 2, 0:1], k.dst_rows[0:P - 1, P - 1:P]).then_inc(loaded, 16)
                    for b in range(1, B):
                        sp.dma_start(ends_i[:, 2, b:b + 1], k.dst_rows[b * P - 1:b * P + P - 1, P - 1:P]).then_inc(loaded, 16)
                sp.wait_ge(loaded, 16 * (B + 2))
                sp.wait_ge(pt_free, B)
                sp.dma_start(k.place_rows.rearrange("(b p) e -> p b e", p=P), place_t[:, :, :]).then_inc(place_out, 16)
                sp.wait_ge(n_rdy, 1)
                sp.dma_start(k.walk_lists[0:1, :], e_list2[:, :]).then_inc(walk_out, 16)
                sp.dma_start(k.walk_lists[1:2, 0:STEPS // PACK], tile_words2[:, :]).then_inc(walk_out, 16)
                sp.dma_start(k.walk_n128, n_row[:, :]).then_inc(walk_out, 16)
                sp.wait_ge(walk_out, 48)
                sp.wait_ge(place_out, 16)

            @block.gpsimd
            def _(pool):
                kw = dict(allow_small_or_imprecise_dtypes=True)
                nc.gpsimd.memset(ends_i[:, 2, :], -P).then_inc(memset_s, 1)
                nc.gpsimd.iota(kk[:, :], [[1, STEP_COLS]], base=0, channel_multiplier=0, **kw).then_inc(iota_s, 1)
                nc.gpsimd.iota(krow[:, :], [[1, STEPS]], base=0, channel_multiplier=0, **kw).then_inc(iota_s, 1)
                nc.gpsimd.iota(kcol[:, :], [[P, B]], base=0, channel_multiplier=1, **kw).then_inc(iota_s, 1)
                for n, b0 in enumerate((0, P - 1, -1)):
                    nc.gpsimd.iota(pos[:, n, :], [[P * P, B]], base=b0, channel_multiplier=P, **kw).then_inc(iota_s, 1)
                nc.gpsimd.iota(tidx[:, :], [[P, B]], base=0, channel_multiplier=1, **kw).then_inc(iota_s, 1)
                pool_records(nc, pool, k, records)
                pool.wait_ge(idx_rdy, 1)
                pool.wait_ge(place_out, 16)
                for b in range(B):
                    pool.indirect_dma_start(out=rows_p[:, b, :], out_offset=None, in_=k.place_rows,
                                            in_offset=bass.IndirectOffsetOnAxis(ap=e_idx[:, b:b + 1], axis=0)).then_inc(gath, 16)
                    for n, rows in ((0, k.src_rows), (1, k.dst_rows)):
                        pool.indirect_dma_start(out=rows_i[:, n, b, :], out_offset=None, in_=rows,
                                                in_offset=bass.IndirectOffsetOnAxis(ap=e_idx[:, b:b + 1], axis=0)).then_inc(gath, 16)
                    pool.indirect_dma_start(out=rows_w[:, b, :], out_offset=None, in_=k.w_rows,
                                            in_offset=bass.IndirectOffsetOnAxis(ap=e_idx[:, b:b + 1], axis=0)).then_inc(gath, 16)
                pool.wait_ge(gath, 16 * 4 * B)
                wait_records(pool, records)

            @block.vector
            def _(dve):
                link = Chain(dve, chain_s)
                for b in range(B):
                    dve.wait_ge(pt_rdy, b + 1)
                    nc.vector.tensor_copy(place_t[:, b, :], x_ps[:, b % 2, 0:P]).then_inc(pt_free, 1)
                dve.wait_ge(loaded, 16 * (B + 2))
                dve.wait_ge(iota_s, 7)
                link(nc.vector.memset(zero[:, :], 0.0))
                link(nc.vector.tensor_scalar(ends_i[:, :, :], ends_i[:, :, :], 7, None, ALU.arith_shift_right))
                link(nc.vector.tensor_copy(lo[:, 0, :], ends_i[:, 0, :]))
                link(nc.vector.tensor_copy(hi[:, 0, :], ends_i[:, 1, :]))
                link(nc.vector.tensor_copy(prev[:, 0, :], ends_i[:, 2, :]))
                for n, out in enumerate((lo, hi, prev)):
                    for b in range(B):
                        link(nc.vector.tensor_scalar(cmp49[:, :], k.bucket_end[:, :], pos[:, n, b:b + 1], None, ALU.is_le))
                        link(nc.vector.tensor_reduce(out[:, 1, b:b + 1], cmp49[:, :], AX.X, ALU.add))
                link(nc.vector.memset(prev[0:1, 1, 0:1], -1.0))
                link(nc.vector.tensor_scalar(valid[:, :], tidx[:, :], float(EDGE_TILES) - 0.5, None, ALU.is_lt))
                link(nc.vector.tensor_tensor(cnt[:, :, :], hi[:, :, :], lo[:, :, :], ALU.subtract))
                nc.vector.tensor_scalar(cnt[:, :, :], cnt[:, :, :], 1.0, None, ALU.add).then_inc(cnt_rdy, 1)
                dve.wait_ge(summed, 1)
                for w in range(2):
                    link(nc.vector.tensor_tensor_scan(inc[:, w, :], m_ps[:, 1, w, :], zero[:, :], 0.0, ALU.add, ALU.add))
                link(nc.vector.tensor_tensor(tot[:, :, :], inc[:, :, :], m_ps[:, 1, :, :], ALU.subtract))
                link(nc.vector.tensor_tensor(start[:, :, :], tot[:, :, :], m_ps[:, 0, :, :], ALU.add))
                for w in range(2):
                    link(nc.vector.tensor_tensor(inc[:, w, :], lo[:, w, :], prev[:, w, :], ALU.subtract))
                    link(nc.vector.tensor_scalar(inc[:, w, :], inc[:, w, :], -1.0, None, ALU.add))
                    link(nc.vector.tensor_tensor(wgt[:, w, :, 1], inc[:, w, :], valid[:, :], ALU.mult))
                    link(nc.vector.tensor_copy(wgt[:, w, :, 0], valid[:, :]))
                    for b in range(B):
                        link(nc.vector.tensor_scalar(cmp[:, w, b, :], kk[:, 0:STEPS], start[:, w, b:b + 1], None, ALU.is_ge))
                    nc.vector.tensor_scalar(cmp49[:, 0:1], kk[:, 0:1], 0.0, None, ALU.mult).then_inc(cmp_rdy, 1)
                    dve.wait_ge(cmp_rdy, w + 1)
                for w in range(2):
                    for f in range(2):
                        dve.wait_ge(row_ps_rdy, 2 * w + f + 1)
                        nc.vector.tensor_copy(row[0:1, w, f, :].rearrange("p (h c) -> p h c", h=2),
                                              r_ps[0:1, :, 0:HALF]).then_inc(row_free, 1)
                        dve.wait_ge(row_free, 2 * w + f + 1)
                    link(nc.vector.tensor_scalar(row[0:1, w, 0, :], row[0:1, w, 0, :], -1.0, None, ALU.add))
                    link(nc.vector.tensor_tensor(row[0:1, w, 1, :], row[0:1, w, 1, :], krow[0:1, :], ALU.add))
                    link(nc.vector.tensor_scalar(row[0:1, w, 1, :], row[0:1, w, 1, :], float(NODE_TILES), None, ALU.min))
                    e_list = k.e_list if w == 0 else e_list2
                    link(nc.vector.tensor_copy(e_list[0:1, 0:STEPS], row[0:1, w, 0, :]))
                    link(nc.vector.memset(e_list[0:1, STEPS:STEP_COLS], EDGE_TILES - 1))
                    link(nc.vector.memset(late[0:1, :], float(NODE_TILES)))
                    link(nc.vector.tensor_copy(late[0:1, 1:STEPS + 1], row[0:1, w, 1, :]))
                    for words, entries in ((k.tile_words if w == 0 else tile_words2, row[0:1, w, 1, :]), (k.late_words, late[0:1, :])):
                        if w == 1 and words is k.late_words:
                            continue
                        entries = entries.rearrange("p (n q) -> p n q", q=PACK)
                        count = entries.shape[1]
                        link(nc.vector.tensor_copy(packed[0:1, 0:count], entries[:, :, PACK - 1]))
                        for q in range(PACK - 2, -1, -1):
                            link(nc.vector.scalar_tensor_tensor(packed[0:1, 0:count], packed[0:1, 0:count], float(1 << PACK_BITS),
                                                                entries[:, :, q], ALU.mult, ALU.add))
                        link(nc.vector.tensor_copy(words[0:1, 0:count], packed[0:1, 0:count]))
                nc.vector.tensor_scalar(n_row[0:1, :], row[0:1, 1, 1, :], float(P), None, ALU.mult).then_inc(n_rdy, 1)
                dve.wait_ge(col_rdy, 1)
                link(nc.vector.memset(colv[:, :, :], 0.0))
                link(nc.vector.memset(colv[:, B - 1, 0:1], float(EDGE_TILES)))
                link(nc.vector.tensor_copy(colv[:, 0:B - 1, :], c_ps[:, 0:B - 1, :]))
                link(nc.vector.tensor_copy(colv[0:STEPS - (B - 1) * P, B - 1, :], c_ps[0:STEPS - (B - 1) * P, B - 1, :]))
                link(nc.vector.tensor_scalar(colv[:, :, 0], colv[:, :, 0], -1.0, None, ALU.add))
                link(nc.vector.tensor_tensor(n128[:, :], colv[:, :, 1], kcol[:, :], ALU.add))
                link(nc.vector.tensor_scalar(n128[:, :], n128[:, :], float(P), None, ALU.mult))
                nc.vector.tensor_copy(e_idx[:, :], colv[:, :, 0]).then_inc(idx_rdy, 1)
                dve.wait_ge(gath, 16 * 4 * B)
                link(nc.vector.tensor_copy(rows_f[:, :, :, :], rows_i[:, :, :, :]))
                for b in range(B):
                    link(nc.vector.tensor_scalar(rows_f[:, 1, b, :], rows_f[:, 1, b, :], n128[:, b:b + 1], None, ALU.subtract))
                link(nc.vector.tensor_scalar(inside[:, :, :], rows_f[:, 1, :, :], 0.0, None, ALU.is_ge))
                link(nc.vector.scalar_tensor_tensor(inside[:, :, :], rows_f[:, 1, :, :], P - 0.5, inside[:, :, :], ALU.is_lt, ALU.mult))
                link(nc.vector.scalar_tensor_tensor(rows_p[:, :, :], rows_p[:, :, :], -float(OUT_OF_BOUNDS), inside[:, :, :], ALU.add, ALU.mult))
                nc.vector.tensor_scalar(rows_p[:, :, :], rows_p[:, :, :], float(OUT_OF_BOUNDS), None, ALU.add).then_inc(rows_rdy, 1)
                m = 0
                for b in range(B):
                    for dest in (k.step_src, k.step_rel, k.step_w, k.step_place):
                        m += 1
                        dve.wait_ge(x_rdy, m)
                        nc.vector.tensor_copy(dest[:, b * P:(b + 1) * P], x_ps[:, m % 2, 0:P]).then_inc(x_free, 1)
                dve.wait_ge(x_free, m)

            @block.tensor
            def _(pe):
                for b in range(B):
                    if b >= 2:
                        pe.wait_ge(pt_free, b - 1)
                    nc.tensor.transpose(x_ps[:, b % 2, 0:P], k.place[:, b * P:(b + 1) * P], k.ident[:, :]).then_inc(pt_rdy, 1)
                pe.wait_ge(cnt_rdy, 1)
                nc.tensor.matmul(m_ps[:, 0, :, :], k.upper[:, :], cnt[:, :, :], start=True, stop=True)
                nc.tensor.matmul(m_ps[:, 1, :, :], k.ones[:, :], cnt[:, :, :], start=True, stop=True).then_inc(summed, 1)
                for w in range(2):
                    pe.wait_ge(cmp_rdy, w + 1)
                    for f in range(2):
                        if w or f:
                            pe.wait_ge(row_free, 2 * w + f)
                        for h in range(2):
                            for b in range(B):
                                last = nc.tensor.matmul(r_ps[0:1, h, 0:HALF], wgt[:, w, b, f:f + 1],
                                                        cmp[:, w, b, h * HALF:(h + 1) * HALF], start=(b == 0), stop=(b == B - 1))
                        last.then_inc(row_ps_rdy, 1)
                for q in range(B):
                    m = min(P, STEPS - q * P)
                    for b in range(B):
                        last = nc.tensor.matmul(c_ps[0:m, q, :], cmp[:, 0, b, q * P:q * P + m], wgt[:, 0, b, :],
                                                start=(b == 0), stop=(b == B - 1))
                last.then_inc(col_rdy, 1)
                pe.wait_ge(rows_rdy, 1)
                m = 0
                for b in range(B):
                    for src in (rows_f[:, 0, b, :], rows_f[:, 1, b, :], rows_w[:, b, :], rows_p[:, b, :]):
                        m += 1
                        if m > 2:
                            pe.wait_ge(x_free, m - 2)
                        else:
                            pe.wait_ge(pt_free, B)
                        nc.tensor.transpose(x_ps[:, m % 2, 0:P], src, k.ident[:, :]).then_inc(x_rdy, 1)


class Kernel:
    pass


def persistent(nc, c, k):
    sb = lambda n, s, d: c.enter_context(nc.sbuf_tensor(n, s, d))
    k.ident = sb("ident", [P, P], F32)
    k.iota = sb("iota", [P, P], F32)
    k.ones = sb("ones", [P, P], F32)
    k.upper = sb("upper", [P, P], F32)
    k.cnt = sb("cnt", [P, 2, NODE_TILES], F32)
    k.bucket_end = sb("bucket_end", [P, NODE_TILES], F32)
    k.e_list = sb("e_list", [1, STEP_COLS], I32)
    k.tile_words = sb("tile_words", [1, STEPS // PACK], I32)
    k.late_words = sb("late_words", [1, STEP_COLS // PACK], I32)
    k.step_src = sb("step_src", [P, STEP_COLS], I32)
    k.step_rel = sb("step_rel", [P, STEP_COLS], F32)
    k.step_w = sb("step_w", [P, STEP_COLS], F32)
    k.step_place = sb("step_place", [P, STEP_COLS], I32)
    k.batches = sb("batches", [P, 1], I32)
    k.dinv = sb("dinv", [P, NODE_TILES], F32)
    k.rot_t = sb("rot_t", [P, 2, D], F32)


class Project:

    def __init__(self, sem, name):
        self.src_ready = sem(name + "_src_ready")
        self.turned = sem(name + "_turned")
        self.copied = sem(name + "_copied")
        self.product = sem(name + "_product")
        self.used = sem(name + "_used")


def pe_project(nc, pe, k, g, s, src, parts, turned_ps, turned_sb, outs):
    def turn(u):
        if u == 0:
            pe.wait_ge(s.src_ready, g + 1)
        pe.wait_ge(s.copied, g * GROUP + max(u - 1, 0))
        for q in range(parts):
            last = nc.tensor.transpose(turned_ps[:, u % 2, q * P:(q + 1) * P], src[:, u, q * P:(q + 1) * P], k.ident[:, :])
        last.then_inc(s.turned, 1)

    def multiply(u):
        pe.wait_ge(s.copied, g * GROUP + (u + 1))
        pe.wait_ge(s.used, g * GROUP + (max(u - 1, 0) if outs[0][0].shape[1] == 2 else 0))
        for out, w in outs:
            width = w.shape[-1]
            for q in range(parts):
                last = nc.tensor.matmul(out[:, u % out.shape[1], 0:width], turned_sb[:, u % 2, q * P:(q + 1) * P], w[:, q, :],
                                        start=(q == 0), stop=(q == parts - 1))
        last.then_inc(s.product, 1)

    turn(0)
    for u in range(GROUP):
        if u + 1 < GROUP:
            turn(u + 1)
        multiply(u)


def act_project(nc, act, g, s, parts, turned_ps, turned_sb, scale=None, bias=None):
    for u in range(GROUP):
        act.wait_ge(s.turned, g * GROUP + (u + 1))
        act.wait_ge(s.product, g * GROUP + max(u - 1, 0))
        if scale is None:
            nc.scalar.copy(turned_sb[:, u % 2, 0:parts * P], turned_ps[:, u % 2, 0:parts * P]).then_inc(s.copied, 1)
        else:
            for q in range(parts):
                last = nc.scalar.activation(turned_sb[:, u % 2, q * P:(q + 1) * P], turned_ps[:, u % 2, q * P:(q + 1) * P],
                                            ACT.Identity, scale=scale[:, q:q + 1], bias=bias[:, q:q + 1])
            last.then_inc(s.copied, 1)


def dve_norm(nc, dve, link, g, n, per_group, sb, x, out):
    for u in range(GROUP):
        last = nc.vector.bn_stats(sb.stats[:, u, :], x[:, u, :])
    link(last)
    settle(dve, sb.settled)
    for u in range(GROUP):
        nc.vector.bn_aggr(sb.mv[:, u, :], sb.stats[:, u, :]).then_inc(sb.aggregated, 1)
    dve.wait_ge(sb.aggregated, (g * per_group + (n + 1)) * GROUP)
    nc.vector.tensor_scalar(sb.var[:, :], sb.mv[:, :, 1], EPS, None, ALU.add).then_inc(sb.var_ready, 1)
    dve.wait_ge(sb.root_ready, g * per_group + (n + 1))
    link(nc.vector.reciprocal(sb.rstd[:, :], sb.root[:, :]))
    for u in range(GROUP):
        last = nc.vector.tensor_scalar(out[:, u, :], x[:, u, :], sb.mv[:, u, 0:1], sb.rstd[:, u:u + 1], ALU.subtract, ALU.mult)
    link(last)


NORM_LINKS = 3


def act_root(nc, act, g, n, per_group, sb):
    act.wait_ge(sb.var_ready, g * per_group + (n + 1))
    nc.scalar.activation(sb.root[:, :], sb.var[:, :], ACT.Sqrt).then_inc(sb.root_ready, 1)


def norm_buffers(sb, sem, name):
    b = Kernel()
    b.stats = sb(name + "_stats", [P, GROUP, 6], F32)
    b.mv = sb(name + "_mv", [P, GROUP, 2], F32)
    b.var = sb(name + "_var", [P, GROUP], F32)
    b.root = sb(name + "_root", [P, GROUP], F32)
    b.rstd = sb(name + "_rstd", [P, GROUP], F32)
    b.aggregated, b.settled = sem(name + "_aggregated"), sem(name + "_settled")
    b.var_ready, b.root_ready = sem(name + "_var_ready"), sem(name + "_root_ready")
    return b


def tiles(ap):
    return ap.rearrange("(n p) d -> p n d", p=P)


def node_phase_0(nc, k):
    with phase(nc) as (sb, ps, sem):
        xg, yg = sb("n0_x", [P, GROUP, D]), sb("n0_y", [P, GROUP, D])
        h = sb("n0_h", [P, GROUP, D])
        root49, mask49 = sb("n0_droot", [P, NODE_TILES]), sb("n0_mask", [P, NODE_TILES])
        nb = norm_buffers(sb, sem, "n0")
        loaded, consumed, made, stored = sem("n0_loaded"), sem("n0_consumed"), sem("n0_made"), sem("n0_stored")
        chain_s, deg_ready, deg_root = sem("n0_chain"), sem("n0_deg_ready"), sem("n0_deg_root")
        with nc.Block() as block:
            @block.sync
            def _(sp):
                @rounds(sp, GROUPS)
                def _(g):
                    sp.wait_ge(consumed, g)
                    sp.dma_start(xg[:, :, :], tiles(k.x)[:, bass.ds(g * GROUP, GROUP), :]).then_inc(loaded, 16)
                    sp.wait_ge(made, g + 1)
                    sp.dma_start(tiles(k.tab_y)[:, bass.ds(g * GROUP, GROUP), :], yg[:, :, :]).then_inc(stored, 16)
                sp.wait_ge(stored, 16 * GROUPS)

            @block.scalar
            def _(act):
                act.wait_ge(deg_ready, 1)
                nc.scalar.activation(root49[:, :], k.dinv[:, :], ACT.Sqrt).then_inc(deg_root, 1)
                @rounds(act, GROUPS)
                def _(g):
                    act_root(nc, act, g, 0, 1, nb)

            @block.vector
            def _(dve):
                link = Chain(dve, chain_s)
                link(nc.vector.tensor_scalar(mask49[:, :], k.cnt[:, 0, :], 0.0, None, ALU.is_gt))
                nc.vector.tensor_scalar(k.dinv[:, :], k.cnt[:, 0, :], 1.0, None, ALU.max).then_inc(deg_ready, 1)
                dve.wait_ge(deg_root, 1)
                link(nc.vector.reciprocal(k.dinv[:, :], root49[:, :]))
                link(nc.vector.tensor_tensor(k.dinv[:, :], k.dinv[:, :], mask49[:, :], ALU.mult))
                base, per = link.n, NORM_LINKS
                @rounds(dve, GROUPS)
                def _(g):
                    link.loop(g, per, base)
                    dve.wait_ge(loaded, g * 16 + 16)
                    dve_norm(nc, dve, link, g, 0, 1, nb, xg, h)
                    dve.wait_ge(stored, g * 16)
                    for u in range(GROUP):
                        last = nc.vector.tensor_scalar(yg[:, u, :], h[:, u, :], 0.0, col(k.dinv, g * GROUP + u), ALU.max, ALU.mult)
                    last.then_inc(made, 1)
                    nc.vector.tensor_scalar(nb.var[:, 0:1], nb.rstd[:, 0:1], 0.0, None, ALU.mult).then_inc(consumed, 1)


def node_phase_1(nc, k):
    with phase(nc) as (sb, ps, sem):
        part = GROUP * D
        xg, ag, h, z = (k.spare[:, n * part:(n + 1) * part].rearrange("p (n d) -> p n d", d=D) for n in range(4))
        kv = k.spare[:, 4 * part:6 * part].rearrange("p (n d) -> p n d", d=2 * D)
        w0 = sb("n1_w0", [P, 2, D])
        wkvq = sb("n1_wkvq", [P, 2, 3 * D])
        bkvq = sb("n1_bkvq", [P, 3 * D])
        bo = sb("n1_bo", [P, D])
        lng, lnb = sb("n1_lng", [P, 2]), sb("n1_lnb", [P, 2])
        turned_sb = sb("n1_turned", [P, 2, D])
        zt_sb = sb("n1_zt", [P, 2, D])
        turned_ps = ps("n1_turned_ps", [P, 2, 512])
        out_ps = ps("n1_out_ps", [P, 2, 512])
        q_ps = ps("n1_q_ps", [P, 2, 512])
        pa, pb = Project(sem, "n1a"), Project(sem, "n1b")
        nb = norm_buffers(sb, sem, "n1")
        weights, loaded, consumed, stored, chain_s = sem("n1_weights"), sem("n1_loaded"), sem("n1_consumed"), sem("n1_stored"), sem("n1_chain")
        z_psum_free = sem("n1_z_psum_free")
        NW = 7
        with nc.Block() as block:
            @block.sync
            def _(sp):
                sp.dma_start(w0[:, :, :], k.w0.rearrange("(q p) n -> p q n", p=P)).then_inc(weights, 16)
                sp.dma_start(wkvq[:, :, :], k.wkvq.rearrange("(q p) n -> p q n", p=P)).then_inc(weights, 16)
                sp.dma_start(bkvq[:, :], k.bkvq.to_broadcast([P, 3 * D])).then_inc(weights, 16)
                sp.dma_start(bo[:, :], k.bo.to_broadcast([P, D])).then_inc(weights, 16)
                with nc.allow_non_contiguous_dma(reason="small vectors"):
                    sp.dma_start(lng[:, :].unsqueeze(2), k.ln1_g.rearrange("(q p o) -> p q o", p=P, o=1)).then_inc(weights, 16)
                    sp.dma_start(lnb[:, :].unsqueeze(2), k.ln1_b.rearrange("(q p o) -> p q o", p=P, o=1)).then_inc(weights, 16)
                @rounds(sp, GROUPS)
                def _(g):
                    sp.wait_ge(stored, g * 32)
                    sp.dma_start(xg[:, :, :], tiles(k.x)[:, bass.ds(g * GROUP, GROUP), :]).then_inc(loaded, 16)
                    sp.wait_ge(pb.used, g * GROUP + GROUP)
                    sp.dma_start(tiles(k.tab_x)[:, bass.ds(g * GROUP, GROUP), :], xg[:, :, :]).then_inc(stored, 16)
                    sp.dma_start(tiles(k.tab_kv)[:, bass.ds(g * GROUP, GROUP), :], kv[:, :, :]).then_inc(stored, 16)
                sp.wait_ge(stored, 32 * GROUPS)

            @block.scalar
            def _(act):
                act.wait_ge(weights, 16 * 6)
                @rounds(act, GROUPS)
                def _(g):
                    act.wait_ge(pa.product, g * GROUP)
                    nc.scalar.copy(ag[:, :, :], k.acc[:, bass.ds(g * (GROUP * D), GROUP * D)].rearrange("p (n d) -> p n d", d=D)
                                   ).then_inc(pa.src_ready, 1)
                    act_project(nc, act, g, pa, 2, turned_ps, turned_sb)
                    act_root(nc, act, g, 0, 2, nb)
                    act_root(nc, act, g, 1, 2, nb)
                    act_project(nc, act, g, pb, 2, turned_ps, zt_sb, lng, lnb)

            @block.vector
            def _(dve):
                link = Chain(dve, chain_s)
                dve.wait_ge(weights, 16 * 6)
                nc.vector.memset(k.node_tab[:, NODE_TILES * D:], 0.0)
                base, per = link.n, 2 * NORM_LINKS + 3
                @rounds(dve, GROUPS)
                def _(g):
                    link.loop(g, per, base)
                    dve.wait_ge(loaded, g * 16 + 16)
                    for u in range(GROUP):
                        dve.wait_ge(pa.product, g * GROUP + (u + 1))
                        nc.vector.scalar_tensor_tensor(xg[:, u, :], out_ps[:, u % 2, 0:D], col(k.dinv, g * GROUP + u), xg[:, u, :],
                                                       ALU.mult, ALU.add).then_inc(pa.used, 1)
                    dve.wait_ge(pa.used, g * GROUP + GROUP)
                    dve_norm(nc, dve, link, g, 0, 2, nb, xg, h)
                    link(nc.vector.tensor_scalar(h[:, :, :], h[:, :, :], 0.0, None, ALU.max))
                    dve_norm(nc, dve, link, g, 1, 2, nb, h, z)
                    link(nc.vector.tensor_tensor(xg[:, :, :], xg[:, :, :], h[:, :, :], ALU.add))
                    link(nc.vector.tensor_tensor(xg[:, :, :], xg[:, :, :], bo[:, :].unsqueeze(1).to_broadcast([P, GROUP, D]), ALU.add))
                    nc.vector.tensor_scalar(nb.var[:, 0:1], nb.rstd[:, 0:1], 0.0, None, ALU.mult).then_inc(pb.src_ready, 1)
                    for u in range(GROUP):
                        dve.wait_ge(pb.product, g * GROUP + (u + 1))
                        dve.wait_ge(stored, g * 32)
                        nc.vector.tensor_tensor(kv[:, u, :], out_ps[:, u % 2, :], bkvq[:, 0:2 * D], ALU.add)
                        nc.vector.tensor_tensor(k.node_tab[:, bass.ds(g * (GROUP * D) + u * D, D)], q_ps[:, u % 2, 0:D],
                                                bkvq[:, 2 * D:3 * D], ALU.add).then_inc(pb.used, 1)

            @block.tensor
            def _(pe):
                pe.wait_ge(weights, 16 * 6)
                @rounds(pe, GROUPS)
                def _(g):
                    pe.wait_ge(pb.copied, g * GROUP)
                    pe.wait_ge(pb.used, g * GROUP)
                    pe_project(nc, pe, k, g, pa, ag, 2, turned_ps, turned_sb, [(out_ps, w0)])
                    pe.wait_ge(pa.used, g * GROUP + GROUP)
                    pe_project(nc, pe, k, g, pb, z, 2, turned_ps, zt_sb, [(out_ps, wkvq[:, :, 0:2 * D]), (q_ps, wkvq[:, :, 2 * D:3 * D])])


def reduce_angle(nc, link, out, turns, x, scale, shift):
    link(nc.vector.tensor_scalar(out, x, scale, shift, ALU.mult, ALU.add))
    link(nc.vector.tensor_scalar(turns, out, 1.0 / TWO_PI, ROUND, ALU.mult, ALU.add))
    link(nc.vector.tensor_scalar(turns, turns, -ROUND, None, ALU.add))
    link(nc.vector.scalar_tensor_tensor(out, turns, -TWO_PI_HI, out, ALU.mult, ALU.add))
    link(nc.vector.scalar_tensor_tensor(out, turns, -TWO_PI_LO, out, ALU.mult, ALU.add))
    link(nc.vector.tensor_scalar(out, out, SIN_MAX, -SIN_MAX, ALU.min, ALU.max))


def cutoffs(nc, k):
    with phase(nc) as (sb, ps, sem):
        ang, turns, cosv, mask = (sb("cut_" + n, [P, STEP_COLS]) for n in ("ang", "turns", "cos", "mask"))
        chain_s, ang_ready, cos_ready = sem("cut_chain"), sem("cut_ang_ready"), sem("cut_cos_ready")
        with nc.Block() as block:
            @block.vector
            def _(dve):
                link = Chain(dve, chain_s)
                reduce_angle(nc, link, ang[:, :], turns[:, :], k.step_w[:, :], float(np.pi / CUTOFF), float(np.pi / 2))
                nc.vector.tensor_scalar(mask[:, :], k.step_w[:, :], CUTOFF, 0.5, ALU.is_lt, ALU.mult).then_inc(ang_ready, 1)
                dve.wait_ge(cos_ready, 1)
                dve.wait_ge(ang_ready, 1)
                link(nc.vector.scalar_tensor_tensor(k.step_w[:, :], cosv[:, :], 1.0, mask[:, :], ALU.add, ALU.mult))

            @block.scalar
            def _(act):
                act.wait_ge(ang_ready, 1)
                nc.scalar.activation(cosv[:, :], ang[:, :], ACT.Sin).then_inc(cos_ready, 1)


def pass_1(nc, k):
    with phase(nc) as (sb, ps, sem):
        begun = sem("p1_begun")
        U, RING = 16, 8
        per = 16 * U // RING
        kv = k.spare[:, 0:RING * 2 * D].rearrange("p (r d) -> p r d", d=2 * D)
        ea = sb("p1_ea", [R + 1, RING, P])
        idx = sb("p1_idx", [P, U], I32)
        wd = sb("p1_wd", [R + 1, 2 * D])
        s_mat = sb("p1_s", [P, 8, P], BF16)
        ident = sb("p1_ident", [P, P], BF16)
        ident_ready = sem("p1_ident_ready")
        st_sb = sb("p1_st", [P, 2, P])
        dkv = sb("p1_dkv", [P, 4, 2 * D])
        qk, qkd = sb("p1_qk", [P, 2, D]), sb("p1_qkd", [P, 2, D])
        dots, acts, attn = sb("p1_dots", [P, 2]), sb("p1_acts", [P, 2]), sb("p1_attn", [P, 4])
        sa = sb("p1_sa", [P, 2, P])
        msg = sb("p1_msg", [P, 2, D])
        sq_ps = [ps(f"p1_sq{i}", [P, 512]) for i in range(4)]
        d_ps = [ps(f"p1_d{i}", [P, 512]) for i in range(2)]
        acc_ps = [ps(f"p1_acc{i}", [P, 512]) for i in range(2)]
        turned_ps = [bank[:, 0:P // 2].bitcast(BF16) for bank in sq_ps]
        gathered = [sem(f"p1_gathered{r}") for r in range(RING)]
        ea_loaded = [sem(f"p1_ea_loaded{r}") for r in range(RING)]
        weights, idx_ready, acc_zero = sem("p1_weights"), sem("p1_idx_ready"), sem("p1_acc_zero")
        s_ready, turned, st_ready = sem("p1_s_ready"), sem("p1_turned"), sem("p1_st_ready")
        d_made, silu_done, q_made, qk_done = sem("p1_d_made"), sem("p1_silu_done"), sem("p1_q_made"), sem("p1_qk_done")
        dot_done, act_done, attn_ready = sem("p1_dot_done"), sem("p1_act_done"), sem("p1_attn_ready")
        sa_ready = sem("p1_sa_ready")
        msg_ready, summed, added = sem("p1_msg_ready"), sem("p1_summed"), sem("p1_added")
        with nc.Block() as block:
            @block.sync
            def _(sp):
                sp.dma_start(wd[:, :], k.wd).then_inc(weights, 16)
                @rounds(sp, STEPS // U)
                def _(i):
                    for u in range(U):
                        e = sp.value_load(k.e_list[0:1, bass.ds(i * U + u, 1)], min_val=0, max_val=EDGE_TILES - 1)
                        sp.wait_ge(d_made, i * U + (u + 1))
                        sp.dma_start(ea[:, u % RING, :], k.ea_t[:, bass.ds(e * P, P)]).then_inc(ea_loaded[u % RING], 16)
                for r in range(RING):
                    sp.wait_ge(ea_loaded[r], 16 * STEPS // RING)

            @block.gpsimd
            def _(pool):
                @rounds(pool, STEPS // U)
                def _(i):
                    for u in range(U):
                        if u % RING == 0:
                            pool.wait_ge(msg_ready, i * U + u)
                            settle(pool, begun)
                            nc.gpsimd.tensor_copy(idx[:, u:u + RING], col(k.step_src, i * U + u, RING)).then_inc(idx_ready, 1)
                            pool.wait_ge(idx_ready, i * 2 + (u // RING + 1))
                        pool.wait_ge(msg_ready, i * U + (u + 1))
                        settle(pool, begun)
                        pool.indirect_dma_start(out=kv[:, u % RING, :], out_offset=None, in_=k.tab_kv,
                                                in_offset=bass.IndirectOffsetOnAxis(ap=idx[:, u:u + 1], axis=0)
                                                ).then_inc(gathered[u % RING], 16)

            @block.vector
            def _(dve):
                nc.vector.tensor_copy(ident[:, :], k.ident[:, :]).then_inc(ident_ready, 1)
                nc.vector.memset(msg[:, :, :], 0.0)
                nc.vector.memset(sa[:, :, :], 0.0)
                nc.vector.memset(k.acc[:, :], 0.0).then_inc(acc_zero, 1)
                dve.wait_ge(acc_zero, 1)
                dve.sem_inc(msg_ready, RING)
                dve.sem_inc(added, 1)
                late_tile = tile_words(dve, k.late_words)

                def one_hot(i, s):
                    nc.vector.tensor_scalar(s_mat[:, s % 8, :], k.iota[:, :], col(k.step_rel, i * U + s), None,
                                            ALU.is_equal).then_inc(s_ready, 1)

                def product(i, s):
                    dve.wait_ge(q_made, i * U + (s + 1))
                    dve.wait_ge(gathered[s % RING], i * per + 16 * (s // RING + 1))
                    nc.vector.tensor_tensor(qk[:, s % 2, :], sq_ps[s % 4][:, P:P + D], kv[:, s % RING, 0:D], ALU.mult).then_inc(qk_done, 1)

                def dot(i, s):
                    dve.wait_ge(silu_done, i * U + (s + 1))
                    dve.wait_ge(qk_done, i * U + (s + 1))
                    nc.vector.tensor_tensor_reduce(out=qkd[:, s % 2, :], in0=qk[:, s % 2, :], in1=dkv[:, s % 4, 0:D], scale=1.0, scalar=0.0,
                                                   op0=ALU.mult, op1=ALU.add, accum_out=dots[:, s % 2:s % 2 + 1]
                                                   ).then_inc(dot_done, 1)

                def steps(i, last=False):
                    for u in range(U):
                        ahead = lambda x: not last or u + x < U
                        n = late_tile(i * U, u)
                        if ahead(3):
                            one_hot(i, u + 3)
                        if ahead(1):
                            product(i, u + 1)
                        dve.wait_ge(summed, i * U + u)
                        nc.vector.tensor_tensor(msg[:, u % 2, :], kv[:, u % RING, D:2 * D], dkv[:, u % 4, D:2 * D], ALU.mult
                                                ).then_inc(msg_ready, 1)
                        if ahead(1):
                            dot(i, u + 1)
                        dve.wait_ge(summed, i * U + (u + 1))
                        dve.wait_ge(added, i * U + (u + 1))
                        nc.vector.tensor_tensor(k.acc[:, bass.ds(n * D, D)], k.acc[:, bass.ds(n * D, D)],
                                                acc_ps[(u + 1) % 2][:, 0:D], ALU.add).then_inc(added, 1)

                for s in range(3):
                    one_hot(0, s)
                product(0, 0)
                dot(0, 0)
                rounds(dve, STEPS // U - 1)(steps)
                steps(STEPS // U - 1, last=True)
                n = late_tile(STEPS, 0)
                dve.wait_ge(summed, STEPS + 1)
                dve.wait_ge(added, STEPS + 1)
                nc.vector.tensor_tensor(k.acc[:, bass.ds(n * D, D)], k.acc[:, bass.ds(n * D, D)], acc_ps[1][:, 0:D], ALU.add).then_inc(added, 1)
                dve.wait_ge(added, STEPS + 2)

            @block.scalar
            def _(act):
                def copy_turned(i, s):
                    act.wait_ge(turned, i * U + (s + 1))
                    nc.scalar.copy(st_sb[:, s % 2, :], turned_ps[s % 4]).then_inc(st_ready, 1)

                def silu(i, s):
                    act.wait_ge(d_made, i * U + (s + RING + 1))
                    act.wait_ge(msg_ready, i * U + (s + RING - 3))
                    nc.scalar.activation(dkv[:, s % 4, :], d_ps[s % 2][:, :], ACT.Silu).then_inc(silu_done, 1)

                def attention(i, s):
                    act.wait_ge(dot_done, i * U + (s + 1))
                    nc.scalar.activation(acts[:, s % 2:s % 2 + 1], dots[:, s % 2:s % 2 + 1], ACT.Silu).then_inc(act_done, 1)

                def weigh(i, s):
                    act.wait_ge(act_done, i * U + (s + 1))
                    nc.scalar.activation(attn[:, s % 4:s % 4 + 1], acts[:, s % 2:s % 2 + 1], ACT.Copy,
                                         scale=col(k.step_w, i * U + s)).then_inc(attn_ready, 1)

                def weigh_s(i, s):
                    act.wait_ge(attn_ready, i * U + (s + 1))
                    act.wait_ge(summed, i * U + s)
                    nc.scalar.activation(sa[:, s % 2, :], s_mat[:, s % 8, :], ACT.Copy, scale=attn[:, s % 4:s % 4 + 1]
                                         ).then_inc(sa_ready, 1)

                def steps(i, last=False):
                    for u in range(U):
                        for x, stage in ((1, attention), (3, copy_turned), (1, weigh), (2, silu), (1, weigh_s)):
                            if not last or u + x < U:
                                stage(i, u + x)

                act.wait_ge(acc_zero, 1)
                for s in range(3):
                    copy_turned(0, s)
                    if s < 2:
                        silu(0, s)
                for stage in (attention, weigh, weigh_s):
                    stage(0, 0)
                rounds(act, STEPS // U - 1)(steps)
                steps(STEPS // U - 1, last=True)

            @block.tensor
            def _(pe):
                own_tile = tile_words(pe, k.tile_words)

                def turn(i, s):
                    if not (isinstance(i, int) and i * U + s < 4):
                        pe.wait_ge(qk_done, i * U + (s - 3))
                    pe.wait_ge(s_ready, i * U + (s + 1))
                    nc.tensor.transpose(turned_ps[s % 4], s_mat[:, s % 8, :], ident[:, :]).then_inc(turned, 1)

                def make_d(i, s):
                    if not (isinstance(i, int) and i * U + s < 2):
                        pe.wait_ge(silu_done, i * U + (s - 1))
                    pe.wait_ge(ea_loaded[s % RING], i * per + 16 * (s // RING + 1))
                    nc.tensor.matmul(d_ps[s % 2][:, :], ea[:, s % RING, :], wd[:, :], start=True, stop=True).then_inc(d_made, 1)

                def make_q(i, s):
                    t = own_tile(i * U, s, fresh=s < 3)
                    pe.wait_ge(st_ready, i * U + (s + 1))
                    nc.tensor.matmul(sq_ps[s % 4][:, P:P + D], st_sb[:, s % 2, :], k.node_tab[:, bass.ds(t * D, D)],
                                     start=True, stop=True).then_inc(q_made, 1)

                def steps(i, last=False):
                    for u in range(U):
                        for x, stage in ((3, turn), (2, make_d), (2, make_q)):
                            if not last or u + x < U:
                                stage(i, u + x)
                        pe.wait_ge(added, i * U + (u + 1))
                        pe.wait_ge(msg_ready, i * U + (u + RING + 1))
                        pe.wait_ge(sa_ready, i * U + (u + 1))
                        nc.tensor.matmul(acc_ps[u % 2][:, 0:D], sa[:, u % 2, :], msg[:, u % 2, :], start=True, stop=True).then_inc(summed, 1)

                pe.wait_ge(weights, 16)
                pe.wait_ge(ident_ready, 1)
                pe.sem_inc(d_made, RING)
                pe.wait_ge(acc_zero, 1)
                nc.tensor.matmul(acc_ps[1][:, 0:D], sa[:, 1, :], msg[:, 1, :], start=True, stop=True).then_inc(summed, 1)
                for stage, s in ((turn, 0), (turn, 1), (make_d, 0), (make_q, 0), (turn, 2), (make_d, 1), (make_q, 1)):
                    stage(0, s)
                rounds(pe, STEPS // U - 1)(steps)
                steps(STEPS // U - 1, last=True)


def node_phase_2(nc, k):
    with phase(nc) as (sb, ps, sem):
        xg = sb("n2_x", [P, GROUP, D])
        ag = sb("n2_acc", [P, GROUP, D])
        h = sb("n2_h", [P, GROUP, D])
        wo = sb("n2_wo", [P, 2, D])
        turned_sb = sb("n2_turned", [P, 2, D])
        turned_ps, out_ps = ps("n2_turned_ps", [P, 2, 512]), ps("n2_out_ps", [P, 2, 512])
        pa = Project(sem, "n2a")
        nb = norm_buffers(sb, sem, "n2")
        weights, loaded, made, stored, chain_s = sem("n2_weights"), sem("n2_loaded"), sem("n2_made"), sem("n2_stored"), sem("n2_chain")
        with nc.Block() as block:
            @block.sync
            def _(sp):
                sp.dma_start(wo[:, :, :], k.wo.rearrange("(q p) n -> p q n", p=P)).then_inc(weights, 16)
                @rounds(sp, GROUPS)
                def _(g):
                    sp.wait_ge(stored, g * 32)
                    sp.dma_start(xg[:, :, :], tiles(k.tab_x)[:, bass.ds(g * GROUP, GROUP), :]).then_inc(loaded, 16)
                    sp.wait_ge(made, g + 1)
                    sp.dma_start(tiles(k.tab_x2)[:, bass.ds(g * GROUP, GROUP), :], xg[:, :, :]).then_inc(stored, 16)
                    sp.dma_start(tiles(k.tab_h)[:, bass.ds(g * GROUP, GROUP), :], h[:, :, :]).then_inc(stored, 16)
                sp.wait_ge(stored, 32 * GROUPS)

            @block.scalar
            def _(act):
                @rounds(act, GROUPS)
                def _(g):
                    act.wait_ge(pa.product, g * GROUP)
                    nc.scalar.copy(ag[:, :, :], k.acc[:, bass.ds(g * (GROUP * D), GROUP * D)].rearrange("p (n d) -> p n d", d=D)
                                   ).then_inc(pa.src_ready, 1)
                    act_project(nc, act, g, pa, 2, turned_ps, turned_sb)
                    act_root(nc, act, g, 0, 1, nb)

            @block.vector
            def _(dve):
                link = Chain(dve, chain_s)
                @rounds(dve, GROUPS)
                def _(g):
                    link.loop(g, NORM_LINKS + 1, 0)
                    dve.wait_ge(loaded, g * 16 + 16)
                    for u in range(GROUP):
                        dve.wait_ge(pa.product, g * GROUP + (u + 1))
                        nc.vector.tensor_tensor(xg[:, u, :], out_ps[:, u % 2, 0:D], xg[:, u, :], ALU.add).then_inc(pa.used, 1)
                    dve.wait_ge(pa.used, g * GROUP + GROUP)
                    dve_norm(nc, dve, link, g, 0, 1, nb, xg, h)
                    link(nc.vector.tensor_scalar(h[:, :, :], h[:, :, :], 0.0, None, ALU.max))
                    nc.vector.tensor_copy(k.node_tab[:, bass.ds(g * (GROUP * D), GROUP * D)].rearrange("p (n d) -> p n d", d=D),
                                          h[:, :, :]).then_inc(made, 1)

            @block.tensor
            def _(pe):
                pe.wait_ge(weights, 16)
                @rounds(pe, GROUPS)
                def _(g):
                    pe_project(nc, pe, k, g, pa, ag, 2, turned_ps, turned_sb, [(out_ps, wo)])


def pass_2(nc, k):
    with phase(nc) as (sb, ps, sem):
        begun = sem("p2_begun")
        U, RING, LEAD = 16, 8, 4
        SLOT = D + SORT_ROW
        slot = sb("p2_slot", [P, RING, SLOT])
        gidx, pidx = sb("p2_gidx", [P, U], I32), sb("p2_pidx", [P, U], I32)
        s_mat = sb("p2_s", [P, 4, P])
        st_sb = sb("p2_st", [P, 2, P])
        h_ps = [ps(f"p2_h{i}", [P, 512]) for i in range(2)]
        acc_ps = [ps(f"p2_acc{i}", [P, 512]) for i in range(2)]
        gathered = [sem(f"p2_gathered{r}") for r in range(RING)]
        e_loaded = [sem(f"p2_e_loaded{r}") for r in range(RING)]
        scattered = [sem(f"p2_scattered{r}") for r in range(RING)]
        gidx_ready, pidx_ready = sem("p2_gidx_ready"), sem("p2_pidx_ready")
        s_ready, turned, st_ready, h_made, h_copied = sem("p2_s_ready"), sem("p2_turned"), sem("p2_st_ready"), sem("p2_h_made"), sem("p2_h_copied")
        summed, added, zeroed = sem("p2_summed"), sem("p2_added"), sem("p2_zeroed")
        W = 2 * D
        per = 16 * U // RING
        with nc.Block() as block:
            @block.sync
            def _(sp):
                @rounds(sp, STEPS // U)
                def _(i):
                    for u in range(U):
                        r = u % RING
                        e = sp.value_load(k.e_list[0:1, bass.ds(i * U + u, 1)], min_val=0, max_val=EDGE_TILES - 1)
                        sp.wait_ge(scattered[r], i * per + 16 * (u // RING))
                        sp.dma_start(slot[:, r, D:2 * D], tiles(k.e256)[:, bass.ds(e, 1), :].rearrange("p o d -> p (o d)")
                                     ).then_inc(e_loaded[r], 16)
                for r in range(RING):
                    sp.wait_ge(e_loaded[r], 16 * STEPS // RING)

            @block.gpsimd
            def _(pool):
                def gather(s, count):
                    r = s % RING
                    pool.wait_ge(scattered[r], count)
                    settle(pool, begun)
                    pool.indirect_dma_start(out=slot[:, r, 0:D], out_offset=None, in_=k.tab_h,
                                            in_offset=bass.IndirectOffsetOnAxis(ap=gidx[:, s % U:s % U + 1], axis=0)
                                            ).then_inc(gathered[r], 16)

                nc.gpsimd.memset(slot[:, :, 3 * D:SLOT], 0.0).then_inc(zeroed, 1)
                nc.gpsimd.tensor_copy(gidx[:, 0:LEAD], k.step_src[:, 0:LEAD]).then_inc(gidx_ready, 1)
                pool.wait_ge(gidx_ready, 1)
                for u in range(LEAD):
                    gather(u, 0)

                @rounds(pool, STEPS // U)
                def _(i):
                    for u in range(U):
                        r = u % RING
                        if u % LEAD == 0:
                            q = (u + LEAD) % U
                            nc.gpsimd.tensor_copy(gidx[:, q:q + LEAD], col(k.step_src, i * U + (u + LEAD), LEAD)).then_inc(gidx_ready, 1)
                            nc.gpsimd.tensor_copy(pidx[:, u:u + LEAD], col(k.step_place, i * U + u, LEAD)).then_inc(pidx_ready, 1)
                            pool.wait_ge(gidx_ready, i * (U // LEAD) + (u // LEAD + 2))
                            pool.wait_ge(pidx_ready, i * (U // LEAD) + (u // LEAD + 1))
                        gather(u + LEAD, i * per + 16 * ((u + LEAD) // RING))
                        pool.wait_ge(h_copied, i * U + (u + 1))
                        pool.wait_ge(summed, i * U + (u + 1))
                        settle(pool, begun)
                        pool.indirect_dma_start(out=k.tab_sorted, out_offset=bass.IndirectOffsetOnAxis(ap=pidx[:, u:u + 1], axis=0),
                                                in_=slot[:, r, D:SLOT], in_offset=None,
                                                bounds_check=EDGES_PAD - 1, oob_is_err=False).then_inc(scattered[r], 16)
                for r in range(RING):
                    pool.wait_ge(scattered[r], 16 * STEPS // RING)
                    pool.wait_ge(gathered[r], 16 * STEPS // RING + (16 if r < LEAD else 0))

            @block.vector
            def _(dve):
                nc.vector.memset(k.acc2[:, :], 0.0).then_inc(added, 2)
                for u in range(2):
                    nc.vector.tensor_scalar(s_mat[:, u, :], k.iota[:, :], k.step_rel[:, u:u + 1], None, ALU.is_equal).then_inc(s_ready, 1)
                tile = tile_words(dve, k.tile_words)

                @rounds(dve, STEPS // U)
                def _(i):
                    for u in range(U):
                        n = tile(i * U, u)
                        nc.vector.tensor_scalar(s_mat[:, (u + 2) % 4, :], k.iota[:, :], col(k.step_rel, i * U + (u + 2)), None,
                                                ALU.is_equal).then_inc(s_ready, 1)
                        dve.wait_ge(summed, i * U + (u + 1))
                        dve.wait_ge(added, i * U + (u + 2))
                        nc.vector.tensor_tensor(k.acc2[:, bass.ds(n * W, W)], k.acc2[:, bass.ds(n * W, W)],
                                                acc_ps[u % 2][:, :], ALU.add).then_inc(added, 1)
                dve.wait_ge(added, STEPS + 2)

            @block.scalar
            def _(act):
                @rounds(act, STEPS // U)
                def _(i):
                    for u in range(U):
                        r = u % RING
                        act.wait_ge(turned, i * U + (u + 1))
                        nc.scalar.copy(st_sb[:, u % 2, :], h_ps[u % 2][:, 0:P]).then_inc(st_ready, 1)
                        act.wait_ge(scattered[r], i * per + 16 * (u // RING))
                        if u == 0:
                            act.wait_ge(zeroed, 1)
                        nc.scalar.copy(slot[:, r, 3 * D:3 * D + 1], col(k.step_src, i * U + u))
                        act.wait_ge(h_made, i * U + (u + 1))
                        nc.scalar.copy(slot[:, r, 2 * D:3 * D], h_ps[u % 2][:, P:P + D]).then_inc(h_copied, 1)

            @block.tensor
            def _(pe):
                def turn(s, n):
                    pe.wait_ge(s_ready, n + 1)
                    nc.tensor.transpose(h_ps[s % 2][:, 0:P], s_mat[:, s % 4, :], k.ident[:, :]).then_inc(turned, 1)

                tile = tile_words(pe, k.tile_words)
                turn(0, 0)

                @rounds(pe, STEPS // U)
                def _(i):
                    for u in range(U):
                        r = u % RING
                        t = tile(i * U, u)
                        pe.wait_ge(h_copied, i * U + u)
                        turn(u + 1, i * U + (u + 1))
                        pe.wait_ge(st_ready, i * U + (u + 1))
                        nc.tensor.matmul(h_ps[u % 2][:, P:P + D], st_sb[:, u % 2, :], k.node_tab[:, bass.ds(t * D, D)],
                                         start=True, stop=True).then_inc(h_made, 1)
                        pe.wait_ge(gathered[r], i * per + 16 * (u // RING + 1))
                        pe.wait_ge(e_loaded[r], i * per + 16 * (u // RING + 1))
                        pe.wait_ge(added, i * U + (u + 1))
                        nc.tensor.matmul(acc_ps[u % 2][:, :], s_mat[:, u % 4, :], slot[:, r, 0:W], start=True, stop=True).then_inc(summed, 1)


def node_phase_3(nc, k):
    with phase(nc) as (sb, ps, sem):
        ag = sb("n3_acc", [P, GROUP, 2 * D])
        fg = sb("n3_f", [P, GROUP, D])
        w = sb("n3_w", [P, 4, D])
        b = sb("n3_b", [P, D])
        turned_sb = sb("n3_turned", [P, 2, 2 * D])
        turned_ps, out_ps = ps("n3_turned_ps", [P, 2, 512]), ps("n3_out_ps", [P, 2, 512])
        pa = Project(sem, "n3a")
        weights, stored = sem("n3_weights"), sem("n3_stored")
        with nc.Block() as block:
            @block.sync
            def _(sp):
                sp.dma_start(w[:, :, :], k.wf.rearrange("(q p) n -> p q n", p=P)).then_inc(weights, 16)
                sp.dma_start(b[:, :], k.bf.to_broadcast([P, D])).then_inc(weights, 16)
                @rounds(sp, GROUPS)
                def _(g):
                    sp.wait_ge(pa.used, g * GROUP + GROUP)
                    sp.dma_start(tiles(k.tab_f)[:, bass.ds(g * GROUP, GROUP), :], fg[:, :, :]).then_inc(stored, 16)
                sp.wait_ge(stored, 16 * GROUPS)

            @block.scalar
            def _(act):
                @rounds(act, GROUPS)
                def _(g):
                    act.wait_ge(pa.product, g * GROUP)
                    nc.scalar.copy(ag[:, :, :], k.acc2[:, bass.ds(g * (GROUP * 2 * D), GROUP * 2 * D)].rearrange("p (n d) -> p n d", d=2 * D)
                                   ).then_inc(pa.src_ready, 1)
                    act_project(nc, act, g, pa, 4, turned_ps, turned_sb)

            @block.vector
            def _(dve):
                dve.wait_ge(weights, 32)
                @rounds(dve, GROUPS)
                def _(g):
                    dve.wait_ge(stored, g * 16)
                    for u in range(GROUP):
                        dve.wait_ge(pa.product, g * GROUP + (u + 1))
                        nc.vector.scalar_tensor_tensor(fg[:, u, :], b[:, :], k.cnt[:, 0, bass.ds(g * GROUP + u, 1)], out_ps[:, u % 2, 0:D],
                                                       ALU.mult, ALU.add).then_inc(pa.used, 1)

            @block.tensor
            def _(pe):
                pe.wait_ge(weights, 32)
                @rounds(pe, GROUPS)
                def _(g):
                    pe_project(nc, pe, k, g, pa, ag, 4, turned_ps, turned_sb, [(out_ps, w)])


def pass_3(nc, k):
    with phase(nc) as (sb, ps, sem):
        U, RING, BANKS = 16, 16, 4
        W = 2 * D
        slot = sb("p3_slot", [P, RING, SORT_ROW])
        s_mat = sb("p3_s", [P, BANKS, P])
        e_list, words = sb("p3_e_list", [1, STEP_COLS], I32), sb("p3_tile_words", [1, STEPS // PACK], I32)
        n128 = sb("p3_n128", [P, STEPS])
        walk = sem("p3_walk")
        acc_ps = [ps(f"p3_acc{i}", [P, 512]) for i in range(BANKS)]
        loaded = [sem(f"p3_loaded{r}") for r in range(RING)]
        s_ready, summed, added = sem("p3_s_ready"), sem("p3_summed"), sem("p3_added")
        per = 16 * U // RING
        def load_steps(eng, parity):
            eng.wait_ge(walk, 48)

            @rounds(eng, STEPS // U)
            def _(i):
                for u in range(parity, U, 2):
                    r = u % RING
                    e = eng.value_load(e_list[0:1, bass.ds(i * U + u, 1)], min_val=0, max_val=EDGE_TILES - 1)
                    eng.wait_ge(summed, i * U + (u + 1))
                    eng.dma_start(slot[:, r, :], tiles(k.tab_sorted)[:, bass.ds(e, 1), :].rearrange("p o d -> p (o d)")
                                  ).then_inc(loaded[r], 16)
            for r in range(parity, RING, 2):
                eng.wait_ge(loaded[r], 16 * STEPS // RING)

        with nc.Block() as block:
            @block.sync
            def _(sp):
                sp.dma_start(e_list[:, :], k.walk_lists[0:1, :]).then_inc(walk, 16)
                sp.dma_start(words[:, :], k.walk_lists[1:2, 0:STEPS // PACK]).then_inc(walk, 16)
                sp.dma_start(n128[:, :], k.walk_n128.to_broadcast([P, STEPS])).then_inc(walk, 16)
                load_steps(sp, 0)

            @block.scalar
            def _(act):
                load_steps(act, 1)

            @block.vector
            def _(dve):
                dve.wait_ge(walk, 48)

                def one_hot(i, s):
                    r = s % RING
                    dve.wait_ge(loaded[r], i * per + 16 * (s // RING + 1))
                    nc.vector.tensor_scalar(s_mat[:, s % BANKS, :], k.iota[:, :], col(n128, i * U + s), slot[:, r, 2 * D:2 * D + 1],
                                            ALU.add, ALU.is_equal).then_inc(s_ready, 1)

                nc.vector.memset(k.acc2[:, :], 0.0).then_inc(added, BANKS)
                for s in range(BANKS - 1):
                    one_hot(0, s)
                tile = tile_words(dve, words)

                def steps(i, last=False):
                    for u in range(U):
                        n = tile(i * U, u)
                        if not last or u + BANKS - 1 < U:
                            one_hot(i, u + BANKS - 1)
                        dve.wait_ge(summed, i * U + (RING + u + 1))
                        dve.wait_ge(added, i * U + (u + BANKS))
                        nc.vector.tensor_tensor(k.acc2[:, bass.ds(n * W, W)], k.acc2[:, bass.ds(n * W, W)],
                                                acc_ps[u % BANKS][:, :], ALU.add).then_inc(added, 1)

                rounds(dve, STEPS // U - 1)(steps)
                steps(STEPS // U - 1, last=True)
                dve.wait_ge(added, STEPS + BANKS)

            @block.tensor
            def _(pe):
                pe.sem_inc(summed, RING)

                @rounds(pe, STEPS // U)
                def _(i):
                    for u in range(U):
                        r = u % RING
                        pe.wait_ge(s_ready, i * U + (u + 1))
                        pe.wait_ge(loaded[r], i * per + 16 * (u // RING + 1))
                        pe.wait_ge(added, i * U + (u + 1))
                        nc.tensor.matmul(acc_ps[u % BANKS][:, :], s_mat[:, u % BANKS, :], slot[:, r, 0:W], start=True, stop=True).then_inc(summed, 1)


def node_phase_4(nc, k):
    with phase(nc) as (sb, ps, sem):
        xg, hg, fg = sb("n4_x", [P, GROUP, D]), sb("n4_h", [P, GROUP, D]), sb("n4_f", [P, GROUP, D])
        ag = sb("n4_acc", [P, GROUP, 2 * D])
        t = sb("n4_t", [P, GROUP, D])
        w = sb("n4_w", [P, 4, D])
        b, lnw, lnb = sb("n4_b", [P, D]), sb("n4_lnw", [P, D]), sb("n4_lnb", [P, D])
        total, inv = sb("n4_total", [P, NODE_TILES]), sb("n4_inv", [P, NODE_TILES])
        padding = sb("n4_padding", [P, NODE_TILES])
        turned_sb = sb("n4_turned", [P, 2, 2 * D])
        turned_ps, out_ps = ps("n4_turned_ps", [P, 2, 512]), ps("n4_out_ps", [P, 2, 512])
        back_ps = ps("n4_back_ps", [P, 8, D])
        pa, pb = Project(sem, "n4a"), Project(sem, "n4b")
        nb = norm_buffers(sb, sem, "n4")
        weights, loaded, stored, chain_s, pad_s = sem("n4_weights"), sem("n4_loaded"), sem("n4_stored"), sem("n4_chain"), sem("n4_pad")
        with nc.Block() as block:
            @block.gpsimd
            def _(pool):
                nc.gpsimd.memset(padding[:, :], 1.0).then_inc(pad_s, 1)
                pool.wait_ge(pad_s, 1)
                nc.gpsimd.affine_select(out=padding[:, :], in_=padding[:, :], compare_op=ALU.is_ge, fill=0.0,
                                        base=-NODES, pattern=[[P, NODE_TILES]], channel_multiplier=1).then_inc(pad_s, 1)

            @block.sync
            def _(sp):
                sp.dma_start(w[:, :, :], k.wb.rearrange("(q p) n -> p q n", p=P)).then_inc(weights, 16)
                for dest, src in ((b, k.bb), (lnw, k.ln2_w), (lnb, k.ln2_b)):
                    sp.dma_start(dest[:, :], src.to_broadcast([P, D])).then_inc(weights, 16)
                @rounds(sp, GROUPS)
                def _(g):
                    sp.wait_ge(stored, g * 16)
                    for dest, src in ((xg, k.tab_x2), (hg, k.tab_h), (fg, k.tab_f)):
                        sp.dma_start(dest[:, :, :], tiles(src)[:, bass.ds(g * GROUP, GROUP), :]).then_inc(loaded, 16)
                    sp.wait_ge(pb.used, g * GROUP + GROUP)
                    sp.dma_start(tiles(k.out)[:, bass.ds(g * GROUP, GROUP), :], xg[:, :, :]).then_inc(stored, 16)
                sp.wait_ge(stored, 16 * GROUPS)

            @block.scalar
            def _(act):
                def back(g):
                    act.wait_ge(pa.product, g * GROUP)
                    nc.scalar.copy(ag[:, :, :], k.acc2[:, bass.ds(g * (GROUP * 2 * D), GROUP * 2 * D)].rearrange("p (n d) -> p n d", d=2 * D)
                                   ).then_inc(pa.src_ready, 1)
                    act_project(nc, act, g, pa, 4, turned_ps, turned_sb)

                def norms(g, last=False):
                    if not last:
                        act.wait_ge(pb.product, g * GROUP)
                        back(g + 1)
                    act_root(nc, act, g, 0, 2, nb)
                    act_root(nc, act, g, 1, 2, nb)
                    act.wait_ge(pa.product, g * GROUP + (GROUP if last else 2 * GROUP))
                    act_project(nc, act, g, pb, 2, turned_ps, turned_sb)

                back(0)
                rounds(act, GROUPS - 1)(norms)
                norms(GROUPS - 1, last=True)

            @block.vector
            def _(dve):
                link = Chain(dve, chain_s)
                dve.wait_ge(weights, 64)
                dve.wait_ge(pad_s, 2)
                link(nc.vector.tensor_tensor(total[:, :], k.cnt[:, 0, :], k.cnt[:, 1, :], ALU.add))
                link(nc.vector.tensor_tensor(total[:, :], total[:, :], padding[:, :], ALU.add))
                link(nc.vector.reciprocal(inv[:, :], total[:, :]))
                base, per = link.n, 2 * NORM_LINKS + 5 + 2
                @rounds(dve, GROUPS)
                def _(g):
                    link.loop(g, per, base)
                    dve.wait_ge(loaded, g * 48 + 48)
                    dve.wait_ge(pa.product, g * GROUP + GROUP)
                    nc.vector.tensor_tensor(t[:, :, :], back_ps[:, 0:GROUP, :], fg[:, :, :], ALU.add).then_inc(pa.used, GROUP)
                    dve.wait_ge(pa.used, g * GROUP + GROUP)
                    for u in range(GROUP):
                        last = nc.vector.scalar_tensor_tensor(t[:, u, :], b[:, :], k.cnt[:, 1, bass.ds(g * GROUP + u, 1)], t[:, u, :],
                                                              ALU.mult, ALU.add)
                    link(last)
                    for u in range(GROUP):
                        last = nc.vector.tensor_scalar(t[:, u, :], t[:, u, :], col(inv, g * GROUP + u), None, ALU.mult)
                    link(last)
                    link(nc.vector.scalar_tensor_tensor(t[:, :, :], t[:, :, :], 0.01, t[:, :, :], ALU.mult, ALU.max))
                    link(nc.vector.tensor_tensor(t[:, :, :], t[:, :, :], hg[:, :, :], ALU.add))
                    dve_norm(nc, dve, link, g, 0, 2, nb, t, hg)
                    link(nc.vector.tensor_tensor(hg[:, :, :], hg[:, :, :], lnw[:, :].unsqueeze(1).to_broadcast([P, GROUP, D]), ALU.mult))
                    link(nc.vector.tensor_tensor(hg[:, :, :], hg[:, :, :], lnb[:, :].unsqueeze(1).to_broadcast([P, GROUP, D]), ALU.add))
                    link(nc.vector.tensor_tensor(xg[:, :, :], xg[:, :, :], hg[:, :, :], ALU.add))
                    dve_norm(nc, dve, link, g, 1, 2, nb, xg, t)
                    nc.vector.tensor_scalar(t[:, :, :], t[:, :, :], 0.0, None, ALU.max).then_inc(pb.src_ready, 1)
                    for u in range(GROUP):
                        dve.wait_ge(pb.product, g * GROUP + (u + 1))
                        nc.vector.tensor_tensor(xg[:, u, :], out_ps[:, u % 2, 0:D], xg[:, u, :], ALU.add).then_inc(pb.used, 1)

            @block.tensor
            def _(pe):
                pe.wait_ge(weights, 64)
                def back(g):
                    pe_project(nc, pe, k, g, pa, ag, 4, turned_ps, turned_sb, [(back_ps, w)])

                def rotate(g, last=False):
                    if not last:
                        pe.wait_ge(pb.copied, g * GROUP)
                        back(g + 1)
                    pe.wait_ge(pa.copied, g * GROUP + (GROUP if last else 2 * GROUP))
                    pe_project(nc, pe, k, g, pb, t, 2, turned_ps, turned_sb, [(out_ps, k.rot_t)])

                back(0)
                rounds(pe, GROUPS - 1)(rotate)
                rotate(GROUPS - 1, last=True)


def rotation_records(nc, k):
    with phase(nc) as (sb, ps, sem):
        T = EDGE_TILES
        H = T // 2
        rec, pos = k.rec, k.rec_pos
        idx_i = sb("rl_idx_i", [P, 2, T], I32)
        f = sb("rl_f", [P, 2, T])
        fc = sb("rl_fc", [P, 2, T])
        m = sb("rl_m", [P, 2, T])
        w = sb("rl_w", [P, T])
        ang = sb("rl_ang", [P, 2, T])
        turns, sign = sb("rl_turns", [P, T]), sb("rl_sign", [P, T])
        sc = sb("rl_sc", [P, 2, T])
        active, both, count = sb("rl_active", [P, T]), sb("rl_both", [P, T]), sb("rl_count", [P, T])
        total, incl, zeros = sb("rl_total", [P, T]), sb("rl_incl", [P, T]), sb("rl_zeros", [P, T])
        nb_f = sb("rl_nb_f", [P, 1])
        zrow = sb("rl_zrow", [P, ROT_PIECE * REC])
        before_ps, total_ps = ps("rl_before", [P, 2, 512]), ps("rl_total_ps", [P, 2, 512])
        loaded, chain_s, ang_ready, sc_ready = sem("rl_loaded"), sem("rl_chain"), sem("rl_ang_ready"), sem("rl_sc_ready")
        count_ready, before_ready, zrow_ready, cleared = sem("rl_count_ready"), sem("rl_before_ready"), sem("rl_zrow_ready"), sem("rl_cleared")
        with nc.Block() as block:
            @block.sync
            def _(sp):
                sp.dma_start(idx_i[:, 0, :], k.src_cols[:, 0:T]).then_inc(loaded, 16)
                sp.dma_start(idx_i[:, 1, :], k.dst_cols[:, 0:T]).then_inc(loaded, 16)
                sp.dma_start(w[:, :], k.w_cols[:, 0:T]).then_inc(loaded, 16)
                sp.wait_ge(zrow_ready, 1)
                sp.dma_start(k.rot_list.rearrange("(p r t) f -> p r (t f)", p=P, t=ROT_PIECE),
                             zrow[:, :].unsqueeze(1).to_broadcast([P, ROT_ROWS // (P * ROT_PIECE), ROT_PIECE * REC])
                             ).then_inc(cleared, 16)
                sp.wait_ge(loaded, 48)
                sp.wait_ge(cleared, 16)

            @block.scalar
            def _(act):
                act.wait_ge(ang_ready, 1)
                nc.scalar.activation(sc[:, :, :], ang[:, :, :], ACT.Sin).then_inc(sc_ready, 1)

            @block.gpsimd
            def _(pool):
                nc.gpsimd.memset(zrow[:, :], 0.0).then_inc(zrow_ready, 1)

            @block.vector
            def _(dve):
                link = Chain(dve, chain_s)
                dve.wait_ge(loaded, 48)
                link(nc.vector.tensor_copy(f[:, :, :], idx_i[:, :, :]))
                link(nc.vector.tensor_scalar(m[:, :, :], f[:, :, :], D - 0.5, None, ALU.is_lt))
                link(nc.vector.tensor_tensor(turns[:, :], f[:, 0, :], f[:, 1, :], ALU.not_equal))
                link(nc.vector.tensor_tensor(m[:, 0, :], m[:, 0, :], turns[:, :], ALU.mult))
                link(nc.vector.tensor_tensor(active[:, :], m[:, 0, :], m[:, 1, :], ALU.max))
                link(nc.vector.tensor_tensor(both[:, :], m[:, 0, :], m[:, 1, :], ALU.mult))
                nc.vector.tensor_tensor(count[:, :], m[:, 0, :], m[:, 1, :], ALU.add).then_inc(count_ready, 1)
                reduce_angle(nc, link, ang[:, 0, :], turns[:, :], w[:, :], 1.0, 0.0)
                reduce_angle(nc, link, ang[:, 1, :], turns[:, :], w[:, :], 1.0, float(np.pi / 2))
                nc.vector.memset(zeros[:, :], 0.0).then_inc(ang_ready, 1)
                dve.wait_ge(ang_ready, 1)
                link(nc.vector.tensor_scalar(fc[:, :, :], f[:, :, :], D - 1.0, None, ALU.min))
                for n, (own, other) in enumerate(((f[:, 0, :], f[:, 1, :]), (fc[:, 1, :], fc[:, 0, :]))):
                    link(nc.vector.tensor_tensor(total[:, :], own, other, ALU.subtract))
                    link(nc.vector.tensor_tensor(total[:, :], total[:, :], m[:, 0, :], ALU.mult))
                    link(nc.vector.tensor_tensor(rec[:, :, n], total[:, :], other, ALU.add))
                    link(nc.vector.tensor_tensor(rec[:, :, 4 + n], other, both[:, :], ALU.mult))
                link(nc.vector.tensor_scalar(rec[:, :, 8], both[:, :], -1.0, None, ALU.mult))
                link(nc.vector.tensor_scalar(sign[:, :], m[:, 0, :], -2.0, 1.0, ALU.mult, ALU.add))
                dve.wait_ge(sc_ready, 1)
                link(nc.vector.tensor_scalar(rec[:, :, 2], sc[:, 1, :], -1.0, None, ALU.add))
                link(nc.vector.tensor_tensor(rec[:, :, 3], sc[:, 0, :], sign[:, :], ALU.mult))
                link(nc.vector.scalar_tensor_tensor(rec[:, :, 6], sc[:, 1, :], -1.0, both[:, :], ALU.add, ALU.mult))
                link(nc.vector.tensor_tensor(rec[:, :, 7], sc[:, 0, :], both[:, :], ALU.mult))
                dve.wait_ge(before_ready, 1)
                link(nc.vector.tensor_copy(total[:, :].rearrange("p (h c) -> p h c", h=2), total_ps[:, :, 0:H]))
                link(nc.vector.tensor_tensor_scan(incl[:, :], total[:, :], zeros[:, :], 0.0, ALU.add, ALU.add))
                link(nc.vector.tensor_tensor(pos[:, :], incl[:, :], total[:, :], ALU.subtract))
                link(nc.vector.tensor_tensor(pos[:, :].rearrange("p (h c) -> p h c", h=2), pos[:, :].rearrange("p (h c) -> p h c", h=2),
                                             before_ps[:, :, 0:H], ALU.add))
                link(nc.vector.scalar_tensor_tensor(pos[:, :], pos[:, :], 1.0 - OUT_OF_BOUNDS, active[:, :], ALU.add, ALU.mult))
                link(nc.vector.tensor_scalar(pos[:, :], pos[:, :], float(OUT_OF_BOUNDS), None, ALU.add))
                link(nc.vector.tensor_scalar(nb_f[:, :], incl[:, T - 1:T], BATCH_UPDATES / 2 - 0.5, 1.0 / BATCH_UPDATES, ALU.add, ALU.mult))
                link(nc.vector.tensor_scalar(nb_f[:, :], nb_f[:, :], ROUND, None, ALU.add))
                link(nc.vector.tensor_scalar(nb_f[:, :], nb_f[:, :], -ROUND, BATCHES_BESIDE + 1.0, ALU.add, ALU.max))
                link(nc.vector.tensor_copy(k.batches[:, :], nb_f[:, :]))

            @block.tensor
            def _(pe):
                pe.wait_ge(count_ready, 1)
                for h in range(2):
                    nc.tensor.matmul(before_ps[:, h, 0:H], k.upper[:, :], count[:, h * H:(h + 1) * H], start=True, stop=True)
                    last = nc.tensor.matmul(total_ps[:, h, 0:H], k.ones[:, :], count[:, h * H:(h + 1) * H], start=True, stop=True)
                last.then_inc(before_ready, 1)


SCATTER_UNROLL = 17


class RecordScatter:

    def __init__(self, sb, sem, name, first, last):
        self.first, self.last = first, last
        self.rec = sb(name + "_rec", [P, SCATTER_UNROLL, REC])
        self.pos = sb(name + "_pos", [P, SCATTER_UNROLL], I32)
        self.slots, self.settled = sem(name + "_slots"), sem(name + "_settled")
        self.scattered = [sem(f"{name}_scattered{r}") for r in range(SCATTER_UNROLL)]


def act_records(nc, act, k, s):
    U = SCATTER_UNROLL

    @rounds(act, s.last - s.first)
    def _(i):
        for u in range(U):
            act.wait_ge(s.scattered[u], i * 16)
            nc.scalar.copy(s.rec[:, u, :], k.rec[:, bass.ds(i * U + (u + s.first * U), 1), :].rearrange("p o f -> p (o f)"))
            nc.scalar.copy(s.pos[:, u:u + 1], col(k.rec_pos, i * U + (u + s.first * U))).then_inc(s.slots, 1)


def pool_records(nc, pool, k, s):
    U = SCATTER_UNROLL

    @rounds(pool, s.last - s.first)
    def _(i):
        for u in range(U):
            pool.wait_ge(s.slots, i * U + (u + 1))
            settle(pool, s.settled)
            pool.indirect_dma_start(out=k.rot_list, out_offset=bass.IndirectOffsetOnAxis(ap=s.pos[:, u:u + 1], axis=0),
                                    in_=s.rec[:, u, :], in_offset=None,
                                    bounds_check=ROT_ROWS - 1, oob_is_err=False).then_inc(s.scattered[u], 16)


def wait_records(pool, s):
    for u in range(SCATTER_UNROLL):
        pool.wait_ge(s.scattered[u], 16 * (s.last - s.first))


def pass_0_and_rotation(nc, k):
    with phase(nc) as (sb, ps, sem):
        U, RING, SLOTS = STEPS_BESIDE_BATCH, 13, 4
        per = 16 * U // RING
        begun = sem("p0_begun")
        gathered_rows = sb("p0_rows", [P, RING, D])
        idx = sb("p0_idx", [P, 2 * RING], I32)
        s_mat = sb("p0_s", [P, SLOTS, P])
        acc_ps = [ps(f"p0_acc{i}", [P, 512]) for i in range(2)]
        gathered = [sem(f"p0_gathered{r}") for r in range(RING)]
        idx_ready, s_ready, summed, added = sem("p0_idx_ready"), sem("p0_s_ready"), sem("p0_summed"), sem("p0_added")
        LEVELS = P.bit_length() - 1
        B = BATCH
        rec_in, sec_in = sb("rm_rec_in", [P, B, 4]), sb("rm_sec_in", [P, B, 5])
        rec, gate = sb("rm_rec", [P, B, 4]), sb("rm_gate", [P, B])
        second = sb("rm_second", [P, B])
        iota = sb("rm_iota", [P, D])
        masks = sb("rm_masks", [P, LEVELS + 3, P])
        edge = sb("rm_edge", [P, 2])
        diag, keep, l1, l2 = (sb("rm_" + n, [P, B, P]) for n in ("diag", "keep", "l1", "l2"))
        lt, t, tt, x = (sb("rm_" + n, [P, B, P]) for n in ("lt", "t", "tt", "x"))
        e, f, f1 = sb("rm_e", [P, B, D]), sb("rm_f", [P, B, D]), sb("rm_f1", [P, B, D])
        v, vt, y = sb("rm_v", [P, B, D]), sb("rm_vt", [P, B, D]), sb("rm_y", [P, 2, D])
        m = sb("rm_m", [P, 2, D])
        lx_ps, lt_ps = ps("rm_lx_ps", [P, B, P]), ps("rm_lt_ps", [P, B, P])
        d_ps = [ps(f"rm_d_ps{i}", [P, B, P]) for i in range(2)]
        v_ps = [bank[:, :, :].rearrange("p b s -> p (b s)").rearrange("p (c d) -> p c d", d=D) for bank in (lx_ps, lt_ps)]
        y_ps, u_ps = ps("rm_y_ps", [P, D]), ps("rm_u_ps", [P, 2, D])
        loaded, ready, chain_s, rec_loaded, taken = (sem("rm_" + n) for n in ("loaded", "ready", "chain", "rec_loaded", "taken"))
        diag_ready, row_made, l_ready, lt_made, lt_ready = (sem("rm_" + n) for n in (
            "diag_ready", "row_made", "l_ready", "lt_made", "lt_ready"))
        t_ready, x_made, x_ready, d_made, f_ready = (sem("rm_" + n) for n in ("t_ready", "x_made", "x_ready", "d_made", "f_ready"))
        v_made, v_ready, vt_made, vt_ready = (sem("rm_" + n) for n in ("v_made", "v_ready", "vt_made", "vt_ready"))
        y_made, y_ready, u_made, m_ready, m_turned = (sem("rm_" + n) for n in (
            "y_made", "y_ready", "u_made", "m_ready", "m_turned"))
        flat = lambda a: a[:, :, :].rearrange("p b s -> p (b s)")
        spread = lambda a: a.unsqueeze(1).to_broadcast([P, B, P])
        PLACES = 4 + 2 * (LEVELS - 1)
        CHAINED = 9 + B

        def batches(eng):
            return eng.value_load(k.batches[0:1, 0:1], min_val=BATCHES_BESIDE + 1, max_val=MAX_BATCHES)

        def all_batches(eng, batch, step):
            def beside(i):
                def fill(place):
                    for u in range(place * U // PLACES, (place + 1) * U // PLACES):
                        step(i, u)
                batch(i, fill)
            rounds(eng, BATCHES_BESIDE)(beside)
            with eng.Fori(BATCHES_BESIDE, batches(eng)) as i:
                batch(i, lambda place: None)

        with nc.Block() as block:
            @block.sync
            def _(sp):
                sp.dma_start(masks[:, :, :], k.rot_masks).then_inc(loaded, 16)
                sp.dma_start(edge[:, :], k.rot_edge).then_inc(loaded, 16)

                @rounds(sp, batches(sp))
                def _(i):
                    sp.wait_ge(taken, i)
                    for c in range(B):
                        at = i * BATCH_UPDATES + c * (P - 1)
                        sp.dma_start(rec_in[:, c, :], k.rot_list[bass.ds(at + 1, P), 0:4]).then_inc(rec_loaded, 16)
                        sp.dma_start(sec_in[:, c, :], k.rot_list[bass.ds(at, P), 4:REC]).then_inc(rec_loaded, 16)
                sp.wait_ge(loaded, 32)

            @block.gpsimd
            def _(pool):
                nc.gpsimd.iota(iota[:, :], [[1, D]], base=0, channel_multiplier=0, allow_small_or_imprecise_dtypes=True).then_inc(ready, 1)
                nc.gpsimd.memset(m[:, :, :], 0.0).then_inc(ready, 1)
                pool.wait_ge(ready, 2)
                for h in range(2):
                    nc.gpsimd.affine_select(out=m[:, h, :], in_=m[:, h, :], compare_op=ALU.not_equal, fill=1.0,
                                            base=h * P, pattern=[[-1, D]], channel_multiplier=1).then_inc(ready, 1)

                @rounds(pool, BATCHES_BESIDE)
                def _(i):
                    for u in range(U):
                        at = u % (2 * RING)
                        if u % RING == 0:
                            nc.gpsimd.tensor_copy(idx[:, at:at + RING], col(k.step_src, i * U + u, RING)).then_inc(idx_ready, 1)
                            pool.wait_ge(idx_ready, i * (U // RING) + (u // RING + 1))
                        pool.wait_ge(summed, i * U + (u + 1))
                        settle(pool, begun)
                        pool.indirect_dma_start(out=gathered_rows[:, u % RING, :], out_offset=None, in_=k.tab_y,
                                                in_offset=bass.IndirectOffsetOnAxis(ap=idx[:, at:at + 1], axis=0)
                                                ).then_inc(gathered[u % RING], 16)

            @block.vector
            def _(dve):
                dve.wait_ge(ready, 4)
                dve.wait_ge(loaded, 32)
                nc.vector.memset(gate[:, :], 0.0).then_inc(m_ready, B + 1)
                nc.vector.memset(k.acc[:, :], 0.0).then_inc(added, 2)
                link = Chain(dve, chain_s)
                of = lambda c, n: rec[:, c, n:n + 1]

                def add_update(c, done):
                    dve.wait_ge(u_made, done + 1)
                    dve.wait_ge(m_ready, done + 1)
                    nc.vector.tensor_tensor(m[:, :, :], m[:, :, :], u_ps[:, :, :], ALU.add).then_inc(m_ready, 1)

                def one_hot(i, s):
                    nc.vector.tensor_scalar(s_mat[:, s % SLOTS, :], k.iota[:, :], col(k.step_rel, i * U + s), None,
                                            ALU.is_equal).then_inc(s_ready, 1)

                def step(i, u):
                    n = tile(i * U, u)
                    one_hot(i, u + SLOTS - 1)
                    dve.wait_ge(summed, i * U + (RING + u + 1))
                    dve.wait_ge(added, i * U + (u + 2))
                    nc.vector.tensor_tensor(k.acc[:, bass.ds(n * D, D)], k.acc[:, bass.ds(n * D, D)],
                                            acc_ps[u % 2][:, 0:D], ALU.add).then_inc(added, 1)

                def batch(i, fill):
                    link.loop(i, CHAINED, 0)
                    dve.wait_ge(rec_loaded, i * (32 * B) + 32 * B)
                    link(nc.vector.tensor_tensor(rec[:, :, :], rec_in[:, :, :], sec_in[:, :, 0:4], ALU.add))
                    link(nc.vector.tensor_copy(second[:, :], sec_in[:, :, 4]))
                    nc.vector.tensor_scalar(gate[:, :], second[:, :], edge[:, 1:2], edge[:, 0:1], ALU.mult, ALU.add).then_inc(taken, 1)
                    dve.wait_ge(taken, i + 1)
                    for c in range(B):
                        last = nc.vector.tensor_scalar(diag[:, c, :], k.ident[:, :], of(c, 0), None, ALU.mult)
                    last.then_inc(diag_ready, 1)
                    link(nc.vector.tensor_tensor(rec[:, :, 2:4], rec[:, :, 2:4], gate[:, :].unsqueeze(2).to_broadcast([P, B, 2]), ALU.mult))
                    for c in range(B):
                        last = nc.vector.scalar_tensor_tensor(keep[:, c, :], masks[:, LEVELS + 2, :], second[:, c:c + 1],
                                                              masks[:, LEVELS + 1, :], ALU.mult, ALU.add)
                    link(last)
                    fill(0)
                    dve.wait_ge(row_made, i + 1)
                    for c in range(B):
                        nc.vector.tensor_scalar(l1[:, c, :], lx_ps[:, c, :], of(c, 0), of(c, 2), ALU.is_equal, ALU.mult)
                        last = nc.vector.tensor_scalar(l2[:, c, :], lx_ps[:, c, :], of(c, 1), of(c, 3), ALU.is_equal, ALU.mult)
                    link(last)
                    link(nc.vector.tensor_tensor(flat(l1), flat(l1), flat(l2), ALU.add))
                    nc.vector.tensor_tensor(flat(l1), flat(l1), flat(keep), ALU.mult).then_inc(l_ready, 1)
                    dve.wait_ge(l_ready, i + 1)
                    link(nc.vector.tensor_tensor(t[:, :, :], l1[:, :, :], spread(masks[:, 0, :]), ALU.mult))
                    link(nc.vector.tensor_tensor(t[:, :, :], t[:, :, :], spread(k.ident[:, :]), ALU.add))
                    dve.wait_ge(lt_ready, i + 1)
                    link(nc.vector.tensor_tensor(tt[:, :, :], lt[:, :, :], spread(masks[:, LEVELS, :]), ALU.mult))
                    nc.vector.tensor_tensor(tt[:, :, :], tt[:, :, :], spread(k.ident[:, :]), ALU.add).then_inc(t_ready, 1)
                    fill(1)
                    for n in range(1, LEVELS):
                        dve.wait_ge(x_made, i * (LEVELS - 1) + n)
                        nc.vector.tensor_tensor(x[:, :, :], lx_ps[:, :, :], spread(masks[:, n, :]), ALU.mult).then_inc(x_ready, 1)
                        if n <= B:
                            c = n - 1
                            nc.vector.tensor_scalar(f1[:, c, :], iota[:, :], of(c, 0), of(c, 2), ALU.is_equal, ALU.mult)
                            link(nc.vector.tensor_scalar(f[:, c, :], iota[:, :], of(c, 1), of(c, 3), ALU.is_equal, ALU.mult))
                        fill(2 * n)
                        dve.wait_ge(d_made, i * (LEVELS - 1) + n)
                        dve.wait_ge(t_ready, i * LEVELS + n)
                        if n < LEVELS - 1:
                            nc.vector.tensor_tensor(flat(t), flat(t), flat(d_ps[0]), ALU.add)
                        nc.vector.tensor_tensor(flat(tt), flat(tt), flat(d_ps[1]), ALU.add).then_inc(t_ready, 1)
                        if n <= B:
                            if not (isinstance(i, int) and i == 0):
                                add_update(c, i * B + c)
                            nc.vector.tensor_tensor(f[:, c, :], f[:, c, :], f1[:, c, :], ALU.add)
                            nc.vector.tensor_scalar(e[:, c, :], iota[:, :], of(c, 0), None, ALU.is_equal).then_inc(f_ready, 1)
                        fill(2 * n + 1)
                    fill(PLACES - 2)
                    fill(PLACES - 1)

                for s in range(SLOTS - 1):
                    one_hot(0, s)
                tile = tile_words(dve, k.tile_words)
                all_batches(dve, batch, step)
                n = batches(dve)
                for c in range(B):
                    add_update(c, n * B + c)
                dve.wait_ge(m_turned, 1)
                for q in range(2):
                    last = nc.vector.tensor_copy(k.rot_t[:, q, :], v_ps[q][:, 0, :])
                last.then_inc(m_turned, 1)

            @block.scalar
            def _(act):
                def copy_y(c, done):
                    act.wait_ge(y_made, done + 1)
                    nc.scalar.copy(y[:, c % 2, :], y_ps[:, :]).then_inc(y_ready, 1)

                act.sem_inc(y_ready, B)
                act.sem_inc(vt_ready, 1)

                def batch(i, fill):
                    act.wait_ge(lt_made, i + 1)
                    nc.scalar.copy(flat(lt), flat(lt_ps)).then_inc(lt_ready, 1)
                    if not (isinstance(i, int) and i == 0):
                        for c in range(B):
                            copy_y(c, i * B + c)
                    for h in range(2):
                        act.wait_ge(v_made, i * 2 + (h + 1))
                        nc.scalar.copy(v[:, 2 * h:2 * h + 2, :], v_ps[h][:, :, :]).then_inc(v_ready, 1)
                    for h in range(2):
                        act.wait_ge(vt_made, i * 2 + (h + 1))
                        nc.scalar.copy(vt[:, 2 * h:2 * h + 2, :].rearrange("p c d -> p (c d)"), flat(d_ps[h])).then_inc(vt_ready, 1)

                all_batches(act, batch, lambda i, u: None)
                n = batches(act)
                for c in range(B):
                    copy_y(c, n * B + c)

            @block.tensor
            def _(pe):
                def make_y(c, done):
                    pe.wait_ge(m_ready, done + 1)
                    for h in range(2):
                        last = nc.tensor.matmul(y_ps[:, :], vt[:, c, h * P:(h + 1) * P], m[:, h, :], start=(h == 0), stop=(h == 1))
                    last.then_inc(y_made, 1)

                def make_u(c, done):
                    pe.wait_ge(y_ready, done + 1)
                    for h in range(2):
                        last = nc.tensor.matmul(u_ps[:, h, :], e[:, c, h * P:(h + 1) * P], y[:, c % 2, :], start=True, stop=True)
                    last.then_inc(u_made, 1)

                pe.sem_inc(y_made, B)
                pe.sem_inc(u_made, B)
                pe.sem_inc(summed, RING)
                pe.wait_ge(ready, 4)
                n_batches = batches(pe)

                def step(i, u):
                    pe.wait_ge(s_ready, i * U + (u + 1))
                    pe.wait_ge(gathered[u % RING], i * per + 16 * (u // RING + 1))
                    pe.wait_ge(added, i * U + (u + 1))
                    nc.tensor.matmul(acc_ps[u % 2][:, 0:D], s_mat[:, u % SLOTS, :], gathered_rows[:, u % RING, :],
                                     start=True, stop=True).then_inc(summed, 1)

                def batch(i, fill):
                    apply_before = not (isinstance(i, int) and i == 0)
                    pe.wait_ge(diag_ready, i + 1)
                    for c in range(B):
                        last = nc.tensor.matmul(lx_ps[:, c, :], k.ones[:, :], diag[:, c, :], start=True, stop=True)
                    last.then_inc(row_made, 1)
                    fill(0)
                    pe.wait_ge(l_ready, i + 1)
                    for c in range(B):
                        last = nc.tensor.transpose(lt_ps[:, c, :], l1[:, c, :], k.ident[:, :])
                    last.then_inc(lt_made, 1)
                    if apply_before:
                        pe.wait_ge(vt_ready, i * 2 + 1)
                        make_y(0, i * B)
                    fill(1)
                    for n in range(1, LEVELS):
                        c = n - 1
                        pe.wait_ge(t_ready, i * LEVELS + n)
                        for b in range(B):
                            last = nc.tensor.matmul(lx_ps[:, b, :], lt[:, b, :], t[:, b, :], start=True, stop=True)
                        last.then_inc(x_made, 1)
                        if apply_before and c < B:
                            make_u(c, i * B + c)
                        fill(2 * n)
                        pe.wait_ge(x_ready, i * (LEVELS - 1) + n)
                        for b in range(B):
                            if n < LEVELS - 1:
                                nc.tensor.matmul(d_ps[0][:, b, :], tt[:, b, :], x[:, b, :], start=True, stop=True)
                            last = nc.tensor.matmul(d_ps[1][:, b, :], x[:, b, :], tt[:, b, :], start=True, stop=True)
                        last.then_inc(d_made, 1)
                        if apply_before and c + 1 < B:
                            make_y(c + 1, i * B + (c + 1))
                        fill(2 * n + 1)
                    pe.wait_ge(t_ready, i * LEVELS + LEVELS)
                    pe.wait_ge(f_ready, i * B + B)
                    for c in range(B):
                        last = nc.tensor.matmul(v_ps[c // 2][:, c % 2, :], tt[:, c, :], f[:, c, :], start=True, stop=True)
                        if c % 2 == 1:
                            last.then_inc(v_made, 1)
                    fill(PLACES - 2)
                    for c in range(B):
                        if c % 2 == 0:
                            pe.wait_ge(v_ready, i * 2 + (c // 2 + 1))
                        for h in range(2):
                            last = nc.tensor.transpose(d_ps[c // 2][:, 2 * (c % 2) + h, :], v[:, c, h * P:(h + 1) * P], k.ident[:, :])
                        if c % 2 == 1:
                            last.then_inc(vt_made, 1)
                    fill(PLACES - 1)

                all_batches(pe, batch, step)
                pe.wait_ge(vt_ready, n_batches * 2 + 1)
                for c in range(B):
                    make_y(c, n_batches * B + c)
                    make_u(c, n_batches * B + c)
                pe.wait_ge(m_ready, n_batches * B + (B + 1))
                for q in range(2):
                    for h in range(2):
                        last = nc.tensor.transpose(v_ps[q][:, 0, h * P:(h + 1) * P], m[:, h, q * P:(q + 1) * P], k.ident[:, :])
                last.then_inc(m_turned, 1)


def build_program(nc, k):
    with ExitStack() as c:
        persistent(nc, c, k)
        constants(nc, k)
        with (nc.sbuf_tensor("rec", [P, EDGE_TILES, REC], F32) as k.rec,
              nc.sbuf_tensor("rec_pos", [P, EDGE_TILES], F32) as k.rec_pos,
              nc.sbuf_tensor("place", [P, STEP_COLS], F32) as k.place):
            rotation_records(nc, k)
            node_counts_and_sort(nc, k)
            step_lists(nc, k)
        k.acc2 = c.enter_context(nc.sbuf_tensor("sums", [P, (NODE_TILES + 1) * 2 * D], F32))
        k.acc, k.spare = k.acc2[:, 0:(NODE_TILES + 1) * D], k.acc2[:, (NODE_TILES + 1) * D:]
        node_phase_0(nc, k)
        pass_0_and_rotation(nc, k)
        with nc.sbuf_tensor("node_tab", [P, (NODE_TILES + 1) * D], F32) as k.node_tab:
            node_phase_1(nc, k)
            cutoffs(nc, k)
            pass_1(nc, k)
            node_phase_2(nc, k)
            pass_2(nc, k)
        node_phase_3(nc, k)
        pass_3(nc, k)
        node_phase_4(nc, k)


def _rotation_masks():
    place = np.arange(P)
    s, t = place[:, None], place[None, :]
    levels = P.bit_length() - 1
    out = np.zeros((P, levels + 3, P), np.float32)
    for n in range(levels):
        out[:, n, :] = ((s >> n) % 2 == 1) & (t >> n == (s >> n) - 1)
    out[:, levels, :] = out[:, 0, :].T
    out[:, levels + 1, :] = t < s
    out[:, levels + 2, :] = t == s - 1
    return out


def _rotation_edge():
    out = np.zeros((P, 2), np.float32)
    out[:P - 1, 0] = 1
    out[0, 1], out[P - 1, 1] = 1, -1
    return out


def kernel(x, src, dst, edge_attr_256, edge_attr_64, edge_weight, L0_gnn_W, L1_gnn_ln_g, L1_gnn_ln_b, L1_gnn_Wq,
           L1_gnn_bq, L1_gnn_Wk, L1_gnn_bk, L1_gnn_Wv, L1_gnn_bv, L1_gnn_Wo, L1_gnn_bo, L1_gnn_Wdk, L1_gnn_bdk,
           L1_gnn_Wdv, L1_gnn_bdv, L2_gnn_queries, L2_gnn_influence_weights, L2_gnn_W_fwd, L2_gnn_b_fwd,
           L2_gnn_W_back, L2_gnn_b_back, L2_gnn_ln_w, L2_gnn_ln_b):
    import concourse.bacc as bacc
    from concourse.bass_utils import run_bass_kernel_spmd

    def padded(a, rows, fill):
        a = np.asarray(a)
        out = np.full((rows,) + a.shape[1:], fill, a.dtype)
        out[:len(a)] = a
        return out

    row = lambda a: np.asarray(a).reshape(1, -1)
    t = lambda a: np.asarray(a).T
    rows = lambda a, fill: padded(a, STEP_COLS * P, fill).reshape(STEP_COLS, P)
    ordered = dict(src=rows(src, PAD_NODE), dst=rows(dst, PAD_NODE), w=rows(edge_weight, 0))
    arrays = {n + "_rows": a for n, a in ordered.items()} | {n + "_cols": a.T for n, a in ordered.items()}
    back = t(L2_gnn_W_back)
    arrays |= dict(
        x=padded(x, NODES_PAD, 0),
        e256=padded(edge_attr_256, EDGES_PAD, 0),
        ea_t=np.concatenate([padded(edge_attr_64, EDGES_PAD, 0).T, np.ones((1, EDGES_PAD), np.float32)], 0),
        w0=L0_gnn_W, ln1_g=L1_gnn_ln_g, ln1_b=L1_gnn_ln_b, bo=row(L1_gnn_bo), wo=t(L1_gnn_Wo),
        wkvq=np.concatenate([t(L1_gnn_Wk), t(L1_gnn_Wv), t(L1_gnn_Wq)], 1),
        bkvq=np.concatenate([row(L1_gnn_bk), row(L1_gnn_bv), row(L1_gnn_bq)], 1),
        wd=np.concatenate([np.concatenate([t(L1_gnn_Wdk), t(L1_gnn_Wdv)], 1),
                           np.concatenate([row(L1_gnn_bdk), row(L1_gnn_bdv)], 1)], 0),
        wf=t(L2_gnn_W_fwd), bf=row(L2_gnn_b_fwd),
        wb=np.concatenate([back[D:], back[:D]], 0), bb=row(L2_gnn_b_back),
        ln2_w=row(L2_gnn_ln_w), ln2_b=row(L2_gnn_ln_b),
        rot_masks=_rotation_masks(), rot_edge=_rotation_edge())
    arrays = {n: np.ascontiguousarray(a) for n, a in arrays.items()}

    nc = bacc.Bacc("TRN2", target_bir_lowering=False, num_devices=1)
    k = Kernel()
    for name, a in arrays.items():
        setattr(k, name, nc.dram_tensor("in_" + name, a.shape, mybir.dt.from_np(a.dtype), kind="ExternalInput").ap())
    scratch = dict(tab_y=(NODES_PAD, D), tab_kv=(NODES_PAD, 2 * D), tab_x=(NODES_PAD, D), tab_x2=(NODES_PAD, D),
                   tab_h=(NODES_PAD, D), tab_f=(NODES_PAD, D), tab_sorted=(EDGES_PAD, SORT_ROW),
                   place_rows=(STEP_COLS, P), walk_n128=(1, STEPS), rot_list=(ROT_ROWS, REC))
    for name, shape in scratch.items():
        setattr(k, name, nc.dram_tensor(name, shape, F32).ap())
    k.walk_lists = nc.dram_tensor("walk_lists", (2, STEP_COLS), I32).ap()
    k.out = nc.dram_tensor("out", (NODES_PAD, D), F32, kind="ExternalOutput").ap()
    build_program(nc, k)
    result = run_bass_kernel_spmd(nc, [{"in_" + n: a for n, a in arrays.items()}], core_ids=[0])
    return result.results[0]["out"][:NODES]
```
